# Optimizing a Trainium2 kernel written in Bass

```python
import numpy as np
import jax
import jax.numpy as jnp

def _softmax(x, axis=-1):
    return jax.nn.softmax(x, axis=axis)

def _gelu(x):
    return jax.nn.gelu(x, approximate=True)

def _silu(x):
    return jax.nn.silu(x)

def _sigmoid(x):
    return jax.nn.sigmoid(x)

def _layernorm(x, axis=-1, eps=1e-05):
    m = jnp.mean(x, axis=axis, keepdims=True)
    v = jnp.var(x, axis=axis, keepdims=True)
    return (x - m) / jnp.sqrt(v + eps)

def _scatter_add(tgt, idx, src, axis=0):
    return tgt.at[idx].add(src)

def _segment_sum(src, seg, n):
    return jax.ops.segment_sum(src, seg, n)
kernel_name = 'mk_conv_attn_hybrid_d2_conv_nhwc256_r2_de2a90'

def setup_inputs(seed: int=0):
    np.random.seed(seed)
    _w = jnp.asarray

    def _rec_inputs():
        import jax
        import jax.numpy as jnp
        _gk = jax.random.key(seed)
        x = -0.0005153 + 1.001 * jax.random.normal(jax.random.fold_in(_gk, 1), (4, 56, 56, 128), jnp.float32)
        return x
    x = _rec_inputs()

    def _L0_conv_setup():
        import jax, jax.numpy as jnp
        import numpy as np
        B, H, W, C, G = (4, 56, 56, 128, 16)
        K = 9
        GC = C // G

        def _ln(x, g, b, eps=1e-05):
            mu = jnp.mean(x, axis=-1, keepdims=True)
            var = jnp.mean(jnp.square(x - mu), axis=-1, keepdims=True)
            return (x - mu) * jax.lax.rsqrt(var + eps) * g + b

        def _gelu(x):
            return jax.nn.gelu(x, approximate=False)

        def _dcnv3_core(x, offset, mask):
            xg = x.reshape(B, H * W, G, GC)
            off = offset.reshape(B, H, W, G, K, 2)
            dy, dx = jnp.meshgrid(jnp.arange(-1.0, 2.0), jnp.arange(-1.0, 2.0), indexing='ij')
            dx = dx.reshape(K).astype(x.dtype)
            dy = dy.reshape(K).astype(x.dtype)
            gx = jnp.arange(W, dtype=x.dtype)[None, None, :, None, None]
            gy = jnp.arange(H, dtype=x.dtype)[None, :, None, None, None]
            px = gx + dx + off[..., 0]
            py = gy + dy + off[..., 1]

            def flat(p):
                return p.transpose(0, 1, 2, 4, 3).reshape(B, H * W * K, G)
            pxf, pyf = (flat(px), flat(py))
            x0 = jnp.floor(pxf)
            y0 = jnp.floor(pyf)
            acc = jnp.zeros((B, H * W * K, G, GC), x.dtype)
            for cx, cy in ((x0, y0), (x0 + 1, y0), (x0, y0 + 1), (x0 + 1, y0 + 1)):
                wgt = (1 - jnp.abs(pxf - cx)) * (1 - jnp.abs(pyf - cy))
                valid = ((cx >= 0) & (cx < W) & (cy >= 0) & (cy < H)).astype(x.dtype)
                idx = (jnp.clip(cy, 0, H - 1).astype(jnp.int32) * W + jnp.clip(cx, 0, W - 1).astype(jnp.int32))[..., None]
                v = jnp.take_along_axis(xg, idx, axis=1)
                acc = acc + (wgt * valid)[..., None] * v
            mf = flat(mask)[..., None]
            out = (acc * mf).reshape(B, H * W, K, G, GC).sum(axis=2)
            return out.reshape(B, H, W, C)

        def _dcn(x, w_in, b_in, w_dw, b_dw, ln_dw_g, ln_dw_b, w_off, b_off, w_mask, b_mask, w_out, b_out):
            xp = x @ w_in + b_in
            x1 = jax.lax.conv_general_dilated(x, w_dw, window_strides=(1, 1), padding='SAME', dimension_numbers=('NHWC', 'HWIO', 'NHWC'), feature_group_count=C) + b_dw
            x1 = _gelu(_ln(x1, ln_dw_g, ln_dw_b))
            offset = x1 @ w_off + b_off
            mask = jax.nn.softmax((x1 @ w_mask + b_mask).reshape(B, H, W, G, K), axis=-1)
            y = _dcnv3_core(xp, offset, mask)
            return y @ w_out + b_out

        def _block(x, w_in, b_in, w_dw, b_dw, ln_dw_g, ln_dw_b, w_off, b_off, w_mask, b_mask, w_out, b_out, ln1_g, ln1_b, w_fc1, b_fc1, w_fc2, b_fc2, ln2_g, ln2_b, gamma1, gamma2):
            y = _dcn(x, w_in, b_in, w_dw, b_dw, ln_dw_g, ln_dw_b, w_off, b_off, w_mask, b_mask, w_out, b_out)
            x = x + gamma1 * _ln(y, ln1_g, ln1_b)
            m = _gelu(x @ w_fc1 + b_fc1) @ w_fc2 + b_fc2
            x = x + gamma2 * _ln(m, ln2_g, ln2_b)
            return x
        key = jax.random.key(seed)
        ks = jax.random.split(key, 9)
        f = jnp.float32

        def rn(k, shape, s=0.02):
            return jax.random.normal(k, shape, dtype=f) * s
        return {'x': jax.random.normal(ks[0], (B, H, W, C), dtype=f), 'w_in': rn(ks[1], (C, C)), 'b_in': jnp.zeros((C,), f), 'w_dw': rn(ks[2], (3, 3, 1, C), 0.1), 'b_dw': jnp.zeros((C,), f), 'ln_dw_g': jnp.ones((C,), f), 'ln_dw_b': jnp.zeros((C,), f), 'w_off': rn(ks[3], (C, G * K * 2)), 'b_off': jnp.zeros((G * K * 2,), f), 'w_mask': rn(ks[4], (C, G * K)), 'b_mask': jnp.zeros((G * K,), f), 'w_out': rn(ks[5], (C, C)), 'b_out': jnp.zeros((C,), f), 'ln1_g': jnp.ones((C,), f), 'ln1_b': jnp.zeros((C,), f), 'w_fc1': rn(ks[6], (C, C)), 'b_fc1': jnp.zeros((C,), f), 'w_fc2': rn(ks[7], (C, C)), 'b_fc2': jnp.zeros((C,), f), 'ln2_g': jnp.ones((C,), f), 'ln2_b': jnp.zeros((C,), f), 'gamma1': jnp.ones((C,), f), 'gamma2': jnp.ones((C,), f)}
    _L0_conv_all = _L0_conv_setup()
    _L0_conv_in = {k: v for k, v in _L0_conv_all.items() if k in ('w_in', 'b_in', 'w_dw', 'b_dw', 'ln_dw_g', 'ln_dw_b', 'w_off', 'b_off', 'w_mask', 'b_mask', 'w_out', 'b_out', 'ln1_g', 'ln1_b', 'w_fc1', 'b_fc1', 'w_fc2', 'b_fc2', 'ln2_g', 'ln2_b', 'gamma1', 'gamma2')}
    del _L0_conv_all

    def _L1_attn_setup():
        import jax, jax.numpy as jnp
        import numpy as np
        B, N, C = (16, 1024, 128)
        C4 = C // 4
        BN_EPS = 1e-05
        key = jax.random.key(seed)
        ks = jax.random.split(key, 9)
        return {'x': jax.random.normal(ks[0], (B, N, C), jnp.float32), 'Wq': jax.random.normal(ks[1], (C4, C), jnp.float32) * (1.0 / np.sqrt(C)), 'Wk': jax.random.normal(ks[2], (C4, C), jnp.float32) * (1.0 / np.sqrt(C)), 'Wv': jax.random.normal(ks[3], (C, C), jnp.float32) * (1.0 / np.sqrt(C)), 'bv': jax.random.normal(ks[4], (C,), jnp.float32) * 0.01, 'Wt': jax.random.normal(ks[5], (C, C), jnp.float32) * (1.0 / np.sqrt(C)), 'bt': jax.random.normal(ks[6], (C,), jnp.float32) * 0.01, 'gamma': jnp.ones((C,), jnp.float32), 'beta': jnp.zeros((C,), jnp.float32), 'bn_mean': jax.random.normal(ks[7], (C,), jnp.float32) * 0.1, 'bn_var': jax.random.uniform(ks[8], (C,), jnp.float32, 0.5, 1.5)}
    _L1_attn_all = _L1_attn_setup()
    _L1_attn_in = {k: v for k, v in _L1_attn_all.items() if k in ('Wq', 'Wk', 'Wv', 'bv', 'Wt', 'bt', 'gamma', 'beta', 'bn_mean', 'bn_var')}
    del _L1_attn_all

    def _L1_ffn_setup():
        import math
        import jax, jax.numpy as jnp
        import numpy as np
        CAPACITY_FACTOR = 1.25
        key = jax.random.key(seed)
        ks = jax.random.split(key, 5)
        B, L, D, F, E = (8, 4096, 128, 512, 8)
        h = jax.random.normal(ks[0], (B, L, D), dtype=jnp.float32)
        gate_w = jax.random.normal(ks[1], (D, E), dtype=jnp.float32) * 0.02
        gate_b = jnp.zeros((E,), dtype=jnp.float32)
        w1 = jax.random.normal(ks[2], (E, D, F), dtype=jnp.float32) * (1.0 / math.sqrt(D))
        b1 = jnp.zeros((E, F), dtype=jnp.float32)
        w2 = jax.random.normal(ks[3], (E, F, D), dtype=jnp.float32) * (1.0 / math.sqrt(F))
        b2 = jnp.zeros((E, D), dtype=jnp.float32)
        return {'h': h, 'gate_w': gate_w, 'gate_b': gate_b, 'w1': w1, 'b1': b1, 'w2': w2, 'b2': b2}
    _L1_ffn_all = _L1_ffn_setup()
    _L1_ffn_in = {k: v for k, v in _L1_ffn_all.items() if k in ('gate_w', 'gate_b', 'w1', 'b1', 'w2', 'b2')}
    del _L1_ffn_all
    return {'x': x, 'L0_conv_w_in': _L0_conv_in['w_in'], 'L0_conv_b_in': _L0_conv_in['b_in'], 'L0_conv_w_dw': _L0_conv_in['w_dw'], 'L0_conv_b_dw': _L0_conv_in['b_dw'], 'L0_conv_ln_dw_g': _L0_conv_in['ln_dw_g'], 'L0_conv_ln_dw_b': _L0_conv_in['ln_dw_b'], 'L0_conv_w_off': _L0_conv_in['w_off'], 'L0_conv_b_off': _L0_conv_in['b_off'], 'L0_conv_w_mask': _L0_conv_in['w_mask'], 'L0_conv_b_mask': _L0_conv_in['b_mask'], 'L0_conv_w_out': _L0_conv_in['w_out'], 'L0_conv_b_out': _L0_conv_in['b_out'], 'L0_conv_ln1_g': _L0_conv_in['ln1_g'], 'L0_conv_ln1_b': _L0_conv_in['ln1_b'], 'L0_conv_w_fc1': _L0_conv_in['w_fc1'], 'L0_conv_b_fc1': _L0_conv_in['b_fc1'], 'L0_conv_w_fc2': _L0_conv_in['w_fc2'], 'L0_conv_b_fc2': _L0_conv_in['b_fc2'], 'L0_conv_ln2_g': _L0_conv_in['ln2_g'], 'L0_conv_ln2_b': _L0_conv_in['ln2_b'], 'L0_conv_gamma1': _L0_conv_in['gamma1'], 'L0_conv_gamma2': _L0_conv_in['gamma2'], 'L1_attn_Wq': _L1_attn_in['Wq'], 'L1_attn_Wk': _L1_attn_in['Wk'], 'L1_attn_Wv': _L1_attn_in['Wv'], 'L1_attn_bv': _L1_attn_in['bv'], 'L1_attn_Wt': _L1_attn_in['Wt'], 'L1_attn_bt': _L1_attn_in['bt'], 'L1_attn_gamma': _L1_attn_in['gamma'], 'L1_attn_beta': _L1_attn_in['beta'], 'L1_attn_bn_mean': _L1_attn_in['bn_mean'], 'L1_attn_bn_var': _L1_attn_in['bn_var'], 'L1_ffn_gate_w': _L1_ffn_in['gate_w'], 'L1_ffn_gate_b': _L1_ffn_in['gate_b'], 'L1_ffn_w1': _L1_ffn_in['w1'], 'L1_ffn_b1': _L1_ffn_in['b1'], 'L1_ffn_w2': _L1_ffn_in['w2'], 'L1_ffn_b2': _L1_ffn_in['b2']}

def reference(x, L0_conv_w_in, L0_conv_b_in, L0_conv_w_dw, L0_conv_b_dw, L0_conv_ln_dw_g, L0_conv_ln_dw_b, L0_conv_w_off, L0_conv_b_off, L0_conv_w_mask, L0_conv_b_mask, L0_conv_w_out, L0_conv_b_out, L0_conv_ln1_g, L0_conv_ln1_b, L0_conv_w_fc1, L0_conv_b_fc1, L0_conv_w_fc2, L0_conv_b_fc2, L0_conv_ln2_g, L0_conv_ln2_b, L0_conv_gamma1, L0_conv_gamma2, L1_attn_Wq, L1_attn_Wk, L1_attn_Wv, L1_attn_bv, L1_attn_Wt, L1_attn_bt, L1_attn_gamma, L1_attn_beta, L1_attn_bn_mean, L1_attn_bn_var, L1_ffn_gate_w, L1_ffn_gate_b, L1_ffn_w1, L1_ffn_b1, L1_ffn_w2, L1_ffn_b2):
    import jax
    import jax.numpy as jnp

    def _L0_conv_ref(x, w_in, b_in, w_dw, b_dw, ln_dw_g, ln_dw_b, w_off, b_off, w_mask, b_mask, w_out, b_out, ln1_g, ln1_b, w_fc1, b_fc1, w_fc2, b_fc2, ln2_g, ln2_b, gamma1, gamma2):
        import jax, jax.numpy as jnp
        import numpy as np
        B, H, W, C, G = (4, 56, 56, 128, 16)
        K = 9
        GC = C // G

        def _ln(x, g, b, eps=1e-05):
            mu = jnp.mean(x, axis=-1, keepdims=True)
            var = jnp.mean(jnp.square(x - mu), axis=-1, keepdims=True)
            return (x - mu) * jax.lax.rsqrt(var + eps) * g + b

        def _gelu(x):
            return jax.nn.gelu(x, approximate=False)

        def _dcnv3_core(x, offset, mask):
            xg = x.reshape(B, H * W, G, GC)
            off = offset.reshape(B, H, W, G, K, 2)
            dy, dx = jnp.meshgrid(jnp.arange(-1.0, 2.0), jnp.arange(-1.0, 2.0), indexing='ij')
            dx = dx.reshape(K).astype(x.dtype)
            dy = dy.reshape(K).astype(x.dtype)
            gx = jnp.arange(W, dtype=x.dtype)[None, None, :, None, None]
            gy = jnp.arange(H, dtype=x.dtype)[None, :, None, None, None]
            px = gx + dx + off[..., 0]
            py = gy + dy + off[..., 1]

            def flat(p):
                return p.transpose(0, 1, 2, 4, 3).reshape(B, H * W * K, G)
            pxf, pyf = (flat(px), flat(py))
            x0 = jnp.floor(pxf)
            y0 = jnp.floor(pyf)
            acc = jnp.zeros((B, H * W * K, G, GC), x.dtype)
            for cx, cy in ((x0, y0), (x0 + 1, y0), (x0, y0 + 1), (x0 + 1, y0 + 1)):
                wgt = (1 - jnp.abs(pxf - cx)) * (1 - jnp.abs(pyf - cy))
                valid = ((cx >= 0) & (cx < W) & (cy >= 0) & (cy < H)).astype(x.dtype)
                idx = (jnp.clip(cy, 0, H - 1).astype(jnp.int32) * W + jnp.clip(cx, 0, W - 1).astype(jnp.int32))[..., None]
                v = jnp.take_along_axis(xg, idx, axis=1)
                acc = acc + (wgt * valid)[..., None] * v
            mf = flat(mask)[..., None]
            out = (acc * mf).reshape(B, H * W, K, G, GC).sum(axis=2)
            return out.reshape(B, H, W, C)

        def _dcn(x, w_in, b_in, w_dw, b_dw, ln_dw_g, ln_dw_b, w_off, b_off, w_mask, b_mask, w_out, b_out):
            xp = x @ w_in + b_in
            x1 = jax.lax.conv_general_dilated(x, w_dw, window_strides=(1, 1), padding='SAME', dimension_numbers=('NHWC', 'HWIO', 'NHWC'), feature_group_count=C) + b_dw
            x1 = _gelu(_ln(x1, ln_dw_g, ln_dw_b))
            offset = x1 @ w_off + b_off
            mask = jax.nn.softmax((x1 @ w_mask + b_mask).reshape(B, H, W, G, K), axis=-1)
            y = _dcnv3_core(xp, offset, mask)
            return y @ w_out + b_out

        def _block(x, w_in, b_in, w_dw, b_dw, ln_dw_g, ln_dw_b, w_off, b_off, w_mask, b_mask, w_out, b_out, ln1_g, ln1_b, w_fc1, b_fc1, w_fc2, b_fc2, ln2_g, ln2_b, gamma1, gamma2):
            y = _dcn(x, w_in, b_in, w_dw, b_dw, ln_dw_g, ln_dw_b, w_off, b_off, w_mask, b_mask, w_out, b_out)
            x = x + gamma1 * _ln(y, ln1_g, ln1_b)
            m = _gelu(x @ w_fc1 + b_fc1) @ w_fc2 + b_fc2
            x = x + gamma2 * _ln(m, ln2_g, ln2_b)
            return x
        return _block(x, w_in, b_in, w_dw, b_dw, ln_dw_g, ln_dw_b, w_off, b_off, w_mask, b_mask, w_out, b_out, ln1_g, ln1_b, w_fc1, b_fc1, w_fc2, b_fc2, ln2_g, ln2_b, gamma1, gamma2)

    def _L1_attn_ref(x, Wq, Wk, Wv, bv, Wt, bt, gamma, beta, bn_mean, bn_var):
        import jax, jax.numpy as jnp
        import numpy as np
        B, N, C = (16, 1024, 128)
        C4 = C // 4
        BN_EPS = 1e-05
        xc = jnp.transpose(x, (0, 2, 1))
        q = jnp.einsum('oc,bcn->bno', Wq, xc)
        k = jnp.einsum('oc,bcn->bon', Wk, xc)
        energy = jnp.einsum('bno,bom->bnm', q, k)
        attn = jax.nn.softmax(energy, axis=-1)
        attn = attn / (1e-06 + jnp.sum(attn, axis=1, keepdims=True))
        x_r = jnp.einsum('bcn,bnm->bcm', xc, attn)
        d = xc - x_r
        t = jnp.einsum('oc,bcn->bon', Wt, d) + bt[None, :, None]
        bn = gamma[None, :, None] * (t - bn_mean[None, :, None]) * jax.lax.rsqrt(bn_var[None, :, None] + BN_EPS) + beta[None, :, None]
        out = xc + jnp.maximum(bn, 0.0)
        return jnp.transpose(out, (0, 2, 1))

    def _L1_ffn_ref(h, gate_w, gate_b, w1, b1, w2, b2):
        import math
        import jax, jax.numpy as jnp
        import numpy as np
        CAPACITY_FACTOR = 1.25
        B, L, D = h.shape
        E = gate_w.shape[1]
        T = B * L
        C = max(1, math.ceil(CAPACITY_FACTOR * T / E))
        x = h.reshape(T, D)
        logits = x @ gate_w + gate_b
        probs = jax.nn.softmax(logits, axis=-1)
        idx = jnp.argmax(probs, axis=-1)
        prb = jnp.take_along_axis(probs, idx[:, None], axis=1)[:, 0]
        one_hot = jax.nn.one_hot(idx, E, dtype=jnp.float32)
        pos = (jnp.cumsum(one_hot, axis=0) * one_hot).sum(-1).astype(jnp.int32) - 1
        kept = pos < C
        pos_safe = jnp.where(kept, pos, C)
        buf = jnp.zeros((E, C, D), dtype=h.dtype).at[idx, pos_safe].set(x, mode='drop')
        hmid = jax.nn.relu(jnp.einsum('ecd,edf->ecf', buf, w1) + b1[:, None, :])
        ybuf = jnp.einsum('ecf,efd->ecd', hmid, w2) + b2[:, None, :]
        pos_g = jnp.minimum(pos, C - 1)
        y_tok = ybuf[idx, pos_g] * (prb * kept)[:, None]
        y = y_tok.reshape(B, L, D)
        y = jnp.nan_to_num(y, nan=0.0, posinf=10000.0, neginf=-10000.0)
        return y

    def _gn(v, G=32, eps=1e-05):
        B_, H_, W_, C_ = v.shape
        g = v.reshape(B_, H_, W_, G, C_ // G)
        m = jnp.mean(g, axis=(1, 2, 4), keepdims=True)
        s = jnp.var(g, axis=(1, 2, 4), keepdims=True)
        return ((g - m) / jnp.sqrt(s + eps)).reshape(v.shape)

    def _ln_c(v, eps=1e-06):
        m = jnp.mean(v, axis=-1, keepdims=True)
        s = jnp.var(v, axis=-1, keepdims=True)
        return (v - m) / jnp.sqrt(s + eps)

    def _ln_t(v, eps=1e-05):
        m = jnp.mean(v, axis=-1, keepdims=True)
        s = jnp.var(v, axis=-1, keepdims=True)
        return (v - m) / jnp.sqrt(s + eps)

    def _to_tokens(v):
        B_, H_, W_, C_ = v.shape
        return v.reshape(B_, H_ * W_, C_)

    def _from_tokens(t, like):
        return t.reshape(like.shape)
    x = _L0_conv_ref(x, L0_conv_w_in, L0_conv_b_in, L0_conv_w_dw, L0_conv_b_dw, L0_conv_ln_dw_g, L0_conv_ln_dw_b, L0_conv_w_off, L0_conv_b_off, L0_conv_w_mask, L0_conv_b_mask, L0_conv_w_out, L0_conv_b_out, L0_conv_ln1_g, L0_conv_ln1_b, L0_conv_w_fc1, L0_conv_b_fc1, L0_conv_w_fc2, L0_conv_b_fc2, L0_conv_ln2_g, L0_conv_ln2_b, L0_conv_gamma1, L0_conv_gamma2)
    t = _to_tokens(x)
    t = t + _L1_attn_ref(_ln_t(t), L1_attn_Wq, L1_attn_Wk, L1_attn_Wv, L1_attn_bv, L1_attn_Wt, L1_attn_bt, L1_attn_gamma, L1_attn_beta, L1_attn_bn_mean, L1_attn_bn_var)
    t = t + _L1_ffn_ref(_ln_t(t), L1_ffn_gate_w, L1_ffn_gate_b, L1_ffn_w1, L1_ffn_b1, L1_ffn_w2, L1_ffn_b2)
    x = _from_tokens(t, x)
    return x

_drawn_inputs = setup_inputs


def setup_inputs(seed=0):
    import zlib

    import numpy as np

    out = dict(_drawn_inputs(seed))
    spreads = {'L0_conv_b_in': (0.0, 0.1),
     'L0_conv_b_dw': (0.0, 0.756),
     'L0_conv_ln_dw_g': (1.0, 0.6),
     'L0_conv_ln_dw_b': (0.0, 2.0),
     'L0_conv_b_off': (0.0, 0.445),
     'L0_conv_b_out': (0.0, 0.1),
     'L0_conv_ln1_g': (1.0, 0.2),
     'L0_conv_ln1_b': (0.0, 0.1),
     'L0_conv_b_fc1': (0.0, 0.1),
     'L0_conv_b_fc2': (0.0, 0.1),
     'L0_conv_ln2_g': (1.0, 0.2),
     'L0_conv_ln2_b': (0.0, 0.1),
     'L0_conv_gamma1': (1.0, 0.2),
     'L0_conv_gamma2': (1.0, 0.2),
     'L1_attn_gamma': (1.0, 0.2),
     'L1_attn_beta': (0.0, 0.32),
     'L1_ffn_gate_b': (0.0, 0.724),
     'L1_ffn_b1': (0.0, 2.0),
     'L1_ffn_b2': (0.0, 0.8)}
    factors = {'L1_attn_bt': 8.0, 'L1_ffn_w1': 2.763, 'L0_conv_w_dw': 3.358}
    for name, (base, spread) in spreads.items():
        noise = np.random.default_rng([zlib.crc32(name.encode()), seed]).standard_normal(out[name].shape)
        drawn = base * np.exp(spread * noise) if base else spread * noise
        out[name] = jnp.asarray(drawn.astype(out[name].dtype))
    for name, factor in factors.items():
        out[name] = (out[name] * factor).astype(out[name].dtype)
    return out
```

```python
from contextlib import ExitStack

import concourse.bass as bass
from concourse import mybir

F32 = mybir.dt.float32
I32 = mybir.dt.int32
ALU = mybir.AluOpType
ACT = mybir.ActivationFunctionType
AX = mybir.AxisListType.X
MAX = bass.bass_isa.ReduceOp.max

B, H, W, C = 4, 56, 56, 128
G, K = 16, 9
GC = C // G
HH = H // 2
TP = 2 * W
NPIX = H * W
T = B * NPIX
GK = G * K
OM = 3 * GK
QT = 4
NQ = HH // QT
NB = B * NQ

R = 7
CW = R + 2
ROWS = HH + CW - 1
RING = 16
OFFMAX = 60.0
PAD = (int(OFFMAX) + R + 6) * W
EPS = 1e-5


class Ctx:

    def __init__(self, nc, stack, stage):
        self.nc, self.stack, self.stage, self.sems = nc, stack, stage, []
        stack.callback(self.close)

    def sb(self, name, shape, dt=F32):
        return self.stack.enter_context(self.nc.sbuf_tensor(f"{self.stage}_{name}", shape, dt))

    def ps(self, name, shape):
        return self.stack.enter_context(self.nc.psum_tensor(f"{self.stage}_{name}", shape, F32))

    def sem(self, name):
        self.sems.append(self.nc.alloc_semaphore(f"{self.stage}_{name}"))
        return self.sems[-1]

    def close(self):
        if self.sems:
            self.nc.clear_and_free_semaphores(self.sems)
            self.nc.all_engine_barrier()


def spread(ap, axis, n):
    v = ap.unsqueeze(axis)
    shape = list(v.shape)
    shape[axis] = n
    return v.to_broadcast(shape)


def row(ap):
    return ap.rearrange("(a n) -> a n", a=1)


def col(ap):
    return ap.rearrange("(n a) -> n a", a=1)


def hold(eng, sem, value, own):
    eng.wait_ge(sem, value)
    eng.sem_inc(own, 1)


def identity(nc, c):
    k = {"ident": c.sb("ident", [128, 128]), "own": c.sem("wait_carrier")}
    with ExitStack() as es:
        t = Ctx(nc, es, "identity")
        zeroed = t.sem("zeroed")
        with nc.Block() as block:

            @block.gpsimd
            def _(pool):
                pool.memset(k["ident"][:, :], 0.0).then_inc(zeroed, 1)
                pool.wait_ge(zeroed, 1)
                pool.affine_select(out=k["ident"][:, :], in_=k["ident"][:, :], compare_op=ALU.not_equal, fill=1.0,
                                   base=0, pattern=[[-1, 128]], channel_multiplier=1)
    return k


def constants(nc, c, ins, k):
    for name, src in (("w_in", "L0_conv_w_in"), ("w_out", "L0_conv_w_out"), ("w_fc1", "L0_conv_w_fc1"),
                      ("w_fc2", "L0_conv_w_fc2")):
        k[name] = c.sb(name, [C, C])
    k["w_dw"] = c.sb("w_dw", [C, K])
    k["w_om"] = c.sb("w_om", [C, OM])
    k["b_om"] = c.sb("b_om", [128, OM])
    for name in ("b_in", "b_out", "ln1_g", "ln1_b", "b_fc2", "ln2_g", "ln2_b", "gamma1", "gamma2"):
        k[name] = c.sb(name + "_rows", [128, C])
    for name in ("b_dw", "ln_dw_g", "ln_dw_b", "b_fc1"):
        k[name] = c.sb(name + "_col", [C, 1])
    with ExitStack() as es:
        t = Ctx(nc, es, "const")
        raw_w = t.sb("raw_w", [C, OM])
        raw_b = t.sb("raw_b", [128, OM])
        raw_d = t.sb("raw_dw", [K, C])
        loaded, turned = t.sem("loaded"), t.sem("turned")
        psw = t.ps("psw", [C, 512])
        with nc.Block() as block:
            n_loads = [0]

            @block.sync
            def _(sp):
                def load(dst, src):
                    sp.dma_start(dst, src).then_inc(loaded, 16)
                    n_loads[0] += 16

                for name in ("w_in", "w_out", "w_fc1", "w_fc2"):
                    load(k[name][:, :], ins["L0_conv_" + name])
                load(raw_d[:, :], ins["L0_conv_w_dw"].rearrange("a b o c -> (a b o) c"))
                load(raw_w[:, 0:2 * GK], ins["L0_conv_w_off"])
                load(raw_w[:, 2 * GK:OM], ins["L0_conv_w_mask"])
                load(raw_b[:, 0:2 * GK], row(ins["L0_conv_b_off"]).to_broadcast([128, 2 * GK]))
                load(raw_b[:, 2 * GK:OM], row(ins["L0_conv_b_mask"]).to_broadcast([128, GK]))
                for name in ("b_in", "b_out", "ln1_g", "ln1_b", "b_fc2", "ln2_g", "ln2_b", "gamma1", "gamma2"):
                    load(k[name][:, :], row(ins["L0_conv_" + name]).to_broadcast([128, C]))
                for name in ("b_dw", "ln_dw_g", "ln_dw_b", "b_fc1"):
                    load(k[name][:, :], col(ins["L0_conv_" + name]))

            @block.tensor
            def _(pe):
                pe.wait_ge(loaded, n_loads[0])
                pe.transpose(psw[:, 0:K], raw_d[:, :], k["ident"][0:K, 0:K]).then_inc(turned, 1)

            @block.vector
            def _(dve):
                dve.wait_ge(loaded, n_loads[0])
                for raw, dst in ((raw_w, k["w_om"]), (raw_b, k["b_om"])):
                    for xy in range(2):
                        nc.vector.tensor_copy(
                            dst[:, xy * GK:(xy + 1) * GK].rearrange("c (k g) -> c k g", g=G),
                            raw[:, 0:2 * GK].rearrange("c (g k d) -> c k g d", k=K, d=2)[:, :, :, xy])
                    nc.vector.tensor_copy(dst[:, 2 * GK:OM].rearrange("c (k g) -> c k g", g=G),
                                          raw[:, 2 * GK:OM].rearrange("c (g k) -> c k g", k=K))
                dve.wait_ge(turned, 1)
                nc.vector.tensor_copy(k["w_dw"][:, :], psw[:, 0:K])


def offsets_stage(nc, k, x, xp_d, om_d, extremes):
    own, ident = k["own"], k["ident"]
    with ExitStack() as es:
        t = Ctx(nc, es, "offs")
        x_sb = t.sb("x_sb", [TP, HH, C])
        xpad = t.sb("xpad", [C, (H + 2) * (W + 2)])
        xt = t.sb("xt", [C, HH, TP])
        conv = t.sb("conv", [C, HH, 2, W])
        st = t.sb("st", [TP, 2, QT, 6])
        mv = t.sb("mv", [TP, 2, QT, 2])
        ve = t.sb("ve", [TP, 2, QT])
        rs = t.sb("rs", [TP, 2, QT])
        half = t.sb("half", [TP, QT])
        xn = t.sb("xn", [TP, 2, QT, C])
        x1t = t.sb("x1t", [C, 2, QT * TP])
        om = t.sb("om", [TP, 2, QT, OM])
        mx = t.sb("mx", [TP, 2, QT, G])
        xp = t.sb("xp", [TP, 2, QT, C])
        zero = t.sb("zero", [TP, 4 * C])
        ps_x = [t.ps(f"ps_x{i}", [C, 512]) for i in range(1)]
        ps_c = t.ps("ps_c", [TP, 512])
        ps_n = t.ps("ps_n", [C, 512])
        ps_o = t.ps("ps_o", [TP, QT, 512])
        ps_p = t.ps("ps_p", [TP, 512])
        (x_in, x_used, xT, xT_ev, xT_out, conv_step, conv_done, convT, convT_used, stat, agg, eps, rstd, xn_ok, xnT,
         x1, om_ps, om_ev, om_sub, om_exp, om_clamp, om_max, om_ok, xp_ok, om_st, xp_st, ext, zr, half_ok, xz, pad_st) = [
            t.sem(s) for s in (
                "x_loaded", "x_used", "xT_in_psum", "xT_evacuated", "xT_copied", "conv_step", "conv_done",
                "convT_in_psum", "convT_used", "stats_ready", "mean_var_ready", "var_eps_ready", "rstd_ready",
                "xn_ready", "xnT_in_psum", "x1_ready", "om_in_psum", "om_evacuated", "om_less_max", "om_exp", "om_clamped", "om_max_ready",
                "om_ready", "xp_ready", "om_stored", "xp_stored", "extremes_done", "pad_zero_ready", "half_ready",
                "xpad_zeroed", "pad_stored")]
        xv = x.rearrange("b (h j) x c -> b h x j c", h=2)
        xpv = xp_d[PAD:PAD + T, :].rearrange("(b h j x) c -> b h x j c", b=B, h=2, x=W)
        xpad3 = xpad[:, :].rearrange("c (y x) -> c y x", x=W + 2)
        with nc.Block() as block:

            @block.sync
            def _(sp):
                sp.wait_ge(zr, 1)
                rows_out = TP * 4
                for base in (0, PAD + T):
                    for r0 in range(0, PAD, rows_out):
                        n = min(rows_out, PAD - r0) // 4
                        sp.dma_start(xp_d[base + r0:base + r0 + 4 * n, :].rearrange("(p f) c -> p (f c)", f=4),
                                     zero[0:n, :]).then_inc(pad_st, 16)
                npad = 2 * len(range(0, PAD, rows_out))

                def load(b):
                    for h in range(2):
                        sp.dma_start(x_sb[h * W:(h + 1) * W, :, :], xv[b, h]).then_inc(x_in, 16)

                load(0)
                for b in range(B):
                    if b + 1 < B:
                        sp.wait_ge(x_used, b + 1)
                        load(b + 1)
                    with sp.Fori(0, NQ) as q:
                        n = q + b * NQ
                        sp.wait_ge(xp_ok, n + 1)
                        for h in range(2):
                            sp.dma_start(xpv[b, h, :, bass.ds(q * QT, QT), :],
                                         xp[h * W:(h + 1) * W, n % 2, :, :]).then_inc(xp_st, 16)
                        sp.wait_ge(om_ok, n + 1)
                        sp.dma_start(om_d[bass.ds(n * QT, QT), :, :].rearrange("t p o -> p t o"),
                                     om[:, n % 2, :, :]).then_inc(om_st, 16)
                sp.wait_ge(pad_st, 16 * npad)
                sp.wait_ge(xp_st, 32 * NB + 1)
                sp.wait_ge(om_st, 16 * NB + 1)

            @block.gpsimd
            def _(pool):
                pool.memset(half[:, :], -0.5).then_inc(half_ok, 1)
                pool.wait_ge(half_ok, 1)
                with pool.Fori(0, B) as b:
                    for q in range(NQ):
                        n = b * NQ + q
                        hold(pool, agg, n + 1, own)
                        pool.tensor_scalar(ve[:, q % 2, :], mv[:, q % 2, :, 1], EPS, None, ALU.add).then_inc(eps, 1)
                        hold(pool, eps, n + 1, own)
                        pool.tensor_tensor(rs[:, q % 2, :], ve[:, q % 2, :], half[:, :], ALU.pow).then_inc(rstd, 1)

            @block.tensor
            def _(pe):
                def conv_turn(n, q):
                    hold(pe, convT_used, n + 1, own)
                    for i in range(QT):
                        mm = pe.transpose(ps_c[:, i * C:(i + 1) * C],
                                          conv[:, q * QT + i, :, :].rearrange("c h x -> c (h x)"), ident[:, :])
                    mm.then_inc(convT, 1)

                with pe.Fori(0, B) as b:
                    hold(pe, x_in, 32 * b + 32, own)
                    for q in range(NQ):
                        hold(pe, xT_ev, b * NQ + q + 1, own)
                        for i in range(QT):
                            mm = pe.transpose(ps_x[0][:, i * TP:(i + 1) * TP], x_sb[:, q * QT + i, :],
                                              ident[0:TP, 0:TP])
                        mm.then_inc(xT, 1)
                    hold(pe, conv_done, b + 1 + 1, own)
                    conv_turn(b * NQ, 0)
                    for q in range(NQ):
                        n = b * NQ + q
                        if q + 1 < NQ:
                            conv_turn(n + 1, q + 1)
                        hold(pe, xn_ok, n + 1, own)
                        hold(pe, x1, n + 1, own)
                        for i in range(QT):
                            mm = pe.transpose(ps_n[:, i * TP:(i + 1) * TP], xn[:, q % 2, i, :],
                                              ident[0:TP, 0:TP])
                        mm.then_inc(xnT, 1)
                        hold(pe, om_ev, n + 1, own)
                        for i in range(QT):
                            mm = pe.matmul(ps_p[:, i * C:(i + 1) * C], xt[:, q * QT + i, :], k["w_in"][:, :],
                                           start=True, stop=True)
                        hold(pe, x1, n + 2, own)
                        for i in range(QT):
                            mm = pe.matmul(ps_o[:, i, 0:OM], x1t[:, q % 2, i * TP:(i + 1) * TP],
                                           k["w_om"][:, :], start=True, stop=True)
                        mm.then_inc(om_ps, 1)

            @block.scalar
            def _(act):
                act.sem_inc(xT_ev, 1)
                act.sem_inc(x1, 1)
                act.wait_ge(xz, 1)
                with act.Fori(0, B) as b:
                    for q in range(NQ):
                        n = b * NQ + q
                        if q == 0:
                            hold(act, conv_done, b + 1, own)
                            hold(act, om_ps, b * NQ + 1, own)
                        hold(act, xT, n + 1, own)
                        src = ps_x[0][:, 0:QT * TP].rearrange("c (j h x) -> c j h x", h=2, x=W)
                        for h in range(2):
                            y = h * HH + q * QT + 1
                            nc.scalar.activation(xpad3[:, y:y + QT, 1:W + 1], src[:, :, h, :], ACT.Copy)
                        nc.scalar.activation(xt[:, q * QT:(q + 1) * QT, :],
                                             ps_x[0][:, 0:QT * TP].rearrange("c (j p) -> c j p", p=TP),
                                             ACT.Copy).then_inc(xT_ev, 1)
                        if q == NQ - 1:
                            act.drain().then_inc(x_used, 1)
                    for q in range(NQ):
                        n = b * NQ + q
                        hold(act, xnT, n + 1, own)
                        hold(act, om_ps, n + 1, own)
                        nc.scalar.activation(x1t[:, q % 2, :], ps_n[:, 0:QT * TP], ACT.Gelu,
                                             bias=k["ln_dw_b"][:, 0:1], scale=k["ln_dw_g"][:, 0:1]).then_inc(x1, 1)
                        hold(act, om_sub, n + 1, own)
                        masks = om[:, n % 2, :, 2 * GK:OM]
                        nc.scalar.activation(masks, masks, ACT.Exp).then_inc(om_exp, 1)

            @block.vector
            def _(dve):
                nc.vector.memset(zero[:, :], 0.0).then_inc(zr, 1)
                nc.vector.memset(xpad[:, :], 0.0).then_inc(xz, 1)
                dve.sem_inc(convT_used, 1)
                dve.sem_inc(om_ev, 1)
                for s in (convT, conv_done, om_ps, om_st, xp_st):
                    dve.sem_inc(s, 1)

                def normalise(n, q):
                    hold(dve, convT, n + 1 + 1, own)
                    for i in range(QT):
                        ins_ = nc.vector.bn_stats(st[:, q % 2, i, :], ps_c[:, i * C:(i + 1) * C])
                    ins_.then_inc(stat, 1)
                    hold(dve, stat, n + 1, own)
                    for i in range(QT):
                        ins_ = nc.vector.bn_aggr(mv[:, q % 2, i, :], st[:, q % 2, i, :])
                    ins_.then_inc(agg, 1)
                    hold(dve, rstd, n + 1, own)
                    for i in range(QT):
                        ins_ = nc.vector.tensor_scalar(xn[:, q % 2, i, :], ps_c[:, i * C:(i + 1) * C],
                                                       mv[:, q % 2, i, 0:1], rs[:, q % 2, i:i + 1],
                                                       ALU.subtract, ALU.mult)
                    ins_.then_inc(xn_ok, 1)
                    dve.wait_ge(xn_ok, n + 1)
                    dve.sem_inc(convT_used, 1)

                def evacuate(n):
                    hold(dve, om_ps, n + 1 + 1, own)
                    hold(dve, om_st, 16 * n + 1, own)
                    hold(dve, xp_st, 32 * n + 1, own)
                    nc.vector.tensor_tensor(xp[:, n % 2, :, :],
                                            ps_p[:, :].rearrange("p (t c) -> p t c", c=C),
                                            spread(k["b_in"][0:TP, :], 1, QT), ALU.add).then_inc(xp_ok, 1)
                    nc.vector.tensor_tensor(om[:, n % 2, :, :], ps_o[:, :, 0:OM],
                                            spread(k["b_om"][0:TP, :], 1, QT), ALU.add).then_inc(om_ev, 1)
                    hold(dve, om_ev, n + 2, own)
                    logits = om[:, n % 2, :, 2 * GK:OM]
                    nc.vector.tensor_reduce(mx[:, n % 2, :, :], logits.rearrange("p t (k g) -> p t g k", g=G),
                                            AX, ALU.max).then_inc(om_max, 1)
                    nc.vector.tensor_scalar(om[:, n % 2, :, 0:2 * GK], om[:, n % 2, :, 0:2 * GK],
                                            OFFMAX, -OFFMAX, ALU.min, ALU.max).then_inc(om_clamp, 1)
                    lk = logits.rearrange("p t (k g) -> p t k g", g=G)
                    hold(dve, om_max, 4 * n + 1, own)
                    nc.vector.tensor_tensor(lk, lk, spread(mx[:, n % 2, :, :], 2, K), ALU.subtract)\
                        .then_inc(om_sub, 1)
                    hold(dve, om_clamp, n + 1, own)
                    for xy in range(2):
                        part = om[:, n % 2, :, xy * GK:(xy + 1) * GK]
                        nc.vector.tensor_reduce(extremes[:, n, 2 * xy:2 * xy + 1], part, mybir.AxisListType.XY,
                                                ALU.min, negate=True)
                        last = nc.vector.tensor_reduce(extremes[:, n, 2 * xy + 1:2 * xy + 2], part,
                                                       mybir.AxisListType.XY, ALU.max)
                    hold(dve, om_exp, n + 1, own)
                    nc.vector.tensor_reduce(mx[:, n % 2, :, :], logits.rearrange("p t (k g) -> p t g k", g=G),
                                            AX, ALU.add).then_inc(om_max, 1)
                    hold(dve, om_max, 4 * n + 2, own)
                    nc.vector.reciprocal(mx[:, n % 2, :, :], mx[:, n % 2, :, :]).then_inc(om_max, 1)
                    hold(dve, om_max, 4 * n + 3, own)
                    nc.vector.tensor_tensor(lk, lk, spread(mx[:, n % 2, :, :], 2, K), ALU.mult)\
                        .then_inc(om_max, 1)
                    dve.wait_ge(om_max, 4 * n + 4)
                    dve.sem_inc(om_ok, 1)

                taps = [(ky, kx, h) for ky in range(3) for kx in range(3) for h in range(2)]
                with dve.Fori(0, B) as b:
                    hold(dve, xT_ev, NQ * b + NQ + 1, own)
                    hold(dve, convT, NQ * b + 1, own)
                    for s, (ky, kx, h) in enumerate(taps):
                        out = conv[:, :, h, :]
                        src = xpad3[:, h * HH + ky:h * HH + ky + HH, kx:kx + W]
                        tap = k["w_dw"][:, 3 * ky + kx:3 * ky + kx + 1]
                        if s < 2:
                            nc.vector.tensor_scalar(out, src, tap, k["b_dw"][:, 0:1], ALU.mult, ALU.add)\
                                .then_inc(conv_step, 1)
                        else:
                            dve.wait_ge(conv_step, b * len(taps) + s - 1)
                            nc.vector.scalar_tensor_tensor(out, src, tap, out, ALU.mult, ALU.add)\
                                .then_inc(conv_step, 1)
                    hold(dve, conv_step, b * len(taps) + len(taps), own)
                    dve.sem_inc(conv_done, 1)
                    normalise(b * NQ, 0)
                    for q in range(NQ):
                        n = b * NQ + q
                        if q + 1 < NQ:
                            normalise(n + 1, q + 1)
                        evacuate(n)


def window_stage(nc, k, extremes, base, counts):
    own = k["own"]
    with ExitStack() as es:
        t = Ctx(nc, es, "window")
        ext = t.sb("ext", [TP, 4])
        ext_all = t.sb("ext_all", [TP, 4])
        ei = t.sb("ei", [TP, 4], I32)
        ef = t.sb("ef", [TP, 4])
        eg = t.sb("eg", [TP, 4])
        nb = t.sb("nb", [TP, 2])
        step, allm = t.sem("w_step"), t.sem("w_all")
        with nc.Block() as block:

            @block.gpsimd
            def _(pool):
                pool.wait_ge(step, 1)
                pool.partition_all_reduce(ext_all[:, :], ext[:, :], TP, MAX).then_inc(allm, 1)

            @block.vector
            def _(dve):
                n = [0]

                def do(ins_):
                    n[0] += 1
                    ins_.then_inc(step, 1)
                    dve.wait_ge(step, n[0])

                do(nc.vector.tensor_reduce(ext[:, :], extremes[:, :, :].rearrange("p n s -> p s n"), AX, ALU.max))
                dve.wait_ge(allm, 1)
                for c0 in (0, 2):
                    do(nc.vector.tensor_scalar(ext_all[:, c0:c0 + 1], ext_all[:, c0:c0 + 1], -1.0, None, ALU.mult))

                def floor(v, out, i, f):
                    do(nc.vector.tensor_copy(i, v))
                    do(nc.vector.tensor_copy(f, i))
                    do(nc.vector.tensor_tensor(out, f, v, ALU.is_gt))
                    do(nc.vector.tensor_tensor(out, f, out, ALU.subtract))

                floor(ext_all[:, :], eg[:, :], ei[:, :], ef[:, :])
                do(nc.vector.tensor_copy(base[:, :], eg[:, 0::2]))
                do(nc.vector.tensor_tensor(nb[:, :], eg[:, 1::2], eg[:, 0::2], ALU.subtract))
                do(nc.vector.tensor_scalar(nb[:, :], nb[:, :], float(2 + R - 1) + 0.1, 1.0 / R, ALU.add, ALU.mult))
                floor(nb[:, :], ef[:, 0:2], ei[:, 0:2], eg[:, 0:2])
                do(nc.vector.tensor_copy(counts[:, 0:2], ef[0:1, 0:2]))
                do(nc.vector.tensor_copy(counts[:, 2:4], base[0:1, 0:2]))


def shift_tables(nc, k, c):
    k["steps"] = c.sb("steps", [TP, R])
    k["xpos"] = c.sb("xpos", [TP, CW])
    k["ypos"] = c.sb("ypos", [TP, ROWS])
    with ExitStack() as es:
        t = Ctx(nc, es, "tables")
        raw = t.sb("raw", [TP, ROWS], I32)
        part = t.sb("part", [TP, 1], I32)
        pf = t.sb("pf", [TP, 1])
        hf = t.sb("hf", [TP, 1])
        hx = t.sb("hx", [TP, 1])
        made, step = t.sem("t_made"), t.sem("t_step")
        with nc.Block() as block:

            @block.gpsimd
            def _(pool):
                pool.iota(raw[:, :], [[1, ROWS]], base=0, channel_multiplier=0).then_inc(made, 1)
                pool.iota(part[:, :], [[1, 1]], base=0, channel_multiplier=1).then_inc(made, 1)

            @block.vector
            def _(dve):
                n = [0]

                def do(ins_):
                    n[0] += 1
                    ins_.then_inc(step, 1)
                    dve.wait_ge(step, n[0])

                dve.wait_ge(made, 2)
                do(nc.vector.tensor_copy(pf[:, :], part[:, :]))
                do(nc.vector.tensor_copy(k["steps"][:, :], raw[:, 0:R]))
                do(nc.vector.tensor_copy(k["xpos"][:, :], raw[:, 0:CW]))
                do(nc.vector.tensor_copy(k["ypos"][:, :], raw[:, :]))
                do(nc.vector.tensor_scalar(hf[:, :], pf[:, :], W - 0.5, None, ALU.is_gt))
                do(nc.vector.tensor_scalar(hx[:, :], hf[:, :], -float(W), pf[:, 0:1], ALU.mult, ALU.add))
                do(nc.vector.tensor_scalar(k["xpos"][:, :], k["xpos"][:, :], hx[:, 0:1], -1.0, ALU.add, ALU.add))
                do(nc.vector.tensor_scalar(hf[:, :], hf[:, :], float(HH), -1.0, ALU.mult, ALU.add))
                do(nc.vector.tensor_scalar(k["ypos"][:, :], k["ypos"][:, :], hf[:, 0:1], None, ALU.add))


def zero_stage(nc, regions):
    with ExitStack() as es:
        t = Ctx(nc, es, "zero")
        wide = 64 * C
        z = t.sb("z", [128, wide])
        made, stored = t.sem("made"), t.sem("stored")
        with nc.Block() as block:

            @block.vector
            def _(dve):
                nc.vector.memset(z[:, :], 0.0).then_inc(made, 1)

            @block.sync
            def _(sp):
                sp.wait_ge(made, 1)
                count = 0
                for flat in regions:
                    v = flat.rearrange("(p n) -> p n", p=128)
                    for i in range(0, v.shape[1], wide):
                        n = min(wide, v.shape[1] - i)
                        sp.dma_start(v[:, i:i + n], z[:, 0:n]).then_inc(stored, 16)
                        count += 16
                sp.wait_ge(stored, count)


POOL_TAPS = [6, 7, 8, 5, 4]
DVE_TAPS = [k for k in range(K) if k not in POOL_TAPS]
NPROD = 3
LOW = 1


def window_pass(nc, k, t, bufs, sems, xp_d, om_d, y_d, row0, col0):
    own, ident = k["own"], k["ident"]
    (om, ab, hat, hym, wd, wp, ad, ap, prod, ring, yprev, yout, mask, negr, zeros, cur, vt) = bufs
    (setup, om_in, yp_in, row_in, masked, abs_ok, hats_ok, blank, hym_ok, pstep, wp_ok, w_done, dstep,
     prod_ok, prod_used, acc_free, y_ok, y_st, tile_done, applied) = sems
    acc = t["acc"]
    xpt = xp_d.tensor

    with nc.Block() as block:

        @block.sync
        def _(sp):
            def load_row(b, u, prior):
                if prior is not None:
                    sp.wait_ge(row_in, prior)
                slot = (u + b * ROWS) % RING
                for h in range(2):
                    pix = (u + (row0 - 1 + h * HH)) * W + (col0 - 1 + PAD + b * NPIX)
                    src = bass.AP(xpt, pix * C, [[C, W], [1, CW * C]])
                    sp.dma_start(ring[h * W:(h + 1) * W, slot, :], src).then_inc(row_in, 16)

            def load_tile(n):
                sp.dma_start(om[:, n % 2, :], om_d[n, :, :]).then_inc(om_in, 16)
                sp.dma_start(yprev[:, n % 2, :], y_d[n, :, :]).then_inc(yp_in, 16)

            def store(n):
                hold(sp, y_ok, n + 1, own)
                sp.dma_start(y_d[n, :, :], yout[:, n % 2, :]).then_inc(y_st, 16)

            load_tile(0)
            load_row(0, 0, None)
            sp.wait_ge(om_in, 16)
            sp.wait_ge(yp_in, 16)
            load_tile(1)
            with sp.Fori(1, RING) as u:
                load_row(0, u, 32 * u)
            for b in range(B):
                def step(j, tile, next_row):
                    n = j + b * HH
                    hold(sp, tile_done, n + 1, own)
                    if tile:
                        sp.wait_ge(om_in, 16 * (n + 2))
                        sp.wait_ge(yp_in, 16 * (n + 2))
                        load_tile(n + 2)
                    if next_row == "same":
                        load_row(b, j + RING, 32 * (j + RING + b * ROWS))
                    elif next_row == "next":
                        load_row(b + 1, j - (ROWS - RING), 32 * (j + RING + b * ROWS))
                    if type(n) is not int:
                        store(n - 1)

                first = 0
                if b == 0:
                    step(0, True, "same")
                    first = 1
                with sp.Fori(first, ROWS - RING) as j:
                    step(j, True, "same")
                if b + 1 < B:
                    with sp.Fori(ROWS - RING, HH) as j:
                        step(j, True, "next")
                    with sp.Fori(HH - (ROWS - RING), RING) as u:
                        load_row(b + 1, u, 32 * (u + (b + 1) * ROWS))
                else:
                    with sp.Fori(ROWS - RING, HH - 2) as j:
                        step(j, True, None)
                    with sp.Fori(HH - 2, HH) as j:
                        step(j, False, None)
            store(B * HH - 1)
            sp.wait_ge(y_st, 16 * B * HH + 1)

        def grid(w):
            return w.rearrange("p (y x g) -> p y x g", y=CW, x=CW)

        @block.scalar
        def _(act):
            act.wait_ge(setup, 1)

            def hats(n):
                hold(act, om_in, n * 16 + 16, own)
                hold(act, w_done, n + 1, own)
                for xy in range(2):
                    for r in range(R):
                        last = nc.scalar.activation(ab[:, n % 2, xy, r, :], om[:, n % 2, xy * GK:(xy + 1) * GK],
                                                    ACT.Abs, bias=negr[:, xy, r:r + 1], scale=1.0)
                last.then_inc(abs_ok, 1)
                hold(act, applied, n + 1, own)
                for w, y in ((wp, CW - R), (wd, 0)):
                    right = grid(w[:, n % 2, :])[:, y:y + R, R:CW, :]
                    nc.scalar.activation(right.rearrange("p y x g -> p y (x g)"), spread(zeros[:, 0:(CW - R) * G], 1, R),
                                         ACT.Copy)
                nc.scalar.activation(wp[:, n % 2, LOW * CW * G:(CW - R) * CW * G],
                                     zeros[:, 0:(CW - R - LOW) * CW * G], ACT.Copy)
                nc.scalar.activation(wd[:, n % 2, R * CW * G:CW * CW * G], zeros[:, :], ACT.Copy).then_inc(blank, 1)
                hold(act, abs_ok, n + 1, own)
                nc.scalar.activation(hat[:, n % 2, :, :, :], ab[:, n % 2, :, :, :], ACT.Relu, bias=1.0, scale=-1.0)\
                    .then_inc(hats_ok, 1)

            def mask_row(b, u):
                row_n = u + b * ROWS
                hold(act, row_in, 32 * (row_n + 1), own)
                r3 = ring[:, row_n % RING, :].rearrange("p (s c) -> p s c", c=C)
                for s in range(CW):
                    last = nc.scalar.activation(r3[:, s, :], r3[:, s, :], ACT.Copy, scale=mask[:, u, s:s + 1])
                last.then_inc(masked, 1)

            def finish(n):
                hold(act, prod_used, n * CW + (CW + NPROD), own)
                hold(act, y_st, n * 16 + 1, own)
                nc.scalar.activation(yout[:, n % 2, :], acc[:, n % 2, 0:C], ACT.Copy).then_inc(y_ok, 1)
                hold(act, y_ok, n + 1, own)
                act.sem_inc(acc_free, 1)

            hats(0)
            for b in range(B):
                with act.Fori(0, CW) as u:
                    mask_row(b, u)
                if b:
                    finish(b * HH - 1)
                with act.Fori(0, HH - 1) as j:
                    hats(j + (b * HH + 1))
                    mask_row(b, j + CW)
                    finish(j + b * HH)
                if b + 1 < B:
                    hats(b * HH + HH)
            finish(B * HH - 1)

        def outer(dst, hx, hy, tap):
            return (dst, spread(hx[:, :, tap * G:(tap + 1) * G], 1, R), spread(hy[:, :, tap * G:(tap + 1) * G], 2, R))

        def region(w, tap):
            ky, kx = tap // 3, tap % 3
            return grid(w)[:, ky:ky + R, kx:kx + R, :]

        def box(a):
            return a.rearrange("p (y x g) -> p y x g", y=R, x=R)

        @block.gpsimd
        def _(pool):
            pool.wait_ge(setup, 1)

            PER = 2 * len(POOL_TAPS) - 2
            with pool.Fori(0, B * HH) as n:
                hold(pool, w_done, n + 1, own)
                hold(pool, hats_ok, n + 1, own)
                hx, hy = hat[:, n % 2, 0, :, :], hat[:, n % 2, 1, :, :]
                hm = hym[:, n % 2, :, :]
                pool.tensor_tensor(hm, hy, spread(om[:, n % 2, 2 * GK:OM], 1, R), ALU.mult).then_inc(hym_ok, 1)
                w = wp[:, n % 2, :]
                hold(pool, hym_ok, n + 1, own)
                hold(pool, blank, n + 1, own)
                o, a, c = outer(region(w, POOL_TAPS[0]), hx, hm, POOL_TAPS[0])
                pool.tensor_tensor(o, a, c, ALU.mult).then_inc(pstep, 1)
                done = 1

                def mul(i):
                    o, a, c = outer(box(ap[:, i % 3, :]), hx, hm, POOL_TAPS[i])
                    pool.tensor_tensor(o, a, c, ALU.mult).then_inc(pstep, 1)

                mul(1)
                done += 1
                for i in range(1, len(POOL_TAPS)):
                    ready = done
                    if i + 1 < len(POOL_TAPS):
                        mul(i + 1)
                        done += 1
                    hold(pool, pstep, n * PER + ready, own)
                    r = region(w, POOL_TAPS[i])
                    last = pool.tensor_tensor(r, r, box(ap[:, i % 3, :]), ALU.add)
                    if i + 1 < len(POOL_TAPS):
                        last.then_inc(pstep, 1)
                        done += 1
                last.then_inc(wp_ok, 1)
                assert done == PER, (done, PER)

        @block.tensor
        def _(pe):
            with pe.Fori(0, B * HH) as n:
                pe.wait_ge(acc_free, n + 1)
                out = acc[:, n % 2, 0:C]
                for s in range(CW):
                    pe.wait_ge(prod_ok, n * CW + (s + 1))
                    for i in range(CW):
                        mm = pe.matmul(out, ident[0:TP, 0:TP], prod[:, s % NPROD, i * C:(i + 1) * C],
                                       start=(s == 0 and i == 0), stop=(s == CW - 1 and i == CW - 1))
                    mm.then_inc(prod_used, 1)
                    if s == 0:
                        hold(pe, yp_in, 16 * n + 16, own)
                        pe.matmul(out, ident[0:TP, 0:TP], yprev[:, n % 2, :], start=False, stop=False)

        @block.vector
        def _(dve):
            cnt = [0]

            def do(ins_):
                cnt[0] += 1
                ins_.then_inc(vt["sem"], 1)
                dve.wait_ge(vt["sem"], cnt[0])

            for xy in range(2):
                do(nc.vector.tensor_scalar(negr[:, xy, :], k["steps"][:, :], cur[:, xy:xy + 1], -1.0, ALU.add,
                                           ALU.mult))
            for pos, c0, lim, v in ((k["xpos"], 0, W, vt["x"]), (k["ypos"], 1, H, vt["y"])):
                do(nc.vector.tensor_scalar(v[:, 0, :], pos[:, :], cur[:, c0:c0 + 1], None, ALU.add))
                do(nc.vector.tensor_scalar(v[:, 1, :], v[:, 0, :], -0.5, None, ALU.is_gt))
                do(nc.vector.tensor_scalar(v[:, 0, :], v[:, 0, :], lim - 0.5, None, ALU.is_lt))
                do(nc.vector.tensor_tensor(v[:, 0, :], v[:, 0, :], v[:, 1, :], ALU.mult))
            do(nc.vector.memset(zeros[:, :], 0.0))
            dve.sem_inc(applied, 2)
            dve.sem_inc(w_done, 2)
            dve.sem_inc(prod_used, NPROD)
            dve.sem_inc(acc_free, 2)
            dve.sem_inc(y_st, 1)
            nc.vector.tensor_tensor(mask[:, :, :], spread(vt["y"][:, 0, :], 2, CW), spread(vt["x"][:, 0, :], 1, ROWS),
                                    ALU.mult).then_inc(setup, 2)

            PER = 2 * len(DVE_TAPS) - 1

            def weights(n):
                d = n * PER
                hold(dve, hym_ok, n + 1, own)
                hold(dve, blank, n + 1, own)
                hx, hm = hat[:, n % 2, 0, :, :], hym[:, n % 2, :, :]
                w = wd[:, n % 2, :]
                o, a, c = outer(region(w, DVE_TAPS[0]), hx, hm, DVE_TAPS[0])
                nc.vector.tensor_tensor(o, a, c, ALU.mult).then_inc(dstep, 1)

                def mul(i):
                    o, a, c = outer(box(ad[:, i % 3, :]), hx, hm, DVE_TAPS[i])
                    nc.vector.tensor_tensor(o, a, c, ALU.mult).then_inc(dstep, 1)

                mul(1)
                done = 2
                for i in range(1, len(DVE_TAPS)):
                    ready = done
                    if i + 1 < len(DVE_TAPS):
                        mul(i + 1)
                        done += 1
                    dve.wait_ge(dstep, d + ready)
                    r = region(w, DVE_TAPS[i])
                    nc.vector.tensor_tensor(r, r, box(ad[:, i % 3, :]), ALU.add).then_inc(dstep, 1)
                    done += 1
                hold(dve, dstep, d + done, own)
                hold(dve, wp_ok, n + 1, own)
                low = w[:, LOW * CW * G:]
                nc.vector.tensor_tensor(low, low, wp[:, n % 2, LOW * CW * G:], ALU.add).then_inc(w_done, 1)
                assert done == PER, (done, PER)

            def apply(n, j, b):
                hold(dve, masked, j + (CW + b * ROWS), own)
                hold(dve, w_done, n + 3, own)
                for s in range(CW):
                    dve.wait_ge(prod_used, n * CW + (s + 1))
                    slot = (j + (s + b * ROWS)) % RING
                    nc.vector.tensor_tensor(
                        prod[:, s % NPROD, :].rearrange("p (a c) -> p a c", c=GC),
                        ring[:, slot, :].rearrange("p (a c) -> p a c", c=GC),
                        spread(wd[:, n % 2, s * CW * G:(s + 1) * CW * G], 2, GC), ALU.mult).then_inc(prod_ok, 1)

            def leave(n):
                dve.wait_ge(prod_ok, n * CW + CW)
                dve.sem_inc(tile_done, 1)
                dve.sem_inc(applied, 1)

            weights(0)
            for b in range(B):
                with dve.Fori(0, HH if b + 1 < B else HH - 1) as j:
                    n = j + b * HH
                    apply(n, j, b)
                    leave(n)
                    weights(n + 1)
            apply(B * HH - 1, HH - 1, B - 1)
            leave(B * HH - 1)


def deformable_stage(nc, k, xp_d, om_d, y_d, base, counts):
    with ExitStack() as es:
        t = Ctx(nc, es, "deform")
        names = ("setup om_loaded yprev_loaded row_loaded row_masked abs_ready hats_ready grids_blank "
                 "hym_ready pool_step pool_weights_ready weights_done dve_step prod_ready prod_used "
                 "acc_free y_ready y_stored tile_done applied win_step").split()
        sems = [t.sem(s) for s in names]
        NW = CW * CW * G
        cur = t.sb("cur", [TP, 2])
        vt = {"x": t.sb("vx", [TP, 2, CW]), "y": t.sb("vy", [TP, 2, ROWS]), "sem": sems[-1]}
        zeros = t.sb("zeros", [TP, (CW - R) * CW * G])
        bufs = (t.sb("om", [TP, 2, OM]), t.sb("ab", [TP, 2, 2, R, GK]), t.sb("hat", [TP, 2, 2, R, GK]),
                t.sb("hym", [TP, 2, R, GK]), t.sb("wd", [TP, 2, NW]), t.sb("wp", [TP, 2, NW]),
                t.sb("ad", [TP, 3, R * R * G]), t.sb("ap", [TP, 3, R * R * G]), t.sb("prod", [TP, NPROD, CW * C]),
                t.sb("ring", [TP, RING, CW * C]), t.sb("yprev", [TP, 2, C]), t.sb("yout", [TP, 2, C]),
                t.sb("mask", [TP, ROWS, CW]), t.sb("negr", [TP, 2, R]), zeros, cur, vt)
        acc = t.ps("acc", [TP, 2, 512])

        def move(body):
            with nc.Block() as block:
                @block.vector
                def _(dve):
                    body(dve)

        def restart(dve):
            nc.vector.tensor_copy(cur[:, :], base[:, :])
        def restart_x(dve):
            nc.vector.tensor_copy(cur[:, 0:1], base[:, 0:1])

        move(restart)
        why = "a count of windows and a whole offset, bounded by the clamp of the offsets"
        lim = int(OFFMAX)
        nx, ny = (nc.values_load(counts[0:1, i:i + 1], min_val=1, max_val=(2 * lim + 2) // R + 1,
                                 skip_runtime_bounds_check_because=why) for i in range(2))
        x0, y0 = (nc.values_load(counts[0:1, i:i + 1], min_val=-lim, max_val=lim,
                                 skip_runtime_bounds_check_because=why) for i in (2, 3))
        with nc.Fori(0, ny) as iy:
            with nc.Fori(0, nx) as ix:
                window_pass(nc, k, {"acc": acc}, bufs, sems[:-1], xp_d, om_d, y_d, 
                            (y0 + iy * R).with_bounds(min_val=-lim, max_val=lim + 1),
                            (x0 + ix * R).with_bounds(min_val=-lim, max_val=lim + 1))
                for s in sems + [k["own"]]:
                    nc.gpsimd.sem_clear(s)
                nc.all_engine_barrier()
                move(lambda dve: nc.vector.tensor_scalar(cur[:, 0:1], cur[:, 0:1], float(R), None, ALU.add))
            move(lambda dve: nc.vector.tensor_scalar(cur[:, 1:2], cur[:, 1:2], float(R), None, ALU.add))
            move(restart_x)


def rows_stage(nc, k, x, y_d, t_d, xc_d):
    own, ident = k["own"], k["ident"]
    with ExitStack() as es:
        t = Ctx(nc, es, "rows")
        y = t.sb("y", [TP, 2, QT, C])
        xr = t.sb("x", [TP, 2, QT, C])
        turned = t.sb("turned", [C, 2, QT * TP])
        x2t = t.sb("x2t", [C, 2, QT * TP])
        hid = t.sb("hid", [C, 2, QT * TP])
        z = t.sb("z", [TP, 2, QT, C])
        z2 = t.sb("z2", [TP, 2, QT, C])
        x2 = t.sb("x2", [TP, 2, QT, C])
        x2b = t.sb("x2b", [TP, 2, QT, C])
        tok = t.sb("tok", [TP, 2, QT, C])
        xc = t.sb("xc", [TP, 2, QT, C])
        st = t.sb("st", [TP, 2, QT, 6])
        mv = t.sb("mv", [TP, 2, 3, QT, 2])
        ve = t.sb("ve", [TP, 2, 3, QT])
        rs = t.sb("rs", [TP, 2, 3, QT])
        half = t.sb("half", [TP, QT])
        gg = [t.sb(f"gg{i}", [TP, C]) for i in range(2)]
        gb = [t.sb(f"gb{i}", [TP, C]) for i in range(2)]
        ps_t = [t.ps(f"ps_t{i}", [C, 512]) for i in range(2)]
        ps_o = [t.ps(f"ps_o{i}", [TP, 512]) for i in range(2)]
        ps_f = [t.ps(f"ps_f{i}", [C, 512]) for i in range(2)]
        ps_m = [t.ps(f"ps_m{i}", [TP, 512]) for i in range(2)]
        y_in, x_in, tok_st, xc_st = ([t.sem(f"{s}{p}") for p in range(2)] for s in (
            "y_loaded", "x_loaded", "tokens_stored", "xc_stored"))
        (yT, yT_ok, o_ps, dstep, agg, eps, rstd, x2_ok, x2T, x2T_ok, f_ps, hid_ok, m_ps, xb_ok, x2b_ok,
         tok_ok, xc_ok, cst, half_ok) = [t.sem(s) for s in (
             "yT_in_psum yT_ready o_in_psum dve_step mean_var_ready var_eps_ready rstd_ready "
             "x2_ready x2T_in_psum x2T_ready f_in_psum hid_ready m_in_psum x_plus_bias_ready x2_plus_bias_ready "
             "tokens_ready xc_ready constants_ready half_ready").split()]

        with nc.Block() as block:

            @block.sync
            def _(sp):
                with sp.Fori(0, NB // 2) as i:
                    for p in range(2):
                        n = i * 2 + p
                        hold(sp, tok_ok, n + 1, own)
                        sp.dma_start(y[:, p, :, :], y_d[bass.ds(n * QT, QT), :, :].rearrange("t p c -> p t c"))\
                            .then_inc(y_in[p], 16)
                        for h in range(2):
                            src = bass.AP(x.tensor, ((n // NQ) * NPIX + (n % NQ) * (QT * W) + h * HH * W) * C,
                                          [[C, W], [W * C, QT], [1, C]])
                            sp.dma_start(xr[h * W:(h + 1) * W, p, :, :], src).then_inc(x_in[p], 16)

            @block.gpsimd
            def _(pool):
                pool.memset(half[:, :], -0.5).then_inc(half_ok, 1)
                pool.wait_ge(half_ok, 1)
                pool.wait_ge(cst, 2)

                with pool.Fori(0, NB // 2) as i:
                    for s in range(3):
                        for p in range(2):
                            m = i * 6 + 2 * s + p
                            hold(pool, agg, m + 1, own)
                            pool.tensor_scalar(ve[:, p, s, :], mv[:, p, s, :, 1], EPS, None, ALU.add).then_inc(eps, 1)
                            hold(pool, eps, m + 1, own)
                            pool.tensor_tensor(rs[:, p, s, :], ve[:, p, s, :], half[:, :], ALU.pow).then_inc(rstd, 1)
                        for p in range(2):
                            if s == 0:
                                hold(pool, x_in[p], i * 32 + 32, own)
                                pool.tensor_tensor(xr[:, p, :, :], xr[:, p, :, :], spread(gb[0][:, :], 1, QT),
                                                   ALU.add).then_inc(xb_ok, 1)
                            if s == 1:
                                hold(pool, x2_ok, i * 2 + p + 1, own)
                                pool.tensor_tensor(x2b[:, p, :, :], x2[:, p, :, :], spread(gb[1][:, :], 1, QT),
                                                   ALU.add).then_inc(x2b_ok, 1)

            @block.tensor
            def _(pe):
                with pe.Fori(0, NB // 2) as i:
                    for p in range(2):
                        hold(pe, y_in[p], i * 16 + 16, own)
                        hold(pe, x2T_ok, i * 2 + p + 1, own)
                        for q in range(QT):
                            mm = pe.transpose(ps_t[p][:, q * TP:(q + 1) * TP], y[:, p, q, :], ident[0:TP, 0:TP])
                        mm.then_inc(yT, 1)
                    for p in range(2):
                        hold(pe, yT_ok, i * 2 + p + 1, own)
                        for q in range(QT):
                            mm = pe.matmul(ps_o[p][:, q * C:(q + 1) * C], turned[:, p, q * TP:(q + 1) * TP],
                                           k["w_out"][:, :], start=True, stop=True)
                        mm.then_inc(o_ps, 1)
                    for p in range(2):
                        hold(pe, x2_ok, i * 2 + p + 1, own)
                        for q in range(QT):
                            mm = pe.transpose(ps_t[p][:, q * TP:(q + 1) * TP], x2[:, p, q, :], ident[0:TP, 0:TP])
                        mm.then_inc(x2T, 1)
                    for p in range(2):
                        hold(pe, x2T_ok, i * 2 + p + 3, own)
                        pe.matmul(ps_f[p][:, 0:QT * TP], k["w_fc1"][:, :], x2t[:, p, :], start=True, stop=True)\
                            .then_inc(f_ps, 1)
                    for p in range(2):
                        hold(pe, hid_ok, i * 2 + p + 1, own)
                        for q in range(QT):
                            mm = pe.matmul(ps_m[p][:, q * C:(q + 1) * C], hid[:, p, q * TP:(q + 1) * TP],
                                           k["w_fc2"][:, :], start=True, stop=True)
                        mm.then_inc(m_ps, 1)

            @block.scalar
            def _(act):
                act.sem_inc(x2T_ok, 2)
                with act.Fori(0, NB // 2) as i:
                    for p in range(2):
                        hold(act, yT, i * 2 + p + 1, own)
                        nc.scalar.activation(turned[:, p, :], ps_t[p][:, 0:QT * TP], ACT.Copy).then_inc(yT_ok, 1)
                    for p in range(2):
                        hold(act, x2T, i * 2 + p + 1, own)
                        nc.scalar.activation(x2t[:, p, :], ps_t[p][:, 0:QT * TP], ACT.Copy).then_inc(x2T_ok, 1)
                    for p in range(2):
                        hold(act, f_ps, i * 2 + p + 1, own)
                        nc.scalar.activation(hid[:, p, :], ps_f[p][:, 0:QT * TP], ACT.Gelu,
                                             bias=k["b_fc1"][:, 0:1], scale=1.0).then_inc(hid_ok, 1)
                    for p in range(2):
                        n = i * 2 + p
                        hold(act, tok_ok, n + 3, own)
                        act.dma_start(t_d[bass.ds(n * QT, QT), :, :].rearrange("t p c -> p t c"), tok[:, p, :, :])\
                            .then_inc(tok_st[p], 16)
                        hold(act, xc_ok, n + 1, own)
                        act.dma_start(xc_d[bass.ds(n * QT, QT), :, :].rearrange("t p c -> p t c"), xc[:, p, :, :])\
                            .then_inc(xc_st[p], 16)
                for p in range(2):
                    act.wait_ge(tok_st[p], 8 * NB + 1)
                    act.wait_ge(xc_st[p], 8 * NB + 1)

            @block.vector
            def _(dve):
                dve.sem_inc(tok_ok, 2)
                for s in (*tok_st, *xc_st):
                    dve.sem_inc(s, 1)
                for s, (gm, g, b_) in enumerate((("gamma1", "ln1_g", "ln1_b"), ("gamma2", "ln2_g", "ln2_b"))):
                    nc.vector.tensor_tensor(gg[s][:, :], k[gm][0:TP, :], k[g][0:TP, :], ALU.mult)
                    nc.vector.tensor_tensor(gb[s][:, :], k[gm][0:TP, :], k[b_][0:TP, :], ALU.mult).then_inc(cst, 1)
                dve.wait_ge(cst, 2)
                PER = 2 * (2 * 4 + 1)

                with dve.Fori(0, NB // 2) as i:
                    cnt = [0]

                    def do(ins_):
                        ins_.then_inc(dstep, 1)
                        cnt[0] += 1
                        return cnt[0]

                    def wait(c):
                        hold(dve, dstep, i * PER + c, own)

                    def stats(s, p, src):
                        for q in range(QT):
                            last = nc.vector.bn_stats(st[:, p, q, :], src[:, p, q, :])
                        wait(do(last))
                        for q in range(QT):
                            last = nc.vector.bn_aggr(mv[:, p, s, q, :], st[:, p, q, :])
                        last.then_inc(agg, 1)

                    def normalise(s, p, dst, src):
                        hold(dve, rstd, i * 6 + 2 * s + p + 1, own)
                        for q in range(QT):
                            last = nc.vector.tensor_scalar(dst[:, p, q, :], src[:, p, q, :], mv[:, p, s, q, 0:1],
                                                           rs[:, p, s, q:q + 1], ALU.subtract, ALU.mult)
                        return last

                    for s, (ps, bias, ready) in enumerate(((ps_o, "b_out", o_ps), (ps_m, "b_fc2", m_ps))):
                        seen = []
                        for p in range(2):
                            hold(dve, ready, i * 2 + p + 1, own)
                            seen.append(do(nc.vector.tensor_tensor(
                                z[:, p, :, :], ps[p][:, :].rearrange("p (t c) -> p t c", c=C),
                                spread(k[bias][0:TP, :], 1, QT), ALU.add)))
                        for p in range(2):
                            wait(seen[p])
                            stats(s, p, z)
                        seen = [do(normalise(s, p, z2, z)) for p in range(2)]
                        for p in range(2):
                            wait(seen[p])
                            seen[p] = do(nc.vector.tensor_tensor(z2[:, p, :, :], z2[:, p, :, :],
                                                                 spread(gg[s][:, :], 1, QT), ALU.mult))
                        for p in range(2):
                            wait(seen[p])
                            if s == 0:
                                hold(dve, xb_ok, i * 2 + p + 1, own)
                                nc.vector.tensor_tensor(x2[:, p, :, :], z2[:, p, :, :], xr[:, p, :, :], ALU.add)\
                                    .then_inc(x2_ok, 1)
                            else:
                                hold(dve, x2b_ok, i * 2 + p + 1, own)
                                hold(dve, tok_st[p], i * 16 + 1, own)
                                nc.vector.tensor_tensor(tok[:, p, :, :], z2[:, p, :, :], x2b[:, p, :, :], ALU.add)\
                                    .then_inc(tok_ok, 1)
                    for p in range(2):
                        hold(dve, tok_ok, i * 2 + p + 3, own)
                        stats(2, p, tok)
                    for p in range(2):
                        hold(dve, xc_st[p], i * 16 + 1, own)
                        normalise(2, p, xc, tok).then_inc(xc_ok, 1)
                    assert cnt[0] == PER, cnt


C4 = C // 4
NCH = 4
CK = NPIX // NCH
MT = CK // TP
ST = 4
NS = HH // ST
XA = C + 1
MG = 3
NMG = -(-HH // MG)
BN_EPS = 1e-5


def attention_stage(nc, k, ins, xc_d, t_d, t4_d):
    own, ident = k["own"], k["ident"]
    with ExitStack() as es:
        t = Ctx(nc, es, "attn")
        wraw = t.sb("wraw", [128, C])
        wqk = t.sb("wqk", [C, 2 * C4])
        wt = t.sb("wt", [C, C])
        wtt = t.sb("wtt", [C, C])
        bn = t.sb("bn", [C, 5])
        bs = t.sb("bs", [C, 2])
        bneg = t.sb("bneg", [C, 1])
        xa = t.sb("xa", [TP, HH, XA])
        xct = t.sb("xct", [C, NPIX])
        q = t.sb("q", [C4, NPIX])
        kk = t.sb("kk", [C4, NPIX])
        qs = t.sb("qs", [C4, 2, ST * TP])
        prob = t.sb("prob", [TP, 2, ST, NPIX])
        xs = t.sb("xs", [TP, 2, ST, NCH, XA])
        xr = t.sb("xr", [TP, HH, XA])
        nm = t.sb("nm", [TP, 2, ST, NCH])
        zs = t.sb("zs", [TP, 2, ST, NCH])
        wz = t.sb("wz", [TP, 2, ST, NCH])
        ez = t.sb("ez", [TP, 2, ST, NCH])
        dm = t.sb("dm", [TP, 2, ST, NCH])
        mn = t.sb("mn", [TP, 2, ST])
        zt = t.sb("zt", [TP, 2, ST])
        zr = t.sb("zr", [TP, 2, ST])
        rc = t.sb("rc", [TP, HH])
        dt_ = t.sb("dt", [C, 2, QT * TP])
        un = t.sb("un", [C, 2, QT * TP])
        tin = t.sb("tin", [TP, 2, QT, C])
        tout = t.sb("tout", [TP, 2, QT, C])
        ps_e = [t.ps(f"ps_e{i}", [TP, 2, 512]) for i in range(2)]
        ps_r = [t.ps(f"ps_r{i}", [TP, 512]) for i in range(2)]
        ps_w = [t.ps(f"ps_w{i}", [C, 512]) for i in range(2)]
        (w_in, xa_in, wT, w_ok, pstep, bstep, bn_done, xT, xT_ok, qk, qk_ok, qs_ok, e_ps, mx_ok, ex_ok, sstep, dm_ok, ez_ok,
         w_rdy, xs_ok, r_ps, r_ok, zeroed, d_ok, dT, dT_ok, u_ps, u_ok, uT, tin_ok, t_ok, image_done, const_ok) = [
             t.sem(s) for s in (
                 "weights_loaded xa_loaded weights_turned weights_ready post_step bn_step bn_done xT_in_psum xT_ready "
                 "qk_in_psum qk_ready query_ready energy_in_psum max_ready exp_ready soft_step below_ready "
                 "rescale_ready chunk_weights_ready xs_ready sums_in_psum sums_added sums_zeroed d_ready dT_in_psum "
                 "dT_ready u_in_psum u_ready uT_in_psum residual_ready tokens_ready image_done constants_ready")
             .split()]
        t_in, t_st = ([t.sem(f"{s}{p}") for p in range(2)] for s in ("t_loaded", "t_stored"))

        def uses(p, b, g):
            return b * ((NQ + 1 - p) // 2) + g // 2

        def steps():
            order = [(j / 16.0, 0, j) for j in range(ST * NCH)] + \
                    [(0.28 + 0.72 * g / NMG, 1, g) for g in range(NMG)]
            return [(kind, j) for _, kind, j in sorted(order)]

        ENERGY, SUMS = 0, 1

        def superblocks(eng, b, part):
            part(0, 0, None, None)
            with eng.Fori(0, NS // 2) as i:
                part(i * 2 + 1, 1, i * 2, 0)
                part(i * 2 + 2, 0, i * 2 + 1, 1)
            part(None, None, NS - 1, 0)

        def overall(b, s):
            return None if s is None else s + b * NS

        def interleaved(s_e, s_r):
            return [(kind, j) for kind, j in steps()
                    if (kind == ENERGY and s_e is not None) or (kind == SUMS and s_r is not None)]

        with nc.Block() as block:

            @block.sync
            def _(sp):
                sp.dma_start(wraw[0:C4, :], ins["L1_attn_Wq"]).then_inc(w_in, 16)
                sp.dma_start(wraw[C4:2 * C4, :], ins["L1_attn_Wk"]).then_inc(w_in, 16)
                for i, name in enumerate(("gamma", "beta", "bn_mean", "bn_var", "bt")):
                    sp.dma_start(bn[:, i:i + 1], col(ins["L1_attn_" + name])).then_inc(w_in, 16)
                sp.dma_start(wt[:, :], ins["L1_attn_Wt"]).then_inc(w_in, 16)
                with sp.Fori(0, B) as b:
                    hold(sp, image_done, b + 1, own)
                    sp.dma_start(xa[:, :, 0:C], xc_d[bass.ds(b * HH, HH), :, :].rearrange("t p c -> p t c"))\
                        .then_inc(xa_in, 16)
                    for g in range(NQ):
                        n = b * NQ + g
                        hold(sp, t_ok, n + (2 if g == 0 else 1), own)
                        sp.dma_start(tin[:, g % 2, :, :], t_d[bass.ds(n * QT, QT), :, :].rearrange("t p c -> p t c"))\
                            .then_inc(t_in[g % 2], 16)

            @block.gpsimd
            def _(pool):
                pool.memset(bneg[:, :], -0.5).then_inc(const_ok, 1)
                pool.memset(xa[:, :, C:XA], 1.0).then_inc(const_ok, 1)
                pool.wait_ge(w_in, 128)
                pool.wait_ge(const_ok, 2)
                pool.tensor_scalar(bs[:, 0:1], bn[:, 3:4], BN_EPS, None, ALU.add).then_inc(bstep, 1)
                pool.wait_ge(bstep, 1)
                pool.tensor_tensor(bs[:, 0:1], bs[:, 0:1], bneg[:, :], ALU.pow).then_inc(bstep, 1)
                with pool.Fori(0, B) as b:
                    hold(pool, image_done, b + 1, own)
                    pool.memset(xr[:, :, :], 0.0).then_inc(zeroed, 1)
                    hold(pool, xa_in, b * 16 + 16, own)

                    def queries(s, slot):
                        hold(pool, qk_ok, b * NQ + NQ + 1, own)
                        pool.tensor_copy(qs[:, slot, :], q[:, bass.ds(s * (ST * TP), ST * TP)])\
                            .then_inc(qs_ok, 1)

                    def part(s_e, e, s_r, r):
                        if s_e is not None:
                            if s_r is not None:
                                hold(pool, e_ps, overall(b, s_r) * (ST * NCH) + 1, own)
                            queries(s_e, e)
                        if s_r is not None:
                            hold(pool, w_rdy, overall(b, s_r) + 1, own)
                            for i in range(ST):
                                tile = s_r * ST + i
                                last = pool.tensor_tensor(xs[:, r, i, :, :], spread(xa[:, tile, :], 1, NCH),
                                                          spread(wz[:, r, i, :], 2, XA), ALU.mult)
                            last.then_inc(xs_ok, 1)

                    superblocks(pool, b, part)
                    for g in range(NQ):
                        hold(pool, t_in[g % 2], uses(g % 2, b, g) * 16 + 16, own)
                        pool.tensor_tensor(tin[:, g % 2, :, :], tin[:, g % 2, :, :], xa[:, g * QT:(g + 1) * QT, 0:C],
                                           ALU.add).then_inc(tin_ok, 1)

            @block.tensor
            def _(pe):
                pe.wait_ge(w_in, 128)
                pe.transpose(ps_w[0][:, 0:2 * C4], wraw[0:2 * C4, :], ident[0:2 * C4, 0:2 * C4]).then_inc(wT, 1)
                pe.transpose(ps_w[1][:, 0:C], wt[:, :], ident[:, :]).then_inc(wT, 1)
                pe.wait_ge(w_ok, 1)
                with pe.Fori(0, B) as b:
                    hold(pe, xa_in, b * 16 + 16, own)
                    for g in range(NQ):
                        n = b * NQ + g
                        hold(pe, dT_ok, b * NQ + 1, own)
                        hold(pe, xT_ok, n + 1, own)
                        for i in range(QT):
                            mm = pe.transpose(ps_w[0][:, i * TP:(i + 1) * TP], xa[:, g * QT + i, 0:C],
                                              ident[0:TP, 0:TP])
                        mm.then_inc(xT, 1)
                        hold(pe, xT_ok, n + 2, own)
                        hold(pe, qk_ok, n + 1, own)
                        pe.matmul(ps_w[1][0:2 * C4, 0:QT * TP], wqk[:, :], xct[:, g * QT * TP:(g + 1) * QT * TP],
                                  start=True, stop=True).then_inc(qk, 1)
                    hold(pe, qk_ok, b * NQ + NQ + 1, own)

                    def part(s_e, e, s_r, r):
                        s_e, s_r = overall(b, s_e), overall(b, s_r)
                        if s_e is not None:
                            hold(pe, qs_ok, s_e + 1, own)
                        for kind, j in interleaved(s_e, s_r):
                            if kind == ENERGY:
                                i, ch = j // NCH, j % NCH
                                pe.wait_ge(ex_ok, s_e * (ST * NCH) + (j + 1))
                                for hf in range(2):
                                    m0 = ch * CK + hf * (CK // 2)
                                    mm = pe.matmul(ps_e[ch % 2][:, hf, 0:CK // 2], qs[:, e, i * TP:(i + 1) * TP],
                                                   kk[:, m0:m0 + CK // 2], start=True, stop=True)
                                mm.then_inc(e_ps, 1)
                            else:
                                if j == 0:
                                    hold(pe, xs_ok, s_r + 1, own)
                                hold(pe, r_ok, s_r * NMG + (j + 1), own)
                                tiles = range(j * MG, min((j + 1) * MG, HH))
                                for i in range(ST):
                                    for m in tiles:
                                        mm = pe.matmul(ps_r[j % 2][:, (m - j * MG) * XA:(m - j * MG + 1) * XA],
                                                       prob[:, r, i, m * TP:(m + 1) * TP], xs[:, r, i, m // MT, :],
                                                       start=(i == 0 and m == tiles[0]),
                                                       stop=(i == ST - 1), skip_group_check=True)
                                mm.then_inc(r_ps, 1)

                    superblocks(pe, b, part)

                    def project(g):
                        n = b * NQ + g
                        hold(pe, d_ok, n + 1, own)
                        hold(pe, dT_ok, n + 1, own)
                        for i in range(QT):
                            mm = pe.transpose(ps_w[0][:, i * TP:(i + 1) * TP], xr[:, g * QT + i, 0:C],
                                              ident[0:TP, 0:TP])
                        mm.then_inc(dT, 1)
                        hold(pe, dT_ok, n + 2, own)
                        hold(pe, u_ok, n + 1, own)
                        pe.matmul(ps_w[1][:, 0:QT * TP], wtt[:, :], dt_[:, g % 2, :], start=True, stop=True)\
                            .then_inc(u_ps, 1)

                    def turn(g):
                        n = b * NQ + g
                        hold(pe, u_ok, n + 2, own)
                        hold(pe, t_ok, n + (2 if g == 0 else 1), own)
                        for i in range(QT):
                            mm = pe.transpose(ps_r[g % 2][:, i * C:(i + 1) * C], un[:, g % 2, i * TP:(i + 1) * TP],
                                              ident[:, :])
                        mm.then_inc(uT, 1)

                    project(0)
                    for g in range(NQ):
                        if g + 1 < NQ:
                            project(g + 1)
                        turn(g)

            @block.scalar
            def _(act):
                act.sem_inc(xT_ok, 1)
                act.sem_inc(dT_ok, 1)
                act.sem_inc(u_ok, 1)
                act.sem_inc(ex_ok, 2)
                act.wait_ge(wT, 2)
                nc.scalar.activation(wqk[:, :], ps_w[0][:, 0:2 * C4], ACT.Copy)
                nc.scalar.activation(wtt[:, :], ps_w[1][:, 0:C], ACT.Copy).then_inc(w_ok, 1)
                act.wait_ge(bn_done, 1)
                with act.Fori(0, B) as b:
                    for g in range(NQ):
                        n = b * NQ + g
                        hold(act, xT, n + 1, own)
                        nc.scalar.activation(xct[:, g * QT * TP:(g + 1) * QT * TP], ps_w[0][:, 0:QT * TP], ACT.Copy)\
                            .then_inc(xT_ok, 1)

                    def rescale(S, slot):
                        hold(act, dm_ok, S + 1, own)
                        nc.scalar.activation(ez[:, slot, :, :], dm[:, slot, :, :], ACT.Exp).then_inc(ez_ok, 1)

                    def part(s_e, e, s_r, r):
                        s_e, s_r = overall(b, s_e), overall(b, s_r)
                        if s_r is not None:
                            rescale(s_r, r)
                        if s_e is None:
                            return
                        if s_r is not None:
                            hold(act, r_ps, s_r * NMG + 1, own)
                        for j in range(ST * NCH):
                            i, ch = j // NCH, j % NCH
                            act.wait_ge(mx_ok, s_e * (ST * NCH) + (j + 1))
                            nc.scalar.activation(prob[:, e, i, ch * CK:(ch + 1) * CK]
                                                 .rearrange("p (a f) -> p a f", a=2), ps_e[ch % 2][:, :, 0:CK // 2],
                                                 ACT.Exp, bias=nm[:, e, i, ch:ch + 1], scale=1.0,
                                                 accum_out=zs[:, e, i, ch:ch + 1]).then_inc(ex_ok, 1)

                    superblocks(act, b, part)

                    def store(g):
                        n = b * NQ + g
                        hold(act, t_ok, n + 3, own)
                        for h in range(2):
                            dst = bass.AP(t4_d.tensor, (b * NPIX + (g * QT * W + h * HH * W)) * C,
                                          [[C, W], [W * C, QT], [1, C]])
                            act.dma_start(dst, tout[h * W:(h + 1) * W, g % 2, :, :]).then_inc(t_st[g % 2], 16)

                    def copy_d(g):
                        n = b * NQ + g
                        hold(act, dT, n + 1, own)
                        nc.scalar.activation(dt_[:, g % 2, :], ps_w[0][:, 0:QT * TP], ACT.Copy).then_inc(dT_ok, 1)

                    copy_d(0)
                    for g in range(NQ):
                        n = b * NQ + g
                        hold(act, u_ps, n + 1, own)
                        nc.scalar.activation(un[:, g % 2, :], ps_w[1][:, 0:QT * TP], ACT.Relu, bias=bs[:, 1:2],
                                             scale=bs[:, 0:1]).then_inc(u_ok, 1)
                        if g + 1 < NQ:
                            copy_d(g + 1)
                        if g >= 1:
                            store(g - 1)
                    store(NQ - 1)
                for p in range(2):
                    act.wait_ge(t_st[p], 32 * B * ((NQ + 1 - p) // 2) + 1)

            @block.vector
            def _(dve):
                dve.sem_inc(image_done, 1)
                dve.sem_inc(qk_ok, 1)
                dve.sem_inc(r_ok, 2)
                dve.sem_inc(t_ok, 2)
                for s in (r_ps, *t_st):
                    dve.sem_inc(s, 1)
                dve.wait_ge(bstep, 2)
                nc.vector.tensor_tensor(bs[:, 0:1], bs[:, 0:1], bn[:, 0:1], ALU.mult).then_inc(bstep, 1)
                nc.vector.tensor_tensor(bs[:, 1:2], bn[:, 4:5], bn[:, 2:3], ALU.subtract).then_inc(bstep, 1)
                dve.wait_ge(bstep, 4)
                nc.vector.tensor_tensor(bs[:, 1:2], bs[:, 1:2], bs[:, 0:1], ALU.mult).then_inc(bstep, 1)
                dve.wait_ge(bstep, 5)
                nc.vector.tensor_tensor(bs[:, 1:2], bs[:, 1:2], bn[:, 1:2], ALU.add).then_inc(bn_done, 1)
                SOFT = 4
                POST = 3
                with dve.Fori(0, B) as b:
                    for g in range(NQ):
                        hold(dve, qk, b * NQ + g + 1, own)
                        for dst, lo in ((q, 0), (kk, C4)):
                            last = nc.vector.tensor_copy(dst[:, g * QT * TP:(g + 1) * QT * TP],
                                                         ps_w[1][lo:lo + C4, 0:QT * TP])
                        last.then_inc(qk_ok, 1)
                    hold(dve, zeroed, b + 1, own)

                    def below(S, slot):
                        hold(dve, mx_ok, (S + 1) * (ST * NCH), own)
                        d = S * SOFT
                        nc.vector.tensor_reduce(mn[:, slot, :], nm[:, slot, :, :], AX, ALU.min).then_inc(sstep, 1)
                        dve.wait_ge(sstep, d + 1)
                        nc.vector.tensor_tensor(dm[:, slot, :, :], spread(mn[:, slot, :], 2, NCH), nm[:, slot, :, :],
                                                ALU.subtract).then_inc(dm_ok, 1)

                    def chunk_weights(S, slot):
                        d = S * SOFT
                        hold(dve, ez_ok, S + 1, own)
                        nc.vector.tensor_tensor(zs[:, slot, :, :], zs[:, slot, :, :], ez[:, slot, :, :], ALU.mult)\
                            .then_inc(sstep, 1)
                        dve.wait_ge(sstep, d + 2)
                        nc.vector.tensor_reduce(zt[:, slot, :], zs[:, slot, :, :], AX, ALU.add).then_inc(sstep, 1)
                        dve.wait_ge(sstep, d + 3)
                        nc.vector.reciprocal(zr[:, slot, :], zt[:, slot, :]).then_inc(sstep, 1)
                        dve.wait_ge(sstep, d + 4)
                        nc.vector.tensor_tensor(wz[:, slot, :, :], ez[:, slot, :, :], spread(zr[:, slot, :], 2, NCH),
                                                ALU.mult).then_inc(w_rdy, 1)

                    def part(s_e, e, s_r, r):
                        s_e, s_r = overall(b, s_e), overall(b, s_r)
                        if s_r is not None:
                            below(s_r, r)
                        for at, (kind, j) in enumerate(interleaved(s_e, s_r)):
                            if at == (2 if s_e is not None else 0) and s_r is not None:
                                chunk_weights(s_r, r)
                            if kind == ENERGY:
                                i, ch = j // NCH, j % NCH
                                dve.wait_ge(e_ps, s_e * (ST * NCH) + (j + 1))
                                nc.vector.tensor_reduce(nm[:, e, i, ch:ch + 1], ps_e[ch % 2][:, :, 0:CK // 2],
                                                        mybir.AxisListType.XY, ALU.max, negate=True).then_inc(mx_ok, 1)
                            else:
                                hold(dve, r_ps, s_r * NMG + (j + 1) + 1, own)
                                tiles = min(MG, HH - j * MG)
                                part_ = xr[:, j * MG:j * MG + tiles, :]
                                nc.vector.tensor_tensor(part_, part_, ps_r[j % 2][:, 0:tiles * XA]
                                                        .rearrange("p (m c) -> p m c", c=XA), ALU.add)\
                                    .then_inc(r_ok, 1)

                    superblocks(dve, b, part)
                    hold(dve, r_ok, (b + 1) * (NS * NMG) + 2, own)
                    d = b * POST
                    nc.vector.tensor_scalar(rc[:, :], xr[:, :, C], 1e-6, None, ALU.add).then_inc(pstep, 1)
                    dve.wait_ge(pstep, d + 1)
                    nc.vector.reciprocal(rc[:, :], rc[:, :]).then_inc(pstep, 1)
                    dve.wait_ge(pstep, d + 2)
                    nc.vector.tensor_tensor(xr[:, :, 0:C], xr[:, :, 0:C], spread(rc[:, :], 2, C), ALU.mult)\
                        .then_inc(pstep, 1)
                    dve.wait_ge(pstep, d + 3)
                    for g in range(NQ):
                        part_ = xr[:, g * QT:(g + 1) * QT, 0:C]
                        nc.vector.tensor_tensor(part_, xa[:, g * QT:(g + 1) * QT, 0:C], part_, ALU.subtract)\
                            .then_inc(d_ok, 1)
                    for g in range(NQ):
                        n = b * NQ + g
                        hold(dve, tin_ok, n + 1, own)
                        hold(dve, t_st[g % 2], uses(g % 2, b, g) * 32 + 1, own)
                        hold(dve, uT, n + 1, own)
                        nc.vector.tensor_tensor(tout[:, g % 2, :, :], tin[:, g % 2, :, :],
                                                ps_r[g % 2][:, :].rearrange("p (t c) -> p t c", c=C), ALU.add)\
                            .then_inc(t_ok, 1)
                    hold(dve, t_ok, (b + 1) * NQ + 2, own)
                    dve.sem_inc(image_done, 1)


E8, F = 8, 512
FB = F // 128
CAP = -(-5 * T // (4 * E8))
EBATCH = 512
SLOTS = -(-CAP // EBATCH) * EBATCH
NEB = SLOTS // EBATCH
DROPPED = 1 << 20
NF = T // 128
FG = 7
NFG = NF // FG
BIGGEST = 3.4028234663852886e38


def route_stage(nc, k, ins, t4_d, buf_d, tok, slots, weight):
    own, ident = k["own"], k["ident"]
    with ExitStack() as es:
        t = Ctx(nc, es, "route")
        hall = t.sb("hall", [128, NF, C])
        hn = t.sb("hn", [128, 2, FG, C])
        ht = t.sb("ht", [C, 2, FG * 128])
        gw = t.sb("gw", [C, E8])
        gb = t.sb("gb", [128, E8])
        lg = t.sb("lg", [128, NF, E8])
        ex = t.sb("ex", [128, NF, E8])
        hot = t.sb("hot", [128, NF, E8])
        cum = t.sb("cum", [128, NF, E8])
        iot_i = t.sb("iota_i", [128, E8], I32)
        iot = t.sb("iota", [128, E8])
        less8 = t.sb("iota_less_8", [128, E8])
        one = t.sb("one", [128, NF])
        tri = t.sb("tri", [128, 128])
        tot = t.sb("tot", [128, E8])
        mx, sm, idx, pos, kept, tmp = (t.sb(n, [128, NF]) for n in ("mx", "sm", "idx", "pos", "kept", "tmp"))
        st = t.sb("st", [128, 2, FG, 6])
        mv = t.sb("mv", [128, 2, FG, 2])
        ve = t.sb("ve", [128, 2, FG])
        rs = t.sb("rs", [128, 2, FG])
        half = t.sb("half", [128, FG])
        ps_t = [t.ps(f"ps_t{i}", [C, 2, 512]) for i in range(2)]
        ps_l = [t.ps(f"ps_l{i}", [128, 512]) for i in range(2)]
        (t_in, g_in, stat, agg, eps, rstd, hn_ok, hT, ht_ok, copied, l_ps, lg_ok, cst, step, sm_ok, tri_ps, slot_ok,
         sent, ct) = [t.sem(s) for s in (
             "tokens_loaded gate_loaded stats_ready mean_var_ready var_eps_ready rstd_ready hn_ready hT_in_psum "
             "ht_ready hn_kept logits_in_psum logits_ready constants_ready step exp_ready prefix_in_psum slots_ready "
             "rows_sent totals_ready").split()]

        with nc.Block() as block:

            @block.sync
            def _(sp):
                sp.dma_start(gw[:, :], ins["L1_ffn_gate_w"]).then_inc(g_in, 16)
                sp.dma_start(gb[:, :], row(ins["L1_ffn_gate_b"]).to_broadcast([128, E8])).then_inc(g_in, 16)
                tv = t4_d.rearrange("(p f) c -> p f c", p=128)
                for g in range(NFG):
                    if g:
                        sp.wait_ge(t_in, 16 * g)
                    sp.dma_start(tok[:, g * FG:(g + 1) * FG, :], tv[:, g * FG:(g + 1) * FG, :]).then_inc(t_in, 16)

            @block.gpsimd
            def _(pool):
                pool.memset(half[:, :], -0.5).then_inc(cst, 1)
                pool.iota(iot_i[:, :], [[1, E8]], base=0, channel_multiplier=0).then_inc(cst, 1)
                pool.memset(tri[:, :], 1.0).then_inc(cst, 1)
                pool.wait_ge(cst, 3)
                pool.affine_select(out=tri[:, :], in_=tri[:, :], compare_op=ALU.is_gt, fill=0.0, base=0,
                                   pattern=[[1, 128]], channel_multiplier=-1).then_inc(cst, 1)
                with pool.Fori(0, NFG // 2) as i:
                    for p in range(2):
                        n = i * 2 + p
                        hold(pool, agg, n + 1, own)
                        pool.tensor_scalar(ve[:, p, :], mv[:, p, :, 1], EPS, None, ALU.add).then_inc(eps, 1)
                        hold(pool, eps, n + 1, own)
                        pool.tensor_tensor(rs[:, p, :], ve[:, p, :], half[:, :], ALU.pow).then_inc(rstd, 1)
                pool.wait_ge(slot_ok, 1)
                pool.wait_ge(copied, NFG + 1)
                for f in range(NF):
                    pool.indirect_dma_start(
                        out=buf_d, out_offset=bass.IndirectOffsetOnAxis(ap=slots[:, 0, f:f + 1], axis=0),
                        in_=hall[:, f, :], in_offset=None, bounds_check=E8 * SLOTS - 1, oob_is_err=False)\
                        .then_inc(sent, 16)
                pool.wait_ge(sent, 16 * NF)

            @block.tensor
            def _(pe):
                pe.wait_ge(g_in, 32)

                def turn(n, p):
                    hold(pe, hn_ok, n + 1, own)
                    hold(pe, ht_ok, n + 1, own)
                    for i in range(FG):
                        mm = pe.transpose(ps_t[p][:, i // 4, (i % 4) * 128:(i % 4 + 1) * 128], hn[:, p, i, :],
                                          ident[:, :])
                    mm.then_inc(hT, 1)

                def gate(n, p):
                    hold(pe, ht_ok, n + 3, own)
                    hold(pe, lg_ok, n + 1, own)
                    for i in range(FG):
                        mm = pe.matmul(ps_l[p][:, i * E8:(i + 1) * E8], ht[:, p, i * 128:(i + 1) * 128], gw[:, :],
                                       start=True, stop=True)
                    mm.then_inc(l_ps, 1)

                with pe.Fori(0, NFG // 2) as i:
                    for p in range(2):
                        turn(i * 2 + p, p)
                    for p in range(2):
                        gate(i * 2 + p, p)
                pe.wait_ge(ct, 1)
                pe.matmul(ps_l[0][:, 0:E8], tri[:, :], tot[:, :], start=True, stop=True).then_inc(tri_ps, 1)

            @block.scalar
            def _(act):
                act.sem_inc(ht_ok, 2)
                with act.Fori(0, NFG // 2) as i:
                    for p in range(2):
                        n = i * 2 + p
                        hold(act, hT, n + 1, own)
                        for hb, w in ((0, 4), (1, FG - 4)):
                            last = nc.scalar.activation(ht[:, p, hb * 512:hb * 512 + w * 128],
                                                        ps_t[p][:, hb, 0:w * 128], ACT.Copy)
                        last.then_inc(ht_ok, 1)
                        nc.scalar.activation(hall[:, bass.ds(n * FG, FG), :], hn[:, p, :, :], ACT.Copy)\
                            .then_inc(copied, 1)
                act.wait_ge(sm_ok, 1)
                nc.scalar.activation(ex[:, :, :], ex[:, :, :], ACT.Exp).then_inc(sm_ok, 1)

            @block.vector
            def _(dve):
                dve.sem_inc(lg_ok, 2)
                dve.sem_inc(copied, 1)
                dve.wait_ge(g_in, 32)
                with dve.Fori(0, NFG // 2) as i:
                    for p in range(2):
                        n = i * 2 + p
                        hold(dve, t_in, n * 16 + 16, own)
                        for j in range(FG):
                            last = nc.vector.bn_stats(st[:, p, j, :], tok[:, n * FG + j, :])
                        last.then_inc(stat, 1)
                    for p in range(2):
                        hold(dve, stat, i * 2 + p + 1, own)
                        for j in range(FG):
                            last = nc.vector.bn_aggr(mv[:, p, j, :], st[:, p, j, :])
                        last.then_inc(agg, 1)
                    for p in range(2):
                        n = i * 2 + p
                        hold(dve, rstd, n + 1, own)
                        hold(dve, copied, i * 2 + 1, own)
                        for j in range(FG):
                            last = nc.vector.tensor_scalar(hn[:, p, j, :], tok[:, n * FG + j, :], mv[:, p, j, 0:1],
                                                           rs[:, p, j:j + 1], ALU.subtract, ALU.mult)
                        last.then_inc(hn_ok, 1)
                    for p in range(2):
                        n = i * 2 + p
                        hold(dve, l_ps, n + 1, own)
                        nc.vector.tensor_tensor(lg[:, bass.ds(n * FG, FG), :],
                                                ps_l[p][:, 0:FG * E8].rearrange("p (f e) -> p f e", e=E8),
                                                spread(gb[:, :], 1, FG), ALU.add).then_inc(lg_ok, 1)
                n = [0]

                def do(ins_):
                    n[0] += 1
                    ins_.then_inc(step, 1)
                    dve.wait_ge(step, n[0])

                dve.wait_ge(lg_ok, NFG + 2)
                dve.wait_ge(cst, 4)
                do(nc.vector.memset(one[:, :], 1.0))
                do(nc.vector.tensor_copy(iot[:, :], iot_i[:, :]))
                do(nc.vector.tensor_scalar(less8[:, :], iot[:, :], -float(E8), None, ALU.add))
                do(nc.vector.tensor_reduce(mx[:, :], lg[:, :, :], AX, ALU.max))
                nc.vector.tensor_tensor(ex[:, :, :], lg[:, :, :], spread(mx[:, :], 2, E8), ALU.subtract)\
                    .then_inc(sm_ok, 1)
                do(nc.vector.tensor_tensor(hot[:, :, :], lg[:, :, :], spread(mx[:, :], 2, E8), ALU.is_equal))
                do(nc.vector.tensor_tensor(hot[:, :, :], hot[:, :, :], spread(less8[:, :], 1, NF), ALU.mult))
                do(nc.vector.tensor_reduce(idx[:, :], hot[:, :, :], AX, ALU.min))
                do(nc.vector.tensor_scalar(idx[:, :], idx[:, :], float(E8), None, ALU.add))
                do(nc.vector.tensor_tensor(hot[:, :, :], spread(iot[:, :], 1, NF), spread(idx[:, :], 2, E8),
                                           ALU.is_equal))
                for e in range(E8):
                    do(nc.vector.tensor_tensor_scan(cum[:, :, e], one[:, :], hot[:, :, e], 0.0, ALU.mult, ALU.add))
                nc.vector.tensor_copy(tot[:, :], cum[:, NF - 1, :]).then_inc(ct, 1)
                dve.wait_ge(tri_ps, 1)
                do(nc.vector.tensor_tensor(cum[:, :, :], cum[:, :, :], spread(ps_l[0][:, 0:E8], 1, NF), ALU.add))
                do(nc.vector.tensor_tensor(cum[:, :, :], cum[:, :, :], hot[:, :, :], ALU.mult))
                do(nc.vector.tensor_reduce(pos[:, :], cum[:, :, :], AX, ALU.add))
                do(nc.vector.tensor_scalar(pos[:, :], pos[:, :], -1.0, None, ALU.add))
                do(nc.vector.tensor_scalar(kept[:, :], pos[:, :], float(CAP), None, ALU.is_lt))
                do(nc.vector.tensor_scalar(pos[:, :], pos[:, :], float(CAP - 1), None, ALU.min))
                do(nc.vector.tensor_scalar(tmp[:, :], idx[:, :], float(SLOTS), None, ALU.mult))
                do(nc.vector.tensor_tensor(pos[:, :], pos[:, :], tmp[:, :], ALU.add))
                do(nc.vector.tensor_copy(slots[:, 1, :], pos[:, :]))
                do(nc.vector.tensor_scalar(tmp[:, :], kept[:, :], -float(DROPPED), float(DROPPED), ALU.mult, ALU.add))
                do(nc.vector.tensor_tensor(pos[:, :], pos[:, :], tmp[:, :], ALU.add))
                do(nc.vector.tensor_copy(slots[:, 0, :], pos[:, :]))
                dve.sem_inc(slot_ok, 1)
                dve.wait_ge(sm_ok, 2)
                do(nc.vector.tensor_reduce(sm[:, :], ex[:, :, :], AX, ALU.add))
                do(nc.vector.reciprocal(sm[:, :], sm[:, :]))
                do(nc.vector.tensor_tensor(weight[:, :], sm[:, :], kept[:, :], ALU.mult))


def experts_stage(nc, k, ins, buf_d, res_d):
    own, ident = k["own"], k["ident"]
    NI = EBATCH // 128
    with ExitStack() as es:
        t = Ctx(nc, es, "experts")
        w1 = t.sb("w1", [C, 2, F])
        w2 = t.sb("w2", [128, 2, FB, C])
        b1r = t.sb("b1r", [E8 * FB, 128])
        b1t = t.sb("b1t", [128, E8 * FB])
        b2 = t.sb("b2", [128, E8, C])
        bi = t.sb("bi", [128, 2, NI, C])
        bt_ = t.sb("bt", [C, 2, EBATCH])
        hid = t.sb("hid", [128, 2, FB, EBATCH])
        yo = t.sb("yo", [128, 2, NI, C])
        ps_t = [t.ps(f"ps_t{i}", [C, 512]) for i in range(2)]
        ps_u = [t.ps(f"ps_u{i}", [128, 512]) for i in range(4)]
        ps_y = [t.ps(f"ps_y{i}", [128, 512]) for i in range(2)]
        (b_in, b1_ps, b1_ok, bT, bt_ok, u_ps, hid_ok, y_ps, y_ok) = [t.sem(s) for s in (
            "biases_loaded b1_in_psum b1_ready bT_in_psum bt_ready u_in_psum hidden_ready y_in_psum y_ready").split()]
        w_in, bi_in, y_st = ([t.sem(f"{s}{p}") for p in range(2)] for s in (
            "weights_loaded", "rows_loaded", "y_stored"))
        bufv = buf_d.rearrange("(b i p) c -> b p i c", p=128, i=NI)
        resv = res_d.rearrange("(b i p) c -> b p i c", p=128, i=NI)

        with nc.Block() as block:

            @block.sync
            def _(sp):
                sp.dma_start(b1r[:, :], ins["L1_ffn_b1"].rearrange("e (f p) -> (e f) p", p=128)).then_inc(b_in, 16)
                sp.dma_start(b2[:, :, :], ins["L1_ffn_b2"].rearrange("e c -> (e c)").rearrange("(a n) -> a n", a=1)
                             .to_broadcast([128, E8 * C]).rearrange("p (e c) -> p e c", c=C)).then_inc(b_in, 16)
                with sp.Fori(0, E8 // 2) as i:
                    for x in range(2):
                        e = i * 2 + x
                        hold(sp, y_ps, e * NEB + 1, own)
                        sp.dma_start(w1[:, x, :], ins["L1_ffn_w1"][e, :, :]).then_inc(w_in[x], 16)
                        sp.dma_start(w2[:, x, :, :], ins["L1_ffn_w2"][e, :, :].rearrange("(f p) c -> p f c", p=128))\
                            .then_inc(w_in[x], 16)
                        for q in range(NEB):
                            n = e * NEB + q
                            hold(sp, bT, n + 1, own)
                            sp.dma_start(bi[:, q % 2, :, :], bufv[n]).then_inc(bi_in[q % 2], 16)

            @block.tensor
            def _(pe):
                pe.sem_inc(y_ps, NEB + 1)
                pe.sem_inc(bT, 2)
                pe.wait_ge(b_in, 32)
                pe.transpose(ps_t[0][:, 0:E8 * FB], b1r[:, :], ident[0:E8 * FB, 0:E8 * FB]).then_inc(b1_ps, 1)
                pe.wait_ge(b1_ok, 1)
                with pe.Fori(0, E8 // 2) as i:
                    for x in range(2):
                        hold(pe, w_in[x], i * 32 + 32, own)
                        for q in range(NEB):
                            n = (i * 2 + x) * NEB + q
                            p = q % 2
                            hold(pe, bi_in[p], (i * 2 + x) * (8 * NEB) + 16 * (q // 2 + 1), own)
                            hold(pe, bt_ok, n + 1, own)
                            for j in range(NI):
                                mm = pe.transpose(ps_t[p][:, j * 128:(j + 1) * 128], bi[:, p, j, :], ident[:, :])
                            mm.then_inc(bT, 1)
                            hold(pe, bt_ok, n + 3, own)
                            for f in range(FB):
                                hold(pe, hid_ok, n * FB + (f + 1), own)
                                pe.matmul(ps_u[f][:, :], w1[:, x, f * 128:(f + 1) * 128], bt_[:, p, :], start=True,
                                          stop=True).then_inc(u_ps, 1)
                            hold(pe, hid_ok, n * FB + 2 * FB, own)
                            hold(pe, y_ok, n + 1, own)
                            for j in range(NI):
                                for f in range(FB):
                                    mm = pe.matmul(ps_y[p][:, j * C:(j + 1) * C],
                                                   hid[:, p, f, j * 128:(j + 1) * 128], w2[:, x, f, :],
                                                   start=(f == 0), stop=(f == FB - 1))
                            mm.then_inc(y_ps, 1)

            @block.scalar
            def _(act):
                act.sem_inc(bt_ok, 2)
                act.sem_inc(hid_ok, FB)
                act.wait_ge(b1_ps, 1)
                nc.scalar.activation(b1t[:, :], ps_t[0][:, 0:E8 * FB], ACT.Copy).then_inc(b1_ok, 1)
                act.wait_ge(b1_ok, 1)
                with act.Fori(0, E8 // 2) as i:
                    for x in range(2):
                        e = i * 2 + x
                        for q in range(NEB):
                            n = e * NEB + q
                            p = q % 2
                            hold(act, bT, n + 3, own)
                            nc.scalar.activation(bt_[:, p, :], ps_t[p][:, :], ACT.Copy).then_inc(bt_ok, 1)
                            for f in range(FB):
                                hold(act, u_ps, n * FB + (f + 1), own)
                                nc.scalar.activation(hid[:, p, f, :], ps_u[f][:, :], ACT.Relu,
                                                     bias=b1t[:, bass.ds(e * FB + f, 1)], scale=1.0).then_inc(hid_ok, 1)
                            hold(act, y_ok, n + 3, own)
                            act.dma_start(resv[n], yo[:, p, :, :]).then_inc(y_st[p], 16)
                for p in range(2):
                    act.wait_ge(y_st[p], 16 * E8 * NEB // 2 + 1)

            @block.vector
            def _(dve):
                dve.sem_inc(y_ok, 2)
                for s in y_st:
                    dve.sem_inc(s, 1)
                with dve.Fori(0, E8 // 2) as i:
                    for x in range(2):
                        e = i * 2 + x
                        for q in range(NEB):
                            n = e * NEB + q
                            p = q % 2
                            hold(dve, y_ps, n + NEB + 2, own)
                            hold(dve, y_st[p], e * (8 * NEB) + 16 * (q // 2) + 1, own)
                            nc.vector.tensor_tensor(yo[:, p, :, :], ps_y[p][:, :].rearrange("p (t c) -> p t c", c=C),
                                                    spread(b2[:, e, :], 1, NI), ALU.add).then_inc(y_ok, 1)


def combine_stage(nc, k, res_d, tok, slots, weight, out):
    own = k["own"]
    with ExitStack() as es:
        t = Ctx(nc, es, "combine")
        yg = t.sb("yg", [128, 2, FG, C])
        yc = t.sb("yc", [128, 2, FG, C])
        fx = t.sb("fx", [128, 2, FG, C])
        mk = t.sb("mk", [128, 3, FG, C], I32)
        lim = t.sb("lim", [128, 2, FG, C])
        step, res, cst = (t.sem(s) for s in ("step", "result_ready", "constants_ready"))
        freed = t.sem("rows_freed")
        got = [t.sem(f"gathered{p}") for p in range(2)]
        stored = t.sem("stored")
        outv = out.rearrange("(p f) c -> p f c", p=128)

        with nc.Block() as block:

            @block.gpsimd
            def _(pool):
                pool.memset(lim[:, 0, :, :], 1e4).then_inc(cst, 1)
                pool.memset(lim[:, 1, :, :], -1e4).then_inc(cst, 1)
                for g in range(NFG):
                    if g >= 2:
                        pool.wait_ge(freed, g - 1)
                    for j in range(FG):
                        f = g * FG + j
                        pool.indirect_dma_start(
                            out=yg[:, g % 2, j, :], out_offset=None, in_=res_d,
                            in_offset=bass.IndirectOffsetOnAxis(ap=slots[:, 1, f:f + 1], axis=0),
                            bounds_check=E8 * SLOTS - 1, oob_is_err=False).then_inc(got[g % 2], 16)

            @block.vector
            def _(dve):
                n = [0]

                def do(ins_):
                    n[0] += 1
                    ins_.then_inc(step, 1)
                    return n[0]

                dve.wait_ge(cst, 2)
                for g in range(NFG):
                    p = g % 2
                    part = tok[:, g * FG:(g + 1) * FG, :]
                    dve.wait_ge(got[p], 16 * FG * (g // 2 + 1))
                    a = do(nc.vector.memset(fx[:, p, :, :], 0.0))
                    nc.vector.tensor_tensor(yc[:, p, :, :], yg[:, p, :, :],
                                            spread(weight[:, g * FG:(g + 1) * FG], 2, C), ALU.mult)\
                        .then_inc(freed, 1)
                    dve.wait_ge(freed, g + 1)
                    y = yc[:, p, :, :]
                    do(nc.vector.tensor_tensor(mk[:, 0, :, :], y, y, ALU.is_equal))
                    do(nc.vector.tensor_scalar(mk[:, 1, :, :], y, BIGGEST, None, ALU.is_gt))
                    a = do(nc.vector.tensor_scalar(mk[:, 2, :, :], y, -BIGGEST, None, ALU.is_lt))
                    dve.wait_ge(step, a)
                    dve.wait_ge(step, do(nc.vector.copy_predicated(fx[:, p, :, :], mk[:, 0, :, :], y)))
                    for i in range(2):
                        dve.wait_ge(step, do(nc.vector.copy_predicated(fx[:, p, :, :], mk[:, 1 + i, :, :],
                                                                       lim[:, i, :, :])))
                    nc.vector.tensor_tensor(part, part, fx[:, p, :, :], ALU.add).then_inc(res, 1)

            @block.sync
            def _(sp):
                for g in range(NFG):
                    sp.wait_ge(res, g + 1)
                    sp.dma_start(outv[:, g * FG:(g + 1) * FG, :], tok[:, g * FG:(g + 1) * FG, :]).then_inc(stored, 16)
                sp.wait_ge(stored, 16 * NFG)


def ffn(nc, k, c, ins, t4_d, buf_d, res_d, out):
    tok = c.sb("tokens", [128, NF, C])
    slots = c.sb("slots", [128, 2, NF], I32)
    weight = c.sb("weight", [128, NF])
    route_stage(nc, k, ins, t4_d, buf_d, tok, slots, weight)
    experts_stage(nc, k, ins, buf_d, res_d)
    combine_stage(nc, k, res_d, tok, slots, weight, out)


_NAMES = ["x", "L0_conv_w_in", "L0_conv_b_in", "L0_conv_w_dw", "L0_conv_b_dw", "L0_conv_ln_dw_g", "L0_conv_ln_dw_b",
          "L0_conv_w_off", "L0_conv_b_off", "L0_conv_w_mask", "L0_conv_b_mask", "L0_conv_w_out", "L0_conv_b_out",
          "L0_conv_ln1_g", "L0_conv_ln1_b", "L0_conv_w_fc1", "L0_conv_b_fc1", "L0_conv_w_fc2", "L0_conv_b_fc2",
          "L0_conv_ln2_g", "L0_conv_ln2_b", "L0_conv_gamma1", "L0_conv_gamma2", "L1_attn_Wq", "L1_attn_Wk",
          "L1_attn_Wv", "L1_attn_bv", "L1_attn_Wt", "L1_attn_bt", "L1_attn_gamma", "L1_attn_beta", "L1_attn_bn_mean",
          "L1_attn_bn_var", "L1_ffn_gate_w", "L1_ffn_gate_b", "L1_ffn_w1", "L1_ffn_b1", "L1_ffn_w2", "L1_ffn_b2"]


def build(nc, ins, out):
    def scratch(name, shape):
        return nc.dram_tensor(name, shape, F32, kind="Internal").ap()

    xp_d = scratch("projected", (T + 2 * PAD, C))
    om_d = scratch("offsets_masks", (B * HH, TP, OM))
    y_d = scratch("deformed", (B * HH, TP, C))
    t_d = scratch("block_out", (B * HH, TP, C))
    xc_d = scratch("block_out_normed", (B * HH, TP, C))
    t4_d = scratch("attended", (T, C))
    buf_d = scratch("dispatched", (E8 * SLOTS, C))
    res_d = scratch("expert_out", (E8 * SLOTS, C))

    with ExitStack() as everything:
        k = identity(nc, Ctx(nc, everything, "all"))
        with ExitStack() as block:
            c = Ctx(nc, block, "block")
            constants(nc, c, ins, k)
            shift_tables(nc, k, c)
            extremes = c.sb("extremes", [TP, NB, 4])
            base = c.sb("base", [TP, 2])
            counts = c.sb("counts", [1, 4], I32)
            zero_stage(nc, [y_d.rearrange("t p c -> (t p c)"), buf_d.rearrange("n c -> (n c)")])
            offsets_stage(nc, k, ins["x"], xp_d, om_d, extremes)
            window_stage(nc, k, extremes, base, counts)
            deformable_stage(nc, k, xp_d, om_d, y_d, base, counts)
            rows_stage(nc, k, ins["x"], y_d, t_d, xc_d)
        attention_stage(nc, k, ins, xc_d, t_d, t4_d)
        ffn(nc, k, Ctx(nc, everything, "ffn"), ins, t4_d, buf_d, res_d, out.rearrange("b y x c -> (b y x) c"))


def kernel(**inputs):
    import numpy as np
    import concourse.bacc as bacc
    from concourse.bass_utils import run_bass_kernel_spmd as run

    nc = bacc.Bacc("TRN2", target_bir_lowering=False, num_devices=1)
    arrays, ins = {}, {}
    for name in _NAMES:
        a = np.ascontiguousarray(inputs[name])
        arrays[f"in_{name}"] = a
        ins[name] = nc.dram_tensor(f"in_{name}", a.shape, mybir.dt.from_np(a.dtype), kind="ExternalInput").ap()
    out = nc.dram_tensor("out", (B, H, W, C), F32, kind="ExternalOutput").ap()
    build(nc, ins, out)
    return run(nc, [arrays], core_ids=[0]).results[0]["out"]
```

```python
from contextlib import ExitStack

import concourse.bass as bass
from concourse import mybir

F32 = mybir.dt.float32
I32 = mybir.dt.int32
ALU = mybir.AluOpType
ACT = mybir.ActivationFunctionType
AX = mybir.AxisListType.X
MAX = bass.bass_isa.ReduceOp.max

B, H, W, C = 4, 56, 56, 128
G, K = 16, 9
GC = C // G
HH = H // 2
TP = 2 * W
NPIX = H * W
T = B * NPIX
GK = G * K
OM = 3 * GK
QT = 4
NQ = HH // QT
NB = B * NQ

R = 7
CW = R + 2
ROWS = HH + CW - 1
RING = 16
OFFMAX = 60.0
PAD = (int(OFFMAX) + R + 6) * W
EPS = 1e-5


class Ctx:

    def __init__(self, nc, stack, stage):
        self.nc, self.stack, self.stage, self.sems = nc, stack, stage, []
        stack.callback(self.close)

    def sb(self, name, shape, dt=F32):
        return self.stack.enter_context(self.nc.sbuf_tensor(f"{self.stage}_{name}", shape, dt))

    def ps(self, name, shape):
        return self.stack.enter_context(self.nc.psum_tensor(f"{self.stage}_{name}", shape, F32))

    def sem(self, name):
        self.sems.append(self.nc.alloc_semaphore(f"{self.stage}_{name}"))
        return self.sems[-1]

    def close(self):
        if self.sems:
            self.nc.clear_and_free_semaphores(self.sems)
            self.nc.all_engine_barrier()


def spread(ap, axis, n):
    v = ap.unsqueeze(axis)
    shape = list(v.shape)
    shape[axis] = n
    return v.to_broadcast(shape)


def row(ap):
    return ap.rearrange("(a n) -> a n", a=1)


def col(ap):
    return ap.rearrange("(n a) -> n a", a=1)


def hold(eng, sem, value, own):
    eng.wait_ge(sem, value)
    eng.sem_inc(own, 1)


def identity(nc, c):
    k = {"ident": c.sb("ident", [128, 128]), "own": c.sem("wait_carrier")}
    with ExitStack() as es:
        t = Ctx(nc, es, "identity")
        zeroed = t.sem("zeroed")
        with nc.Block() as block:

            @block.gpsimd
            def _(pool):
                pool.memset(k["ident"][:, :], 0.0).then_inc(zeroed, 1)
                pool.wait_ge(zeroed, 1)
                pool.affine_select(out=k["ident"][:, :], in_=k["ident"][:, :], compare_op=ALU.not_equal, fill=1.0,
                                   base=0, pattern=[[-1, 128]], channel_multiplier=1)
    return k


def constants(nc, c, ins, k):
    for name, src in (("w_in", "L0_conv_w_in"), ("w_out", "L0_conv_w_out"), ("w_fc1", "L0_conv_w_fc1"),
                      ("w_fc2", "L0_conv_w_fc2")):
        k[name] = c.sb(name, [C, C])
    k["w_dw"] = c.sb("w_dw", [C, K])
    k["w_om"] = c.sb("w_om", [C, OM])
    k["b_om"] = c.sb("b_om", [128, OM])
    for name in ("b_in", "b_out", "ln1_g", "ln1_b", "b_fc2", "ln2_g", "ln2_b", "gamma1", "gamma2"):
        k[name] = c.sb(name + "_rows", [128, C])
    for name in ("b_dw", "ln_dw_g", "ln_dw_b", "b_fc1"):
        k[name] = c.sb(name + "_col", [C, 1])
    with ExitStack() as es:
        t = Ctx(nc, es, "const")
        raw_w = t.sb("raw_w", [C, OM])
        raw_b = t.sb("raw_b", [128, OM])
        raw_d = t.sb("raw_dw", [K, C])
        loaded, turned = t.sem("loaded"), t.sem("turned")
        psw = t.ps("psw", [C, 512])
        with nc.Block() as block:
            n_loads = [0]

            @block.sync
            def _(sp):
                def load(dst, src):
                    sp.dma_start(dst, src).then_inc(loaded, 16)
                    n_loads[0] += 16

                for name in ("w_in", "w_out", "w_fc1", "w_fc2"):
                    load(k[name][:, :], ins["L0_conv_" + name])
                load(raw_d[:, :], ins["L0_conv_w_dw"].rearrange("a b o c -> (a b o) c"))
                load(raw_w[:, 0:2 * GK], ins["L0_conv_w_off"])
                load(raw_w[:, 2 * GK:OM], ins["L0_conv_w_mask"])
                load(raw_b[:, 0:2 * GK], row(ins["L0_conv_b_off"]).to_broadcast([128, 2 * GK]))
                load(raw_b[:, 2 * GK:OM], row(ins["L0_conv_b_mask"]).to_broadcast([128, GK]))
                for name in ("b_in", "b_out", "ln1_g", "ln1_b", "b_fc2", "ln2_g", "ln2_b", "gamma1", "gamma2"):
                    load(k[name][:, :], row(ins["L0_conv_" + name]).to_broadcast([128, C]))
                for name in ("b_dw", "ln_dw_g", "ln_dw_b", "b_fc1"):
                    load(k[name][:, :], col(ins["L0_conv_" + name]))

            @block.tensor
            def _(pe):
                pe.wait_ge(loaded, n_loads[0])
                pe.transpose(psw[:, 0:K], raw_d[:, :], k["ident"][0:K, 0:K]).then_inc(turned, 1)

            @block.vector
            def _(dve):
                dve.wait_ge(loaded, n_loads[0])
                for raw, dst in ((raw_w, k["w_om"]), (raw_b, k["b_om"])):
                    for xy in range(2):
                        nc.vector.tensor_copy(
                            dst[:, xy * GK:(xy + 1) * GK].rearrange("c (k g) -> c k g", g=G),
                            raw[:, 0:2 * GK].rearrange("c (g k d) -> c k g d", k=K, d=2)[:, :, :, xy])
                    nc.vector.tensor_copy(dst[:, 2 * GK:OM].rearrange("c (k g) -> c k g", g=G),
                                          raw[:, 2 * GK:OM].rearrange("c (g k) -> c k g", k=K))
                dve.wait_ge(turned, 1)
                nc.vector.tensor_copy(k["w_dw"][:, :], psw[:, 0:K])


def offsets_stage(nc, k, x, xp_d, om_d, extremes):
    own, ident = k["own"], k["ident"]
    with ExitStack() as es:
        t = Ctx(nc, es, "offs")
        x_sb = t.sb("x_sb", [TP, HH, C])
        xpad = t.sb("xpad", [C, (H + 2) * (W + 2)])
        xt = t.sb("xt", [C, HH, TP])
        conv = t.sb("conv", [C, HH, 2, W])
        st = t.sb("st", [TP, 2, QT, 6])
        mv = t.sb("mv", [TP, 2, QT, 2])
        ve = t.sb("ve", [TP, 2, QT])
        rs = t.sb("rs", [TP, 2, QT])
        half = t.sb("half", [TP, QT])
        xn = t.sb("xn", [TP, 2, QT, C])
        x1t = t.sb("x1t", [C, 2, QT * TP])
        om = t.sb("om", [TP, 2, QT, OM])
        mx = t.sb("mx", [TP, 2, QT, G])
        xp = t.sb("xp", [TP, 2, QT, C])
        zero = t.sb("zero", [TP, 4 * C])
        ps_x = [t.ps(f"ps_x{i}", [C, 512]) for i in range(1)]
        ps_c = t.ps("ps_c", [TP, 512])
        ps_n = t.ps("ps_n", [C, 512])
        ps_o = t.ps("ps_o", [TP, QT, 512])
        ps_p = t.ps("ps_p", [TP, 512])
        (x_in, x_used, xT, xT_ev, xT_out, conv_step, conv_done, convT, convT_used, stat, agg, eps, rstd, xn_ok, xnT,
         x1, om_ps, om_ev, om_sub, om_exp, om_clamp, om_max, om_ok, xp_ok, om_st, xp_st, ext, zr, half_ok, xz, pad_st) = [
            t.sem(s) for s in (
                "x_loaded", "x_used", "xT_in_psum", "xT_evacuated", "xT_copied", "conv_step", "conv_done",
                "convT_in_psum", "convT_used", "stats_ready", "mean_var_ready", "var_eps_ready", "rstd_ready",
                "xn_ready", "xnT_in_psum", "x1_ready", "om_in_psum", "om_evacuated", "om_less_max", "om_exp", "om_clamped", "om_max_ready",
                "om_ready", "xp_ready", "om_stored", "xp_stored", "extremes_done", "pad_zero_ready", "half_ready",
                "xpad_zeroed", "pad_stored")]
        xv = x.rearrange("b (h j) x c -> b h x j c", h=2)
        xpv = xp_d[PAD:PAD + T, :].rearrange("(b h j x) c -> b h x j c", b=B, h=2, x=W)
        xpad3 = xpad[:, :].rearrange("c (y x) -> c y x", x=W + 2)
        with nc.Block() as block:

            @block.sync
            def _(sp):
                sp.wait_ge(zr, 1)
                rows_out = TP * 4
                for base in (0, PAD + T):
                    for r0 in range(0, PAD, rows_out):
                        n = min(rows_out, PAD - r0) // 4
                        sp.dma_start(xp_d[base + r0:base + r0 + 4 * n, :].rearrange("(p f) c -> p (f c)", f=4),
                                     zero[0:n, :]).then_inc(pad_st, 16)
                npad = 2 * len(range(0, PAD, rows_out))

                def load(b):
                    for h in range(2):
                        sp.dma_start(x_sb[h * W:(h + 1) * W, :, :], xv[b, h]).then_inc(x_in, 16)

                load(0)
                for b in range(B):
                    if b + 1 < B:
                        sp.wait_ge(x_used, b + 1)
                        load(b + 1)
                    with sp.Fori(0, NQ) as q:
                        n = q + b * NQ
                        sp.wait_ge(xp_ok, n + 1)
                        for h in range(2):
                            sp.dma_start(xpv[b, h, :, bass.ds(q * QT, QT), :],
                                         xp[h * W:(h + 1) * W, n % 2, :, :]).then_inc(xp_st, 16)
                        sp.wait_ge(om_ok, n + 1)
                        sp.dma_start(om_d[bass.ds(n * QT, QT), :, :].rearrange("t p o -> p t o"),
                                     om[:, n % 2, :, :]).then_inc(om_st, 16)
                sp.wait_ge(pad_st, 16 * npad)
                sp.wait_ge(xp_st, 32 * NB + 1)
                sp.wait_ge(om_st, 16 * NB + 1)

            @block.gpsimd
            def _(pool):
                pool.memset(half[:, :], -0.5).then_inc(half_ok, 1)
                pool.wait_ge(half_ok, 1)
                with pool.Fori(0, B) as b:
                    for q in range(NQ):
                        n = b * NQ + q
                        hold(pool, agg, n + 1, own)
                        pool.tensor_scalar(ve[:, q % 2, :], mv[:, q % 2, :, 1], EPS, None, ALU.add).then_inc(eps, 1)
                        hold(pool, eps, n + 1, own)
                        pool.tensor_tensor(rs[:, q % 2, :], ve[:, q % 2, :], half[:, :], ALU.pow).then_inc(rstd, 1)

            @block.tensor
            def _(pe):
                def conv_turn(n, q):
                    hold(pe, convT_used, n + 1, own)
                    for i in range(QT):
                        mm = pe.transpose(ps_c[:, i * C:(i + 1) * C],
                                          conv[:, q * QT + i, :, :].rearrange("c h x -> c (h x)"), ident[:, :])
                    mm.then_inc(convT, 1)

                with pe.Fori(0, B) as b:
                    hold(pe, x_in, 32 * b + 32, own)
                    for q in range(NQ):
                        hold(pe, xT_ev, b * NQ + q + 1, own)
                        for i in range(QT):
                            mm = pe.transpose(ps_x[0][:, i * TP:(i + 1) * TP], x_sb[:, q * QT + i, :],
                                              ident[0:TP, 0:TP])
                        mm.then_inc(xT, 1)
                    hold(pe, conv_done, b + 1 + 1, own)
                    conv_turn(b * NQ, 0)
                    for q in range(NQ):
                        n = b * NQ + q
                        if q + 1 < NQ:
                            conv_turn(n + 1, q + 1)
                        hold(pe, xn_ok, n + 1, own)
                        hold(pe, x1, n + 1, own)
                        for i in range(QT):
                            mm = pe.transpose(ps_n[:, i * TP:(i + 1) * TP], xn[:, q % 2, i, :],
                                              ident[0:TP, 0:TP])
                        mm.then_inc(xnT, 1)
                        hold(pe, om_ev, n + 1, own)
                        for i in range(QT):
                            mm = pe.matmul(ps_p[:, i * C:(i + 1) * C], xt[:, q * QT + i, :], k["w_in"][:, :],
                                           start=True, stop=True)
                        hold(pe, x1, n + 2, own)
                        for i in range(QT):
                            mm = pe.matmul(ps_o[:, i, 0:OM], x1t[:, q % 2, i * TP:(i + 1) * TP],
                                           k["w_om"][:, :], start=True, stop=True)
                        mm.then_inc(om_ps, 1)

            @block.scalar
            def _(act):
                act.sem_inc(xT_ev, 1)
                act.sem_inc(x1, 1)
                act.wait_ge(xz, 1)
                with act.Fori(0, B) as b:
                    for q in range(NQ):
                        n = b * NQ + q
                        if q == 0:
                            hold(act, conv_done, b + 1, own)
                            hold(act, om_ps, b * NQ + 1, own)
                        hold(act, xT, n + 1, own)
                        src = ps_x[0][:, 0:QT * TP].rearrange("c (j h x) -> c j h x", h=2, x=W)
                        for h in range(2):
                            y = h * HH + q * QT + 1
                            nc.scalar.activation(xpad3[:, y:y + QT, 1:W + 1], src[:, :, h, :], ACT.Copy)
                        nc.scalar.activation(xt[:, q * QT:(q + 1) * QT, :],
                                             ps_x[0][:, 0:QT * TP].rearrange("c (j p) -> c j p", p=TP),
                                             ACT.Copy).then_inc(xT_ev, 1)
                        if q == NQ - 1:
                            act.drain().then_inc(x_used, 1)
                    for q in range(NQ):
                        n = b * NQ + q
                        hold(act, xnT, n + 1, own)
                        hold(act, om_ps, n + 1, own)
                        nc.scalar.activation(x1t[:, q % 2, :], ps_n[:, 0:QT * TP], ACT.Gelu,
                                             bias=k["ln_dw_b"][:, 0:1], scale=k["ln_dw_g"][:, 0:1]).then_inc(x1, 1)
                        hold(act, om_sub, n + 1, own)
                        masks = om[:, n % 2, :, 2 * GK:OM]
                        nc.scalar.activation(masks, masks, ACT.Exp).then_inc(om_exp, 1)

            @block.vector
            def _(dve):
                nc.vector.memset(zero[:, :], 0.0).then_inc(zr, 1)
                nc.vector.memset(xpad[:, :], 0.0).then_inc(xz, 1)
                dve.sem_inc(convT_used, 1)
                dve.sem_inc(om_ev, 1)
                for s in (convT, conv_done, om_ps, om_st, xp_st):
                    dve.sem_inc(s, 1)

                def normalise(n, q):
                    hold(dve, convT, n + 1 + 1, own)
                    for i in range(QT):
                        ins_ = nc.vector.bn_stats(st[:, q % 2, i, :], ps_c[:, i * C:(i + 1) * C])
                    ins_.then_inc(stat, 1)
                    hold(dve, stat, n + 1, own)
                    for i in range(QT):
                        ins_ = nc.vector.bn_aggr(mv[:, q % 2, i, :], st[:, q % 2, i, :])
                    ins_.then_inc(agg, 1)
                    hold(dve, rstd, n + 1, own)
                    for i in range(QT):
                        ins_ = nc.vector.tensor_scalar(xn[:, q % 2, i, :], ps_c[:, i * C:(i + 1) * C],
                                                       mv[:, q % 2, i, 0:1], rs[:, q % 2, i:i + 1],
                                                       ALU.subtract, ALU.mult)
                    ins_.then_inc(xn_ok, 1)
                    dve.wait_ge(xn_ok, n + 1)
                    dve.sem_inc(convT_used, 1)

                def evacuate(n):
                    hold(dve, om_ps, n + 1 + 1, own)
                    hold(dve, om_st, 16 * n + 1, own)
                    hold(dve, xp_st, 32 * n + 1, own)
                    nc.vector.tensor_tensor(xp[:, n % 2, :, :],
                                            ps_p[:, :].rearrange("p (t c) -> p t c", c=C),
                                            spread(k["b_in"][0:TP, :], 1, QT), ALU.add).then_inc(xp_ok, 1)
                    nc.vector.tensor_tensor(om[:, n % 2, :, :], ps_o[:, :, 0:OM],
                                            spread(k["b_om"][0:TP, :], 1, QT), ALU.add).then_inc(om_ev, 1)
                    hold(dve, om_ev, n + 2, own)
                    logits = om[:, n % 2, :, 2 * GK:OM]
                    nc.vector.tensor_reduce(mx[:, n % 2, :, :], logits.rearrange("p t (k g) -> p t g k", g=G),
                                            AX, ALU.max).then_inc(om_max, 1)
                    nc.vector.tensor_scalar(om[:, n % 2, :, 0:2 * GK], om[:, n % 2, :, 0:2 * GK],
                                            OFFMAX, -OFFMAX, ALU.min, ALU.max).then_inc(om_clamp, 1)
                    lk = logits.rearrange("p t (k g) -> p t k g", g=G)
                    hold(dve, om_max, 4 * n + 1, own)
                    nc.vector.tensor_tensor(lk, lk, spread(mx[:, n % 2, :, :], 2, K), ALU.subtract)\
                        .then_inc(om_sub, 1)
                    hold(dve, om_clamp, n + 1, own)
                    for xy in range(2):
                        part = om[:, n % 2, :, xy * GK:(xy + 1) * GK]
                        nc.vector.tensor_reduce(extremes[:, n, 2 * xy:2 * xy + 1], part, mybir.AxisListType.XY,
                                                ALU.min, negate=True)
                        last = nc.vector.tensor_reduce(extremes[:, n, 2 * xy + 1:2 * xy + 2], part,
                                                       mybir.AxisListType.XY, ALU.max)
                    hold(dve, om_exp, n + 1, own)
                    nc.vector.tensor_reduce(mx[:, n % 2, :, :], logits.rearrange("p t (k g) -> p t g k", g=G),
                                            AX, ALU.add).then_inc(om_max, 1)
                    hold(dve, om_max, 4 * n + 2, own)
                    nc.vector.reciprocal(mx[:, n % 2, :, :], mx[:, n % 2, :, :]).then_inc(om_max, 1)
                    hold(dve, om_max, 4 * n + 3, own)
                    nc.vector.tensor_tensor(lk, lk, spread(mx[:, n % 2, :, :], 2, K), ALU.mult)\
                        .then_inc(om_max, 1)
                    dve.wait_ge(om_max, 4 * n + 4)
                    dve.sem_inc(om_ok, 1)

                taps = [(ky, kx, h) for ky in range(3) for kx in range(3) for h in range(2)]
                with dve.Fori(0, B) as b:
                    hold(dve, xT_ev, NQ * b + NQ + 1, own)
                    hold(dve, convT, NQ * b + 1, own)
                    for s, (ky, kx, h) in enumerate(taps):
                        out = conv[:, :, h, :]
                        src = xpad3[:, h * HH + ky:h * HH + ky + HH, kx:kx + W]
                        tap = k["w_dw"][:, 3 * ky + kx:3 * ky + kx + 1]
                        if s < 2:
                            nc.vector.tensor_scalar(out, src, tap, k["b_dw"][:, 0:1], ALU.mult, ALU.add)\
                                .then_inc(conv_step, 1)
                        else:
                            dve.wait_ge(conv_step, b * len(taps) + s - 1)
                            nc.vector.scalar_tensor_tensor(out, src, tap, out, ALU.mult, ALU.add)\
                                .then_inc(conv_step, 1)
                    hold(dve, conv_step, b * len(taps) + len(taps), own)
                    dve.sem_inc(conv_done, 1)
                    normalise(b * NQ, 0)
                    for q in range(NQ):
                        n = b * NQ + q
                        if q + 1 < NQ:
                            normalise(n + 1, q + 1)
                        evacuate(n)


def window_stage(nc, k, extremes, base, counts):
    own = k["own"]
    with ExitStack() as es:
        t = Ctx(nc, es, "window")
        ext = t.sb("ext", [TP, 4])
        ext_all = t.sb("ext_all", [TP, 4])
        ei = t.sb("ei", [TP, 4], I32)
        ef = t.sb("ef", [TP, 4])
        eg = t.sb("eg", [TP, 4])
        nb = t.sb("nb", [TP, 2])
        step, allm = t.sem("w_step"), t.sem("w_all")
        with nc.Block() as block:

            @block.gpsimd
            def _(pool):
                pool.wait_ge(step, 1)
                pool.partition_all_reduce(ext_all[:, :], ext[:, :], TP, MAX).then_inc(allm, 1)

            @block.vector
            def _(dve):
                n = [0]

                def do(ins_):
                    n[0] += 1
                    ins_.then_inc(step, 1)
                    dve.wait_ge(step, n[0])

                do(nc.vector.tensor_reduce(ext[:, :], extremes[:, :, :].rearrange("p n s -> p s n"), AX, ALU.max))
                dve.wait_ge(allm, 1)
                for c0 in (0, 2):
                    do(nc.vector.tensor_scalar(ext_all[:, c0:c0 + 1], ext_all[:, c0:c0 + 1], -1.0, None, ALU.mult))

                def floor(v, out, i, f):
                    do(nc.vector.tensor_copy(i, v))
                    do(nc.vector.tensor_copy(f, i))
                    do(nc.vector.tensor_tensor(out, f, v, ALU.is_gt))
                    do(nc.vector.tensor_tensor(out, f, out, ALU.subtract))

                floor(ext_all[:, :], eg[:, :], ei[:, :], ef[:, :])
                do(nc.vector.tensor_copy(base[:, :], eg[:, 0::2]))
                do(nc.vector.tensor_tensor(nb[:, :], eg[:, 1::2], eg[:, 0::2], ALU.subtract))
                do(nc.vector.tensor_scalar(nb[:, :], nb[:, :], float(2 + R - 1) + 0.1, 1.0 / R, ALU.add, ALU.mult))
                floor(nb[:, :], ef[:, 0:2], ei[:, 0:2], eg[:, 0:2])
                do(nc.vector.tensor_copy(counts[:, 0:2], ef[0:1, 0:2]))
                do(nc.vector.tensor_copy(counts[:, 2:4], base[0:1, 0:2]))


def shift_tables(nc, k, c):
    k["steps"] = c.sb("steps", [TP, R])
    k["xpos"] = c.sb("xpos", [TP, CW])
    k["ypos"] = c.sb("ypos", [TP, ROWS])
    with ExitStack() as es:
        t = Ctx(nc, es, "tables")
        raw = t.sb("raw", [TP, ROWS], I32)
        part = t.sb("part", [TP, 1], I32)
        pf = t.sb("pf", [TP, 1])
        hf = t.sb("hf", [TP, 1])
        hx = t.sb("hx", [TP, 1])
        made, step = t.sem("t_made"), t.sem("t_step")
        with nc.Block() as block:

            @block.gpsimd
            def _(pool):
                pool.iota(raw[:, :], [[1, ROWS]], base=0, channel_multiplier=0).then_inc(made, 1)
                pool.iota(part[:, :], [[1, 1]], base=0, channel_multiplier=1).then_inc(made, 1)

            @block.vector
            def _(dve):
                n = [0]

                def do(ins_):
                    n[0] += 1
                    ins_.then_inc(step, 1)
                    dve.wait_ge(step, n[0])

                dve.wait_ge(made, 2)
                do(nc.vector.tensor_copy(pf[:, :], part[:, :]))
                do(nc.vector.tensor_copy(k["steps"][:, :], raw[:, 0:R]))
                do(nc.vector.tensor_copy(k["xpos"][:, :], raw[:, 0:CW]))
                do(nc.vector.tensor_copy(k["ypos"][:, :], raw[:, :]))
                do(nc.vector.tensor_scalar(hf[:, :], pf[:, :], W - 0.5, None, ALU.is_gt))
                do(nc.vector.tensor_scalar(hx[:, :], hf[:, :], -float(W), pf[:, 0:1], ALU.mult, ALU.add))
                do(nc.vector.tensor_scalar(k["xpos"][:, :], k["xpos"][:, :], hx[:, 0:1], -1.0, ALU.add, ALU.add))
                do(nc.vector.tensor_scalar(hf[:, :], hf[:, :], float(HH), -1.0, ALU.mult, ALU.add))
                do(nc.vector.tensor_scalar(k["ypos"][:, :], k["ypos"][:, :], hf[:, 0:1], None, ALU.add))


def zero_stage(nc, regions):
    with ExitStack() as es:
        t = Ctx(nc, es, "zero")
        wide = 64 * C
        z = t.sb("z", [128, wide])
        made, stored = t.sem("made"), t.sem("stored")
        with nc.Block() as block:

            @block.vector
            def _(dve):
                nc.vector.memset(z[:, :], 0.0).then_inc(made, 1)

            @block.sync
            def _(sp):
                sp.wait_ge(made, 1)
                count = 0
                for flat in regions:
                    v = flat.rearrange("(p n) -> p n", p=128)
                    for i in range(0, v.shape[1], wide):
                        n = min(wide, v.shape[1] - i)
                        sp.dma_start(v[:, i:i + n], z[:, 0:n]).then_inc(stored, 16)
                        count += 16
                sp.wait_ge(stored, count)


POOL_TAPS = [6, 7, 8, 5, 4]
DVE_TAPS = [k for k in range(K) if k not in POOL_TAPS]
NPROD = 4
NOM = 4
LOW = 1


def window_pass(nc, k, t, bufs, sems, xp_d, om_d, y_d, row0, col0):
    own, ident = k["own"], k["ident"]
    (om, ab, hat, hym, wd, wp, ad, ap, prod, ring, yprev, yout, mask, negr, zeros, cur, vt) = bufs
    (setup, om_in, yp_in, row_in, masked, abs_ok, hats_ok, blank, hym_ok, pstep, wp_ok, w_done, dstep,
     prod_ok, prod_used, acc_free, y_ok, y_st, tile_done, applied) = sems
    acc = t["acc"]
    xpt = xp_d.tensor

    with nc.Block() as block:

        @block.sync
        def _(sp):
            def load_row(b, u, prior):
                if prior is not None:
                    sp.wait_ge(row_in, prior)
                slot = (u + b * ROWS) % RING
                for h in range(2):
                    pix = (u + (row0 - 1 + h * HH)) * W + (col0 - 1 + PAD + b * NPIX)
                    src = bass.AP(xpt, pix * C, [[C, W], [1, CW * C]])
                    sp.dma_start(ring[h * W:(h + 1) * W, slot, :], src).then_inc(row_in, 16)

            def load_tile(n):
                sp.dma_start(om[:, n % NOM, :], om_d[n, :, :]).then_inc(om_in, 16)
                sp.dma_start(yprev[:, n % NOM, :], y_d[n, :, :]).then_inc(yp_in, 16)

            def store(n):
                hold(sp, y_ok, n + 1, own)
                sp.dma_start(y_d[n, :, :], yout[:, n % 2, :]).then_inc(y_st, 16)

            load_tile(0)
            load_row(0, 0, None)
            for n in range(1, NOM - 1):
                sp.wait_ge(om_in, 16 * n)
                sp.wait_ge(yp_in, 16 * n)
                load_tile(n)
            with sp.Fori(1, RING) as u:
                load_row(0, u, 32 * u)
            for b in range(B):
                def step(j, tile, next_row):
                    n = j + b * HH
                    hold(sp, tile_done, n + 1, own)
                    if tile:
                        sp.wait_ge(om_in, 16 * (n + NOM - 1))
                        sp.wait_ge(yp_in, 16 * (n + NOM - 1))
                        load_tile(n + (NOM - 1))
                    if next_row == "same":
                        load_row(b, j + RING, 32 * (j + RING + b * ROWS))
                    elif next_row == "next":
                        load_row(b + 1, j - (ROWS - RING), 32 * (j + RING + b * ROWS))
                    if type(n) is not int:
                        store(n - 1)

                first = 0
                if b == 0:
                    step(0, True, "same")
                    first = 1
                with sp.Fori(first, ROWS - RING) as j:
                    step(j, True, "same")
                if b + 1 < B:
                    with sp.Fori(ROWS - RING, HH) as j:
                        step(j, True, "next")
                    with sp.Fori(HH - (ROWS - RING), RING) as u:
                        load_row(b + 1, u, 32 * (u + (b + 1) * ROWS))
                else:
                    with sp.Fori(ROWS - RING, HH - NOM + 1) as j:
                        step(j, True, None)
                    with sp.Fori(HH - NOM + 1, HH) as j:
                        step(j, False, None)
            store(B * HH - 1)
            sp.wait_ge(y_st, 16 * B * HH + 1)

        def grid(w):
            return w.rearrange("p (y x g) -> p y x g", y=CW, x=CW)

        @block.scalar
        def _(act):
            act.wait_ge(setup, 1)

            def hats(n):
                hold(act, om_in, n * 16 + 16, own)
                hold(act, w_done, n + 1, own)
                for xy in range(2):
                    for r in range(R):
                        last = nc.scalar.activation(ab[:, n % 2, xy, r, :], om[:, n % NOM, xy * GK:(xy + 1) * GK],
                                                    ACT.Abs, bias=negr[:, xy, r:r + 1], scale=1.0)
                last.then_inc(abs_ok, 1)
                clear_edge(wp[:, n % 2, :], CW - R)
                nc.scalar.activation(wp[:, n % 2, LOW * CW * G:(CW - R) * CW * G],
                                     zeros[:, 0:(CW - R - LOW) * CW * G], ACT.Copy)
                hold(act, abs_ok, n + 1, own)
                nc.scalar.activation(hat[:, n % 2, :, :, :], ab[:, n % 2, :, :, :], ACT.Relu, bias=1.0, scale=-1.0)\
                    .then_inc(hats_ok, 1)

            def clear_edge(w, y):
                right = grid(w)[:, y:y + R, R:CW, :]
                nc.scalar.activation(right.rearrange("p y x g -> p y (x g)"), spread(zeros[:, 0:(CW - R) * G], 1, R),
                                     ACT.Copy)

            def clear_sum(n):
                hold(act, applied, n + 1, own)
                clear_edge(wd[:, n % 2, :], 0)
                nc.scalar.activation(wd[:, n % 2, R * CW * G:CW * CW * G], zeros[:, :], ACT.Copy).then_inc(blank, 1)

            def mask_row(b, u):
                row_n = u + b * ROWS
                hold(act, row_in, 32 * (row_n + 1), own)
                r3 = ring[:, row_n % RING, :].rearrange("p (s c) -> p s c", c=C)
                for s in range(CW):
                    last = nc.scalar.activation(r3[:, s, :], r3[:, s, :], ACT.Copy, scale=mask[:, u, s:s + 1])
                last.then_inc(masked, 1)

            def finish(n):
                hold(act, prod_used, n * CW + (CW + NPROD), own)
                hold(act, y_st, n * 16 + 1, own)
                nc.scalar.activation(yout[:, n % 2, :], acc[:, n % 2, 0:C], ACT.Copy).then_inc(y_ok, 1)
                hold(act, y_ok, n + 1, own)
                act.sem_inc(acc_free, 1)

            for n in range(2):
                hats(n)
                clear_sum(n)
            for b in range(B):
                with act.Fori(0, CW) as u:
                    mask_row(b, u)
                with act.Fori(0, HH - 1 if b + 1 < B else HH - 2) as j:
                    n = j + b * HH
                    hats(n + 2)
                    mask_row(b, j + CW)
                    clear_sum(n + 2)
                    finish(n)
                if b + 1 < B:
                    n = b * HH + HH - 1
                    hats(n + 2)
                    clear_sum(n + 2)
                    finish(n)
            mask_row(B - 1, ROWS - 1)
            for n in range(B * HH - 2, B * HH):
                finish(n)

        def outer(dst, hx, hy, tap):
            return (dst, spread(hx[:, :, tap * G:(tap + 1) * G], 1, R), spread(hy[:, :, tap * G:(tap + 1) * G], 2, R))

        def region(w, tap):
            ky, kx = tap // 3, tap % 3
            return grid(w)[:, ky:ky + R, kx:kx + R, :]

        def box(a):
            return a.rearrange("p (y x g) -> p y x g", y=R, x=R)

        @block.gpsimd
        def _(pool):
            pool.wait_ge(setup, 1)

            PER = 2 * len(POOL_TAPS) - 2
            with pool.Fori(0, B * HH) as n:
                hold(pool, w_done, n + 1, own)
                hold(pool, hats_ok, n + 1, own)
                hx, hy = hat[:, n % 2, 0, :, :], hat[:, n % 2, 1, :, :]
                hm = hym[:, n % 2, :, :]
                pool.tensor_tensor(hm, hy, spread(om[:, n % NOM, 2 * GK:OM], 1, R), ALU.mult).then_inc(hym_ok, 1)
                w = wp[:, n % 2, :]
                hold(pool, hym_ok, n + 1, own)
                o, a, c = outer(region(w, POOL_TAPS[0]), hx, hm, POOL_TAPS[0])
                pool.tensor_tensor(o, a, c, ALU.mult).then_inc(pstep, 1)
                done = 1

                def mul(i):
                    o, a, c = outer(box(ap[:, i % 3, :]), hx, hm, POOL_TAPS[i])
                    pool.tensor_tensor(o, a, c, ALU.mult).then_inc(pstep, 1)

                mul(1)
                done += 1
                for i in range(1, len(POOL_TAPS)):
                    ready = done
                    if i + 1 < len(POOL_TAPS):
                        mul(i + 1)
                        done += 1
                    hold(pool, pstep, n * PER + ready, own)
                    r = region(w, POOL_TAPS[i])
                    last = pool.tensor_tensor(r, r, box(ap[:, i % 3, :]), ALU.add)
                    if i + 1 < len(POOL_TAPS):
                        last.then_inc(pstep, 1)
                        done += 1
                last.then_inc(wp_ok, 1)
                assert done == PER, (done, PER)

        @block.tensor
        def _(pe):
            with pe.Fori(0, B * HH) as n:
                pe.wait_ge(acc_free, n + 1)
                out = acc[:, n % 2, 0:C]
                for s in range(CW):
                    pe.wait_ge(prod_ok, n * CW + (s + 1))
                    for i in range(CW):
                        mm = pe.matmul(out, ident[0:TP, 0:TP], prod[:, (n + s) % NPROD, i * C:(i + 1) * C],
                                       start=(s == 0 and i == 0), stop=(s == CW - 1 and i == CW - 1))
                    mm.then_inc(prod_used, 1)
                    if s == 0:
                        hold(pe, yp_in, 16 * n + 16, own)
                        pe.matmul(out, ident[0:TP, 0:TP], yprev[:, n % NOM, :], start=False, stop=False)

        @block.vector
        def _(dve):
            cnt = [0]

            def do(ins_):
                cnt[0] += 1
                ins_.then_inc(vt["sem"], 1)
                dve.wait_ge(vt["sem"], cnt[0])

            for xy in range(2):
                do(nc.vector.tensor_scalar(negr[:, xy, :], k["steps"][:, :], cur[:, xy:xy + 1], -1.0, ALU.add,
                                           ALU.mult))
            for pos, c0, lim, v in ((k["xpos"], 0, W, vt["x"]), (k["ypos"], 1, H, vt["y"])):
                do(nc.vector.tensor_scalar(v[:, 0, :], pos[:, :], cur[:, c0:c0 + 1], None, ALU.add))
                do(nc.vector.tensor_scalar(v[:, 1, :], v[:, 0, :], -0.5, None, ALU.is_gt))
                do(nc.vector.tensor_scalar(v[:, 0, :], v[:, 0, :], lim - 0.5, None, ALU.is_lt))
                do(nc.vector.tensor_tensor(v[:, 0, :], v[:, 0, :], v[:, 1, :], ALU.mult))
            do(nc.vector.memset(zeros[:, :], 0.0))
            dve.sem_inc(applied, 2)
            dve.sem_inc(w_done, 2)
            dve.sem_inc(prod_used, NPROD)
            dve.sem_inc(acc_free, 2)
            dve.sem_inc(y_st, 1)
            nc.vector.tensor_tensor(mask[:, :, :], spread(vt["y"][:, 0, :], 2, CW), spread(vt["x"][:, 0, :], 1, ROWS),
                                    ALU.mult).then_inc(setup, 2)

            PER = 2 * len(DVE_TAPS) - 1

            def multiply(n, i):
                hx, hm = hat[:, n % 2, 0, :, :], hym[:, n % 2, :, :]
                dst = region(wd[:, n % 2, :], DVE_TAPS[0]) if i == 0 else box(ad[:, i % 3, :])
                o, a, c = outer(dst, hx, hm, DVE_TAPS[i])
                nc.vector.tensor_tensor(o, a, c, ALU.mult).then_inc(dstep, 1)

            def add(n, i, ready):
                dve.wait_ge(dstep, n * PER + ready)
                r = region(wd[:, n % 2, :], DVE_TAPS[i])
                nc.vector.tensor_tensor(r, r, box(ad[:, i % 3, :]), ALU.add).then_inc(dstep, 1)

            def begin(n):
                hold(dve, hym_ok, n + 1, own)
                hold(dve, blank, n + 1, own)
                multiply(n, 0)

            def end(n):
                hold(dve, dstep, n * PER + PER, own)
                hold(dve, wp_ok, n + 1, own)
                low = wd[:, n % 2, LOW * CW * G:]
                nc.vector.tensor_tensor(low, low, wp[:, n % 2, LOW * CW * G:], ALU.add).then_inc(w_done, 1)

            steps = [begin, lambda n: multiply(n, 1), lambda n: multiply(n, 2), lambda n: add(n, 1, 2),
                     lambda n: multiply(n, 3), lambda n: add(n, 2, 4), lambda n: add(n, 3, 6), end]
            assert len(DVE_TAPS) == 4 and len(steps) == CW - 1

            def apply(n, j, b, next_tile):
                hold(dve, masked, j + (CW + b * ROWS), own)
                hold(dve, w_done, n + 3, own)
                for s in range(CW):
                    dve.wait_ge(prod_used, n * CW + (s + 1))
                    slot = (j + (s + b * ROWS)) % RING
                    nc.vector.tensor_tensor(
                        prod[:, (n + s) % NPROD, :].rearrange("p (a c) -> p a c", c=GC),
                        ring[:, slot, :].rearrange("p (a c) -> p a c", c=GC),
                        spread(wd[:, n % 2, s * CW * G:(s + 1) * CW * G], 2, GC), ALU.mult).then_inc(prod_ok, 1)
                    if next_tile and s >= 1:
                        steps[s - 1](n + 1)
                dve.wait_ge(prod_ok, n * CW + CW)
                dve.sem_inc(tile_done, 1)
                dve.sem_inc(applied, 1)

            for step in steps:
                step(0)
            for b in range(B):
                with dve.Fori(0, HH if b + 1 < B else HH - 1) as j:
                    apply(j + b * HH, j, b, True)
            apply(B * HH - 1, HH - 1, B - 1, False)


def deformable_stage(nc, k, xp_d, om_d, y_d, base, counts):
    with ExitStack() as es:
        t = Ctx(nc, es, "deform")
        names = ("setup om_loaded yprev_loaded row_loaded row_masked abs_ready hats_ready grids_blank "
                 "hym_ready pool_step pool_weights_ready weights_done dve_step prod_ready prod_used "
                 "acc_free y_ready y_stored tile_done applied win_step").split()
        sems = [t.sem(s) for s in names]
        NW = CW * CW * G
        cur = t.sb("cur", [TP, 2])
        vt = {"x": t.sb("vx", [TP, 2, CW]), "y": t.sb("vy", [TP, 2, ROWS]), "sem": sems[-1]}
        zeros = t.sb("zeros", [TP, (CW - R) * CW * G])
        bufs = (t.sb("om", [TP, NOM, OM]), t.sb("ab", [TP, 2, 2, R, GK]), t.sb("hat", [TP, 2, 2, R, GK]),
                t.sb("hym", [TP, 2, R, GK]), t.sb("wd", [TP, 2, NW]), t.sb("wp", [TP, 2, NW]),
                t.sb("ad", [TP, 3, R * R * G]), t.sb("ap", [TP, 3, R * R * G]), t.sb("prod", [TP, NPROD, CW * C]),
                t.sb("ring", [TP, RING, CW * C]), t.sb("yprev", [TP, NOM, C]), t.sb("yout", [TP, 2, C]),
                t.sb("mask", [TP, ROWS, CW]), t.sb("negr", [TP, 2, R]), zeros, cur, vt)
        acc = t.ps("acc", [TP, 2, 512])

        def move(body):
            with nc.Block() as block:
                @block.vector
                def _(dve):
                    body(dve)

        def restart(dve):
            nc.vector.tensor_copy(cur[:, :], base[:, :])
        def restart_x(dve):
            nc.vector.tensor_copy(cur[:, 0:1], base[:, 0:1])

        move(restart)
        why = "a count of windows and a whole offset, bounded by the clamp of the offsets"
        lim = int(OFFMAX)
        nx, ny = (nc.values_load(counts[0:1, i:i + 1], min_val=1, max_val=(2 * lim + 2) // R + 1,
                                 skip_runtime_bounds_check_because=why) for i in range(2))
        x0, y0 = (nc.values_load(counts[0:1, i:i + 1], min_val=-lim, max_val=lim,
                                 skip_runtime_bounds_check_because=why) for i in (2, 3))
        with nc.Fori(0, ny) as iy:
            with nc.Fori(0, nx) as ix:
                window_pass(nc, k, {"acc": acc}, bufs, sems[:-1], xp_d, om_d, y_d, 
                            (y0 + iy * R).with_bounds(min_val=-lim, max_val=lim + 1),
                            (x0 + ix * R).with_bounds(min_val=-lim, max_val=lim + 1))
                for s in sems + [k["own"]]:
                    nc.gpsimd.sem_clear(s)
                nc.all_engine_barrier()
                move(lambda dve: nc.vector.tensor_scalar(cur[:, 0:1], cur[:, 0:1], float(R), None, ALU.add))
            move(lambda dve: nc.vector.tensor_scalar(cur[:, 1:2], cur[:, 1:2], float(R), None, ALU.add))
            move(restart_x)


def rows_stage(nc, k, x, y_d, t_d, xc_d):
    own, ident = k["own"], k["ident"]
    with ExitStack() as es:
        t = Ctx(nc, es, "rows")
        y = t.sb("y", [TP, 2, QT, C])
        xr = t.sb("x", [TP, 2, QT, C])
        turned = t.sb("turned", [C, 2, QT * TP])
        x2t = t.sb("x2t", [C, 2, QT * TP])
        hid = t.sb("hid", [C, 2, QT * TP])
        z = t.sb("z", [TP, 2, QT, C])
        z2 = t.sb("z2", [TP, 2, QT, C])
        x2 = t.sb("x2", [TP, 2, QT, C])
        x2b = t.sb("x2b", [TP, 2, QT, C])
        tok = t.sb("tok", [TP, 2, QT, C])
        xc = t.sb("xc", [TP, 2, QT, C])
        st = t.sb("st", [TP, 2, QT, 6])
        mv = t.sb("mv", [TP, 2, 3, QT, 2])
        ve = t.sb("ve", [TP, 2, 3, QT])
        rs = t.sb("rs", [TP, 2, 3, QT])
        half = t.sb("half", [TP, QT])
        gg = [t.sb(f"gg{i}", [TP, C]) for i in range(2)]
        gb = [t.sb(f"gb{i}", [TP, C]) for i in range(2)]
        ps_t = [t.ps(f"ps_t{i}", [C, 512]) for i in range(2)]
        ps_o = [t.ps(f"ps_o{i}", [TP, 512]) for i in range(2)]
        ps_f = [t.ps(f"ps_f{i}", [C, 512]) for i in range(2)]
        ps_m = [t.ps(f"ps_m{i}", [TP, 512]) for i in range(2)]
        y_in, x_in, tok_st, xc_st = ([t.sem(f"{s}{p}") for p in range(2)] for s in (
            "y_loaded", "x_loaded", "tokens_stored", "xc_stored"))
        (yT, yT_ok, o_ps, dstep, agg, eps, rstd, x2_ok, x2T, x2T_ok, f_ps, hid_ok, m_ps, xb_ok, x2b_ok,
         tok_ok, xc_ok, cst, half_ok) = [t.sem(s) for s in (
             "yT_in_psum yT_ready o_in_psum dve_step mean_var_ready var_eps_ready rstd_ready "
             "x2_ready x2T_in_psum x2T_ready f_in_psum hid_ready m_in_psum x_plus_bias_ready x2_plus_bias_ready "
             "tokens_ready xc_ready constants_ready half_ready").split()]

        with nc.Block() as block:

            @block.sync
            def _(sp):
                with sp.Fori(0, NB // 2) as i:
                    for p in range(2):
                        n = i * 2 + p
                        hold(sp, tok_ok, n + 1, own)
                        sp.dma_start(y[:, p, :, :], y_d[bass.ds(n * QT, QT), :, :].rearrange("t p c -> p t c"))\
                            .then_inc(y_in[p], 16)
                        for h in range(2):
                            src = bass.AP(x.tensor, ((n // NQ) * NPIX + (n % NQ) * (QT * W) + h * HH * W) * C,
                                          [[C, W], [W * C, QT], [1, C]])
                            sp.dma_start(xr[h * W:(h + 1) * W, p, :, :], src).then_inc(x_in[p], 16)

            @block.gpsimd
            def _(pool):
                pool.memset(half[:, :], -0.5).then_inc(half_ok, 1)
                pool.wait_ge(half_ok, 1)
                pool.wait_ge(cst, 2)

                with pool.Fori(0, NB // 2) as i:
                    for s in range(3):
                        for p in range(2):
                            m = i * 6 + 2 * s + p
                            hold(pool, agg, m + 1, own)
                            pool.tensor_scalar(ve[:, p, s, :], mv[:, p, s, :, 1], EPS, None, ALU.add).then_inc(eps, 1)
                            hold(pool, eps, m + 1, own)
                            pool.tensor_tensor(rs[:, p, s, :], ve[:, p, s, :], half[:, :], ALU.pow).then_inc(rstd, 1)
                        for p in range(2):
                            if s == 0:
                                hold(pool, x_in[p], i * 32 + 32, own)
                                pool.tensor_tensor(xr[:, p, :, :], xr[:, p, :, :], spread(gb[0][:, :], 1, QT),
                                                   ALU.add).then_inc(xb_ok, 1)
                            if s == 1:
                                hold(pool, x2_ok, i * 2 + p + 1, own)
                                pool.tensor_tensor(x2b[:, p, :, :], x2[:, p, :, :], spread(gb[1][:, :], 1, QT),
                                                   ALU.add).then_inc(x2b_ok, 1)

            @block.tensor
            def _(pe):
                with pe.Fori(0, NB // 2) as i:
                    for p in range(2):
                        hold(pe, y_in[p], i * 16 + 16, own)
                        hold(pe, x2T_ok, i * 2 + p + 1, own)
                        for q in range(QT):
                            mm = pe.transpose(ps_t[p][:, q * TP:(q + 1) * TP], y[:, p, q, :], ident[0:TP, 0:TP])
                        mm.then_inc(yT, 1)
                    for p in range(2):
                        hold(pe, yT_ok, i * 2 + p + 1, own)
                        for q in range(QT):
                            mm = pe.matmul(ps_o[p][:, q * C:(q + 1) * C], turned[:, p, q * TP:(q + 1) * TP],
                                           k["w_out"][:, :], start=True, stop=True)
                        mm.then_inc(o_ps, 1)
                    for p in range(2):
                        hold(pe, x2_ok, i * 2 + p + 1, own)
                        for q in range(QT):
                            mm = pe.transpose(ps_t[p][:, q * TP:(q + 1) * TP], x2[:, p, q, :], ident[0:TP, 0:TP])
                        mm.then_inc(x2T, 1)
                    for p in range(2):
                        hold(pe, x2T_ok, i * 2 + p + 3, own)
                        pe.matmul(ps_f[p][:, 0:QT * TP], k["w_fc1"][:, :], x2t[:, p, :], start=True, stop=True)\
                            .then_inc(f_ps, 1)
                    for p in range(2):
                        hold(pe, hid_ok, i * 2 + p + 1, own)
                        for q in range(QT):
                            mm = pe.matmul(ps_m[p][:, q * C:(q + 1) * C], hid[:, p, q * TP:(q + 1) * TP],
                                           k["w_fc2"][:, :], start=True, stop=True)
                        mm.then_inc(m_ps, 1)

            @block.scalar
            def _(act):
                act.sem_inc(x2T_ok, 2)
                with act.Fori(0, NB // 2) as i:
                    for p in range(2):
                        hold(act, yT, i * 2 + p + 1, own)
                        nc.scalar.activation(turned[:, p, :], ps_t[p][:, 0:QT * TP], ACT.Copy).then_inc(yT_ok, 1)
                    for p in range(2):
                        hold(act, x2T, i * 2 + p + 1, own)
                        nc.scalar.activation(x2t[:, p, :], ps_t[p][:, 0:QT * TP], ACT.Copy).then_inc(x2T_ok, 1)
                    for p in range(2):
                        hold(act, f_ps, i * 2 + p + 1, own)
                        nc.scalar.activation(hid[:, p, :], ps_f[p][:, 0:QT * TP], ACT.Gelu,
                                             bias=k["b_fc1"][:, 0:1], scale=1.0).then_inc(hid_ok, 1)
                    for p in range(2):
                        n = i * 2 + p
                        hold(act, tok_ok, n + 3, own)
                        act.dma_start(t_d[bass.ds(n * QT, QT), :, :].rearrange("t p c -> p t c"), tok[:, p, :, :])\
                            .then_inc(tok_st[p], 16)
                        hold(act, xc_ok, n + 1, own)
                        act.dma_start(xc_d[bass.ds(n * QT, QT), :, :].rearrange("t p c -> p t c"), xc[:, p, :, :])\
                            .then_inc(xc_st[p], 16)
                for p in range(2):
                    act.wait_ge(tok_st[p], 8 * NB + 1)
                    act.wait_ge(xc_st[p], 8 * NB + 1)

            @block.vector
            def _(dve):
                dve.sem_inc(tok_ok, 2)
                for s in (*tok_st, *xc_st):
                    dve.sem_inc(s, 1)
                for s, (gm, g, b_) in enumerate((("gamma1", "ln1_g", "ln1_b"), ("gamma2", "ln2_g", "ln2_b"))):
                    nc.vector.tensor_tensor(gg[s][:, :], k[gm][0:TP, :], k[g][0:TP, :], ALU.mult)
                    nc.vector.tensor_tensor(gb[s][:, :], k[gm][0:TP, :], k[b_][0:TP, :], ALU.mult).then_inc(cst, 1)
                dve.wait_ge(cst, 2)
                PER = 2 * (2 * 4 + 1)

                with dve.Fori(0, NB // 2) as i:
                    cnt = [0]

                    def do(ins_):
                        ins_.then_inc(dstep, 1)
                        cnt[0] += 1
                        return cnt[0]

                    def wait(c):
                        hold(dve, dstep, i * PER + c, own)

                    def stats(s, p, src):
                        for q in range(QT):
                            last = nc.vector.bn_stats(st[:, p, q, :], src[:, p, q, :])
                        wait(do(last))
                        for q in range(QT):
                            last = nc.vector.bn_aggr(mv[:, p, s, q, :], st[:, p, q, :])
                        last.then_inc(agg, 1)

                    def normalise(s, p, dst, src):
                        hold(dve, rstd, i * 6 + 2 * s + p + 1, own)
                        for q in range(QT):
                            last = nc.vector.tensor_scalar(dst[:, p, q, :], src[:, p, q, :], mv[:, p, s, q, 0:1],
                                                           rs[:, p, s, q:q + 1], ALU.subtract, ALU.mult)
                        return last

                    for s, (ps, bias, ready) in enumerate(((ps_o, "b_out", o_ps), (ps_m, "b_fc2", m_ps))):
                        seen = []
                        for p in range(2):
                            hold(dve, ready, i * 2 + p + 1, own)
                            seen.append(do(nc.vector.tensor_tensor(
                                z[:, p, :, :], ps[p][:, :].rearrange("p (t c) -> p t c", c=C),
                                spread(k[bias][0:TP, :], 1, QT), ALU.add)))
                        for p in range(2):
                            wait(seen[p])
                            stats(s, p, z)
                        seen = [do(normalise(s, p, z2, z)) for p in range(2)]
                        for p in range(2):
                            wait(seen[p])
                            seen[p] = do(nc.vector.tensor_tensor(z2[:, p, :, :], z2[:, p, :, :],
                                                                 spread(gg[s][:, :], 1, QT), ALU.mult))
                        for p in range(2):
                            wait(seen[p])
                            if s == 0:
                                hold(dve, xb_ok, i * 2 + p + 1, own)
                                nc.vector.tensor_tensor(x2[:, p, :, :], z2[:, p, :, :], xr[:, p, :, :], ALU.add)\
                                    .then_inc(x2_ok, 1)
                            else:
                                hold(dve, x2b_ok, i * 2 + p + 1, own)
                                hold(dve, tok_st[p], i * 16 + 1, own)
                                nc.vector.tensor_tensor(tok[:, p, :, :], z2[:, p, :, :], x2b[:, p, :, :], ALU.add)\
                                    .then_inc(tok_ok, 1)
                    for p in range(2):
                        hold(dve, tok_ok, i * 2 + p + 3, own)
                        stats(2, p, tok)
                    for p in range(2):
                        hold(dve, xc_st[p], i * 16 + 1, own)
                        normalise(2, p, xc, tok).then_inc(xc_ok, 1)
                    assert cnt[0] == PER, cnt


C4 = C // 4
NCH = 4
CK = NPIX // NCH
MT = CK // TP
ST = 4
NS = HH // ST
BK = CK // 2
NMG = NPIX // BK
EPS_SUM = 1e-6
NE = 3
BF16 = mybir.dt.bfloat16
NEXT_QUERY = 0
BN_EPS = 1e-5


def attention_stage(nc, k, ins, xc_d, t_d, t4_d):
    own, ident = k["own"], k["ident"]
    with ExitStack() as es:
        t = Ctx(nc, es, "attn")
        wraw = t.sb("wraw", [128, C])
        wq, wk = (t.sb(w, [C, 4, C4]) for w in ("wq", "wk"))
        ones = t.sb("ones", [TP, C])
        wt = t.sb("wt", [C, C])
        wtt = t.sb("wtt", [C, C])
        bn = t.sb("bn", [C, 5])
        bs = t.sb("bs", [C, 2])
        bneg = t.sb("bneg", [C, 1])
        xa = t.sb("xa", [TP, HH, C])
        xct = t.sb("xct", [C, NPIX])
        ka, kb = t.sb("ka", [4 * C4, NPIX], BF16), t.sb("kb", [2 * C4, NPIX], BF16)
        qa, qb = t.sb("qa", [4 * C4, 2, ST * TP], BF16), t.sb("qb", [2 * C4, 2, ST * TP], BF16)
        k_mid, q_mid = t.sb("k_mid", [4 * C4, 2, QT * TP], BF16), t.sb("q_mid", [4 * C4, ST * TP], BF16)
        q_rest = t.sb("q_rest", [4 * C4, ST * TP])
        prob = t.sb("prob", [TP, 2, ST, NPIX])
        xs = t.sb("xs", [TP, 2, ST, NCH, C])
        xr = t.sb("xr", [C, NPIX])
        cs = t.sb("cs", [TP, NPIX])
        nm = t.sb("nm", [TP, 2, ST, NCH])
        zs = t.sb("zs", [TP, 2, ST, NCH])
        wz = t.sb("wz", [TP, 2, ST, NCH])
        ez = t.sb("ez", [TP, 2, ST, NCH])
        dm = t.sb("dm", [TP, 2, ST, NCH])
        mn = t.sb("mn", [TP, 2, ST])
        zt = t.sb("zt", [TP, 2, ST])
        zr = t.sb("zr", [TP, 2, ST])
        rc = t.sb("rc", [C, 2, QT * TP])
        k_rest = rc
        un = t.sb("un", [C, 2, QT * TP])
        tin = t.sb("tin", [TP, 2, QT, C])
        tout = t.sb("tout", [TP, 2, QT, C])
        ps_e = [t.ps(f"ps_e{i}", [C, 2, 512]) for i in range(NE)]
        ps_r = [t.ps(f"ps_r{i}", [C, 512]) for i in range(2)]
        (w_in, xa_in, wT, w_ok, bstep, bn_done, xT, xT_ok, k_ps, k_hi, k_ok, k_step, k_low, q_ps, q_hi, q_left,
         q_step, qs_ok, e_ps, mx_ok, ex_ok, sstep, dm_ok,
         ez_ok, w_rdy, xs_ok, r_ps, r_ok, zeroed, cstep, c_ps, c_ok, pstep, d_ok, u_ps, u_ok, uT, tin_ok, t_ok,
         image_done, const_ok) = [
             t.sem(s) for s in (
                 "weights_loaded xa_loaded weights_turned weights_ready bn_step bn_done xT_in_psum xT_ready "
                 "keys_in_psum keys_rounded keys_rest_ready keys_step keys_ready query_in_psum query_rounded "
                 "query_rest_ready query_step query_ready energy_in_psum max_ready exp_ready soft_step "
                 "below_ready rescale_ready chunk_weights_ready xs_ready sums_in_psum sums_added sums_zeroed "
                 "column_step columns_in_psum columns_used post_step d_ready u_in_psum u_ready uT_in_psum "
                 "residual_ready tokens_ready image_done constants_ready")
             .split()]
        t_in, t_st = ([t.sem(f"{s}{p}") for p in range(2)] for s in ("t_loaded", "t_stored"))

        def uses(p, b, g):
            return b * ((NQ + 1 - p) // 2) + g // 2

        def steps():
            order = [(j / 16.0, 0, j) for j in range(ST * NCH)] + \
                    [(0.28 + 0.72 * g / NMG, 1, g) for g in range(NMG)]
            return [(kind, j) for _, kind, j in sorted(order)]

        ENERGY, SUMS = 0, 1

        def superblocks(eng, b, part):
            part(0, 0, None, None)
            with eng.Fori(0, NS // 2) as i:
                part(i * 2 + 1, 1, i * 2, 0)
                part(i * 2 + 2, 0, i * 2 + 1, 1)
            part(None, None, NS - 1, 0)

        def energies(e, j):
            return ps_e[(j + e) % NE]

        def overall(b, s):
            return None if s is None else s + b * NS

        def interleaved(s_e, s_r):
            return [(kind, j) for kind, j in steps()
                    if (kind == ENERGY and s_e is not None) or (kind == SUMS and s_r is not None)]

        with nc.Block() as block:

            @block.sync
            def _(sp):
                sp.dma_start(wraw[0:C4, :], ins["L1_attn_Wq"]).then_inc(w_in, 16)
                sp.dma_start(wraw[C4:2 * C4, :], ins["L1_attn_Wk"]).then_inc(w_in, 16)
                for i, name in enumerate(("gamma", "beta", "bn_mean", "bn_var", "bt")):
                    sp.dma_start(bn[:, i:i + 1], col(ins["L1_attn_" + name])).then_inc(w_in, 16)
                sp.dma_start(wt[:, :], ins["L1_attn_Wt"]).then_inc(w_in, 16)
                with sp.Fori(0, B) as b:
                    hold(sp, image_done, b + 1, own)
                    sp.dma_start(xa[:, :, :], xc_d[bass.ds(b * HH, HH), :, :].rearrange("t p c -> p t c"))\
                        .then_inc(xa_in, 16)
                    for g in range(NQ):
                        n = b * NQ + g
                        hold(sp, t_ok, n + (2 if g == 0 else 1), own)
                        sp.dma_start(tin[:, g % 2, :, :], t_d[bass.ds(n * QT, QT), :, :].rearrange("t p c -> p t c"))\
                            .then_inc(t_in[g % 2], 16)

            @block.gpsimd
            def _(pool):
                pool.memset(bneg[:, :], -0.5).then_inc(const_ok, 1)
                pool.memset(ones[:, :], 1.0).then_inc(const_ok, 1)
                pool.wait_ge(w_in, 128)
                pool.wait_ge(const_ok, 2)
                pool.tensor_scalar(bs[:, 0:1], bn[:, 3:4], BN_EPS, None, ALU.add).then_inc(bstep, 1)
                pool.wait_ge(bstep, 1)
                pool.tensor_tensor(bs[:, 0:1], bs[:, 0:1], bneg[:, :], ALU.pow).then_inc(bstep, 1)
                with pool.Fori(0, B) as b:
                    hold(pool, image_done, b + 1, own)
                    pool.memset(xr[:, :], 0.0)
                    pool.memset(cs[:, :], 0.0).then_inc(zeroed, 1)
                    hold(pool, xa_in, b * 16 + 16, own)

                    def part(s_e, e, s_r, r):
                        if s_r is not None:
                            hold(pool, w_rdy, overall(b, s_r) + 1, own)
                            for i in range(ST):
                                tile = s_r * ST + i
                                last = pool.tensor_tensor(xs[:, r, i, :, :], spread(xa[:, tile, :], 1, NCH),
                                                          spread(wz[:, r, i, :], 2, C), ALU.mult)
                            last.then_inc(xs_ok, 1)

                    superblocks(pool, b, part)
                    for g in range(NQ):
                        hold(pool, t_in[g % 2], uses(g % 2, b, g) * 16 + 16, own)
                        pool.tensor_tensor(tin[:, g % 2, :, :], tin[:, g % 2, :, :], xa[:, g * QT:(g + 1) * QT, :],
                                           ALU.add).then_inc(tin_ok, 1)

            @block.tensor
            def _(pe):
                pe.wait_ge(w_in, 128)
                pe.transpose(ps_e[0][:, 0, 0:2 * C4], wraw[0:2 * C4, :], ident[0:2 * C4, 0:2 * C4]).then_inc(wT, 1)
                pe.transpose(ps_e[1][:, 0, 0:C], wt[:, :], ident[:, :]).then_inc(wT, 1)
                pe.wait_ge(w_ok, 1)
                pe.wait_ge(const_ok, 2)
                with pe.Fori(0, B) as b:
                    hold(pe, xa_in, b * 16 + 16, own)
                    hold(pe, t_ok, b * NQ + 2, own)

                    def turn_x(g):
                        hold(pe, xT_ok, b * NQ + g + 1, own)
                        for i in range(QT):
                            mm = pe.transpose(ps_r[g % 2][:, i * TP:(i + 1) * TP], xa[:, g * QT + i, :],
                                              ident[0:TP, 0:TP])
                        mm.then_inc(xT, 1)

                    def keys(g):
                        hold(pe, xT_ok, b * NQ + g + 3, own)
                        hold(pe, k_ok, b * NQ + g + 1, own)
                        pe.matmul(ps_e[g % 2][:, 0, 0:QT * TP], wk[:, :, :].rearrange("c a n -> c (a n)"),
                                  xct[:, g * QT * TP:(g + 1) * QT * TP], start=True, stop=True).then_inc(k_ps, 1)

                    def query(s):
                        pe.matmul(ps_r[1][:, 0:ST * TP], wq[:, :, :].rearrange("c a n -> c (a n)"),
                                  xct[:, bass.ds((s % NS) * (ST * TP), ST * TP)], start=True, stop=True)\
                            .then_inc(q_ps, 1)

                    turn_x(0)
                    for g in range(NQ):
                        if g + 1 < NQ:
                            turn_x(g + 1)
                        keys(g)
                    hold(pe, k_ok, b * NQ + NQ + 2, own)
                    query(0)
                    hold(pe, k_low, b * NQ + NQ + 2, own)
                    hold(pe, k_step, (b + 1) * (2 * NQ), own)

                    def part(s_e, e, s_r, r):
                        if s_e is not None:
                            hold(pe, qs_ok, b * (NS + 1) + (s_e + 2), own)
                        s_n = s_e
                        s_e, s_r = overall(b, s_e), overall(b, s_r)
                        for kind, j in interleaved(s_e, s_r):
                            if kind == ENERGY:
                                i, ch = j // NCH, j % NCH
                                pe.wait_ge(ex_ok, s_e * (ST * NCH) + (j + 1 + (e == 0 and j < 2)))
                                q_ = slice(i * TP, (i + 1) * TP)
                                for qp, kp in ((qa, ka), (qb, kb)):
                                    for hf in range(2):
                                        m0 = ch * CK + hf * BK
                                        mm = pe.matmul(energies(e, j)[0:TP, hf, 0:BK], qp[:, e, q_], kp[:, m0:m0 + BK],
                                                       start=qp is qa, stop=qp is qb)
                                mm.then_inc(e_ps, 1)
                                if j == NEXT_QUERY:
                                    if s_r is not None:
                                        hold(pe, r_ok, s_r * NMG + 2, own)
                                    query(s_n + 1)
                            else:
                                if j == 0:
                                    hold(pe, xs_ok, s_r + 1, own)
                                if j == 1 and s_n is not None:
                                    hold(pe, q_left, b * (NS + 1) + (s_n + 2), own)
                                hold(pe, r_ok, s_r * NMG + (j + 1), own)
                                for i in range(ST):
                                    mm = pe.matmul(ps_r[j % 2][:, 0:BK], xs[:, r, i, j // 2, :],
                                                   prob[:, r, i, j * BK:(j + 1) * BK], start=(i == 0),
                                                   stop=(i == ST - 1))
                                mm.then_inc(r_ps, 1)

                    superblocks(pe, b, part)

                    def columns(g):
                        hold(pe, c_ok, b * NQ + g + 1, own)
                        pe.matmul(ps_e[2][:, g % 2, 0:QT * TP], ones[:, :], cs[:, g * QT * TP:(g + 1) * QT * TP],
                                  start=True, stop=True).then_inc(c_ps, 1)

                    def project(g):
                        hold(pe, d_ok, b * NQ + g + 1, own)
                        hold(pe, u_ok, b * NQ + g + 1, own)
                        pe.matmul(ps_e[g % 2][:, 0, 0:QT * TP], wtt[:, :], xr[:, g * QT * TP:(g + 1) * QT * TP],
                                  start=True, stop=True).then_inc(u_ps, 1)

                    def turn(g):
                        hold(pe, u_ok, b * NQ + g + 3, own)
                        hold(pe, t_ok, b * NQ + g + 1, own)
                        for i in range(QT):
                            mm = pe.transpose(ps_r[g % 2][0:TP, i * C:(i + 1) * C], un[:, g % 2, i * TP:(i + 1) * TP],
                                              ident[:, :])
                        mm.then_inc(uT, 1)

                    hold(pe, qs_ok, b * (NS + 1) + (NS + 2), own)
                    hold(pe, cstep, (b + 1) * (NS * ST * NCH) + 1, own)
                    hold(pe, r_ok, (b + 1) * (NS * NMG) + 2, own)
                    hold(pe, ex_ok, (b + 1) * (NS * ST * NCH) + NE, own)
                    columns(0)
                    columns(1)
                    for g in range(NQ):
                        project(g)
                        if g + 2 < NQ:
                            columns(g + 2)
                        if g:
                            turn(g - 1)
                    turn(NQ - 1)

            @block.scalar
            def _(act):
                act.sem_inc(xT_ok, 2)
                act.sem_inc(u_ok, 2)
                act.sem_inc(ex_ok, NE)
                act.wait_ge(wT, 2)
                for i, w in enumerate((wq, wk)):
                    nc.scalar.activation(w[:, :, :], spread(ps_e[0][:, 0, i * C4:(i + 1) * C4], 1, 4), ACT.Copy)
                nc.scalar.activation(wtt[:, :], ps_e[1][:, 0, 0:C], ACT.Copy).then_inc(w_ok, 1)
                act.wait_ge(bn_done, 1)
                with act.Fori(0, B) as b:
                    def keys_mid(g):
                        hold(act, k_ok, b * NQ + g + 3, own)
                        for blk in (1, 3):
                            rows = slice(blk * C4, (blk + 1) * C4)
                            last = nc.scalar.activation(ka[rows, g * QT * TP:(g + 1) * QT * TP],
                                                        k_rest[rows, g % 2, :], ACT.Copy)
                        last.then_inc(k_low, 1)

                    def query_mid(s, slot):
                        hold(act, q_left, b * (NS + 1) + (s + 1), own)
                        lo, mid = slice(C4, 2 * C4), slice(2 * C4, 4 * C4)
                        nc.scalar.activation(q_mid[lo, :], q_rest[lo, :], ACT.Copy)
                        nc.scalar.activation(qa[mid, slot, :], q_rest[mid, :], ACT.Copy).then_inc(q_step, 1)

                    def keys(g):
                        hold(act, k_ps, b * NQ + g + 1, own)
                        cols = slice(g * QT * TP, (g + 1) * QT * TP)
                        nc.scalar.activation(kb[C4:2 * C4, cols], ps_e[g % 2][C4:2 * C4, 0, 0:QT * TP], ACT.Copy)
                        nc.scalar.activation(ka[:, cols], ps_e[g % 2][:, 0, 0:QT * TP], ACT.Copy).then_inc(k_hi, 1)

                    for g in range(NQ):
                        n = b * NQ + g
                        hold(act, xT, n + 1, own)
                        nc.scalar.activation(xct[:, g * QT * TP:(g + 1) * QT * TP], ps_r[g % 2][:, 0:QT * TP], ACT.Copy)\
                            .then_inc(xT_ok, 1)
                        if g >= 1:
                            keys(g - 1)
                        if g >= 2:
                            keys_mid(g - 2)
                    keys(NQ - 1)
                    keys_mid(NQ - 2)
                    keys_mid(NQ - 1)

                    def query(s, slot):
                        hold(act, q_ps, b * (NS + 1) + (s + 1), own)
                        nc.scalar.activation(qb[0:C4, slot, :], ps_r[1][0:C4, 0:ST * TP], ACT.Copy)
                        nc.scalar.activation(qa[:, slot, :], ps_r[1][:, 0:ST * TP], ACT.Copy).then_inc(q_hi, 1)

                    query(0, 0)
                    query_mid(0, 0)

                    def rescale(S, slot):
                        hold(act, dm_ok, S + 1, own)
                        nc.scalar.activation(ez[:, slot, :, :], dm[:, slot, :, :], ACT.Exp).then_inc(ez_ok, 1)

                    def part(s_e, e, s_r, r):
                        s_n = s_e
                        s_e, s_r = overall(b, s_e), overall(b, s_r)
                        if s_r is not None:
                            rescale(s_r, r)
                        if s_e is None:
                            return
                        if s_r is not None:
                            hold(act, r_ps, s_r * NMG + 1, own)
                            hold(act, cstep, s_r * (ST * NCH) + 1, own)
                        for j in range(ST * NCH):
                            i, ch = j // NCH, j % NCH
                            act.wait_ge(mx_ok, s_e * (ST * NCH) + (j + 1))
                            nc.scalar.activation(prob[:, e, i, ch * CK:(ch + 1) * CK]
                                                 .rearrange("p (a f) -> p a f", a=2), energies(e, j)[0:TP, :, 0:BK],
                                                 ACT.Exp, bias=nm[:, e, i, ch:ch + 1], scale=1.0,
                                                 accum_out=zs[:, e, i, ch:ch + 1]).then_inc(ex_ok, 1)
                            if j == NEXT_QUERY + 1:
                                query(s_n + 1, 1 - e)
                            elif j == NEXT_QUERY + 3:
                                query_mid(s_n + 1, 1 - e)

                    superblocks(act, b, part)

                    def store(g):
                        n = b * NQ + g
                        hold(act, t_ok, n + 3, own)
                        for h in range(2):
                            dst = bass.AP(t4_d.tensor, (b * NPIX + (g * QT * W + h * HH * W)) * C,
                                          [[C, W], [W * C, QT], [1, C]])
                            act.dma_start(dst, tout[h * W:(h + 1) * W, g % 2, :, :]).then_inc(t_st[g % 2], 16)

                    for g in range(NQ):
                        n = b * NQ + g
                        hold(act, u_ps, n + 1, own)
                        nc.scalar.activation(un[:, g % 2, :], ps_e[g % 2][:, 0, 0:QT * TP], ACT.Relu, bias=bs[:, 1:2],
                                             scale=bs[:, 0:1]).then_inc(u_ok, 1)
                        if g >= 2:
                            store(g - 2)
                    store(NQ - 2)
                    store(NQ - 1)
                for p in range(2):
                    act.wait_ge(t_st[p], 32 * B * ((NQ + 1 - p) // 2) + 1)

            @block.vector
            def _(dve):
                dve.sem_inc(image_done, 1)
                dve.sem_inc(k_ok, 2)
                dve.sem_inc(k_low, 2)
                dve.sem_inc(qs_ok, 1)
                dve.sem_inc(c_ok, 2)
                dve.sem_inc(r_ok, 2)
                dve.sem_inc(t_ok, 2)
                for s in (r_ps, cstep, *t_st):
                    dve.sem_inc(s, 1)
                dve.wait_ge(bstep, 2)
                nc.vector.tensor_tensor(bs[:, 0:1], bs[:, 0:1], bn[:, 0:1], ALU.mult).then_inc(bstep, 1)
                nc.vector.tensor_tensor(bs[:, 1:2], bn[:, 4:5], bn[:, 2:3], ALU.subtract).then_inc(bstep, 1)
                dve.wait_ge(bstep, 4)
                nc.vector.tensor_tensor(bs[:, 1:2], bs[:, 1:2], bs[:, 0:1], ALU.mult).then_inc(bstep, 1)
                dve.wait_ge(bstep, 5)
                nc.vector.tensor_tensor(bs[:, 1:2], bs[:, 1:2], bn[:, 1:2], ALU.add).then_inc(bn_done, 1)
                SOFT = 4
                POST = 2
                with dve.Fori(0, B) as b:
                    for g in range(NQ):
                        n = b * NQ + g
                        cols = slice(g * QT * TP, (g + 1) * QT * TP)
                        rest, mid = k_rest[:, g % 2, :], k_mid[0:C4, g % 2, :]
                        hold(dve, k_hi, n + 1, own)
                        hold(dve, k_low, n + 1, own)
                        nc.vector.tensor_tensor(rest, ps_e[g % 2][:, 0, 0:QT * TP], ka[:, cols], ALU.subtract)\
                            .then_inc(k_ok, 1)
                        hold(dve, k_ok, n + 3, own)
                        nc.vector.tensor_copy(mid, rest[0:C4]).then_inc(k_step, 1)
                        hold(dve, k_step, n * 2 + 1, own)
                        nc.vector.tensor_tensor(kb[0:C4, cols], rest[0:C4], mid, ALU.subtract).then_inc(k_step, 1)

                    def query(s, slot):
                        qn = b * (NS + 1) + s
                        hold(dve, q_hi, qn + 1, own)
                        hold(dve, qs_ok, qn + 1, own)
                        nc.vector.tensor_tensor(q_rest[:, :], ps_r[1][:, 0:ST * TP], qa[:, slot, :],
                                                ALU.subtract).then_inc(q_left, 1)

                    def query_low(s, slot):
                        hold(dve, q_step, b * (NS + 1) + (s + 1), own)
                        lo = slice(C4, 2 * C4)
                        nc.vector.tensor_tensor(qb[lo, slot, :], q_rest[lo, :], q_mid[lo, :], ALU.subtract)\
                            .then_inc(qs_ok, 1)

                    query(0, 0)
                    query_low(0, 0)
                    hold(dve, zeroed, b + 1, own)

                    def below(S, slot):
                        hold(dve, mx_ok, (S + 1) * (ST * NCH), own)
                        d = S * SOFT
                        nc.vector.tensor_reduce(mn[:, slot, :], nm[:, slot, :, :], AX, ALU.min).then_inc(sstep, 1)
                        dve.wait_ge(sstep, d + 1)
                        nc.vector.tensor_tensor(dm[:, slot, :, :], spread(mn[:, slot, :], 2, NCH), nm[:, slot, :, :],
                                                ALU.subtract).then_inc(dm_ok, 1)

                    def chunk_weights(S, slot):
                        d = S * SOFT
                        hold(dve, ez_ok, S + 1, own)
                        nc.vector.tensor_tensor(zs[:, slot, :, :], zs[:, slot, :, :], ez[:, slot, :, :], ALU.mult)\
                            .then_inc(sstep, 1)
                        dve.wait_ge(sstep, d + 2)
                        nc.vector.tensor_reduce(zt[:, slot, :], zs[:, slot, :, :], AX, ALU.add).then_inc(sstep, 1)
                        dve.wait_ge(sstep, d + 3)
                        nc.vector.reciprocal(zr[:, slot, :], zt[:, slot, :]).then_inc(sstep, 1)
                        dve.wait_ge(sstep, d + 4)
                        nc.vector.tensor_tensor(wz[:, slot, :, :], ez[:, slot, :, :], spread(zr[:, slot, :], 2, NCH),
                                                ALU.mult).then_inc(w_rdy, 1)

                    def column(S, slot, j):
                        i, ch = j // NCH, j % NCH
                        dve.wait_ge(cstep, S * (ST * NCH) + max(j - NCH + 1, 0) + 1)
                        part_ = cs[:, ch * CK:(ch + 1) * CK]
                        nc.vector.scalar_tensor_tensor(part_, prob[:, slot, i, ch * CK:(ch + 1) * CK],
                                                       wz[:, slot, i, ch:ch + 1], part_, ALU.mult, ALU.add)\
                            .then_inc(cstep, 1)

                    def part(s_e, e, s_r, r):
                        s_n = s_e
                        s_e, s_r = overall(b, s_e), overall(b, s_r)
                        if s_r is not None:
                            below(s_r, r)
                        left = list(range(ST * NCH)) if s_r is not None else []
                        ready = False
                        for at, (kind, j) in enumerate(interleaved(s_e, s_r)):
                            if at == (2 if s_e is not None else 0) and s_r is not None:
                                chunk_weights(s_r, r)
                                hold(dve, w_rdy, s_r + 1, own)
                                ready = True
                            if kind == ENERGY:
                                i, ch = j // NCH, j % NCH
                                dve.wait_ge(e_ps, s_e * (ST * NCH) + (j + 1))
                                nc.vector.tensor_reduce(nm[:, e, i, ch:ch + 1], energies(e, j)[0:TP, :, 0:BK],
                                                        mybir.AxisListType.XY, ALU.max, negate=True).then_inc(mx_ok, 1)
                                if j == NEXT_QUERY + 2:
                                    query(s_n + 1, 1 - e)
                                elif j == NEXT_QUERY + 6:
                                    query_low(s_n + 1, 1 - e)
                            else:
                                hold(dve, r_ps, s_r * NMG + (j + 1) + 1, own)
                                part_ = xr[:, j * BK:(j + 1) * BK]
                                nc.vector.tensor_tensor(part_, part_, ps_r[j % 2][:, 0:BK], ALU.add)\
                                    .then_inc(r_ok, 1)
                            if ready and left and (kind == ENERGY or s_e is None):
                                column(s_r, r, left.pop(0))
                        for j in left:
                            column(s_r, r, j)

                    superblocks(dve, b, part)
                    hold(dve, r_ok, (b + 1) * (NS * NMG) + 2, own)
                    def difference(g):
                        n = b * NQ + g
                        d = n * POST
                        hold(dve, c_ps, n + 1, own)
                        r_ = rc[:, g % 2, :]
                        nc.vector.tensor_scalar(r_, ps_e[2][:, g % 2, 0:QT * TP], EPS_SUM, None, ALU.add)\
                            .then_inc(c_ok, 1)
                        hold(dve, c_ok, n + 3, own)
                        nc.vector.reciprocal(r_, r_).then_inc(pstep, 1)
                        hold(dve, pstep, d + 1, own)
                        part_ = xr[:, g * QT * TP:(g + 1) * QT * TP]
                        nc.vector.tensor_tensor(part_, part_, r_, ALU.mult).then_inc(pstep, 1)
                        hold(dve, pstep, d + 2, own)
                        nc.vector.tensor_tensor(part_, xct[:, g * QT * TP:(g + 1) * QT * TP], part_, ALU.subtract)\
                            .then_inc(d_ok, 1)

                    def residual(g):
                        n = b * NQ + g
                        hold(dve, tin_ok, n + 1, own)
                        hold(dve, t_st[g % 2], uses(g % 2, b, g) * 32 + 1, own)
                        hold(dve, uT, n + 1, own)
                        nc.vector.tensor_tensor(tout[:, g % 2, :, :], tin[:, g % 2, :, :],
                                                ps_r[g % 2][0:TP, :].rearrange("p (t c) -> p t c", c=C), ALU.add)\
                            .then_inc(t_ok, 1)

                    for g in range(NQ):
                        difference(g)
                        if g >= 3:
                            residual(g - 3)
                    for g in range(NQ - 3, NQ):
                        residual(g)
                    hold(dve, t_ok, (b + 1) * NQ + 2, own)
                    dve.sem_inc(image_done, 1)


E8, F = 8, 512
FB = F // 128
CAP = -(-5 * T // (4 * E8))
EBATCH = 512
SLOTS = -(-CAP // EBATCH) * EBATCH
NEB = SLOTS // EBATCH
DROPPED = 1 << 20
NF = T // 128
FG = 7
NFG = NF // FG
BIGGEST = 3.4028234663852886e38


def route_stage(nc, k, ins, t4_d, buf_d, tok, slots, weight):
    own, ident = k["own"], k["ident"]
    with ExitStack() as es:
        t = Ctx(nc, es, "route")
        hall = t.sb("hall", [128, NF, C])
        hn = t.sb("hn", [128, 2, FG, C])
        ht = t.sb("ht", [C, 2, FG * 128])
        gw = t.sb("gw", [C, E8])
        gb = t.sb("gb", [128, E8])
        lg = t.sb("lg", [128, NF, E8])
        ex = t.sb("ex", [128, NF, E8])
        hot = t.sb("hot", [128, NF, E8])
        cum = t.sb("cum", [128, NF, E8])
        iot_i = t.sb("iota_i", [128, E8], I32)
        iot = t.sb("iota", [128, E8])
        less8 = t.sb("iota_less_8", [128, E8])
        one = t.sb("one", [128, NF])
        tri = t.sb("tri", [128, 128])
        tot = t.sb("tot", [128, E8])
        mx, sm, idx, pos, kept, tmp = (t.sb(n, [128, NF]) for n in ("mx", "sm", "idx", "pos", "kept", "tmp"))
        st = t.sb("st", [128, 2, FG, 6])
        mv = t.sb("mv", [128, 2, FG, 2])
        ve = t.sb("ve", [128, 2, FG])
        rs = t.sb("rs", [128, 2, FG])
        half = t.sb("half", [128, FG])
        ps_t = [t.ps(f"ps_t{i}", [C, 2, 512]) for i in range(2)]
        ps_l = [t.ps(f"ps_l{i}", [128, 512]) for i in range(2)]
        (t_in, g_in, stat, agg, eps, rstd, hn_ok, hT, ht_ok, copied, l_ps, lg_ok, cst, step, sm_ok, tri_ps, slot_ok,
         sent, ct) = [t.sem(s) for s in (
             "tokens_loaded gate_loaded stats_ready mean_var_ready var_eps_ready rstd_ready hn_ready hT_in_psum "
             "ht_ready hn_kept logits_in_psum logits_ready constants_ready step exp_ready prefix_in_psum slots_ready "
             "rows_sent totals_ready").split()]

        with nc.Block() as block:

            @block.sync
            def _(sp):
                sp.dma_start(gw[:, :], ins["L1_ffn_gate_w"]).then_inc(g_in, 16)
                sp.dma_start(gb[:, :], row(ins["L1_ffn_gate_b"]).to_broadcast([128, E8])).then_inc(g_in, 16)
                tv = t4_d.rearrange("(p f) c -> p f c", p=128)
                for g in range(NFG):
                    if g:
                        sp.wait_ge(t_in, 16 * g)
                    sp.dma_start(tok[:, g * FG:(g + 1) * FG, :], tv[:, g * FG:(g + 1) * FG, :]).then_inc(t_in, 16)

            @block.gpsimd
            def _(pool):
                pool.memset(half[:, :], -0.5).then_inc(cst, 1)
                pool.iota(iot_i[:, :], [[1, E8]], base=0, channel_multiplier=0).then_inc(cst, 1)
                pool.memset(tri[:, :], 1.0).then_inc(cst, 1)
                pool.wait_ge(cst, 3)
                pool.affine_select(out=tri[:, :], in_=tri[:, :], compare_op=ALU.is_gt, fill=0.0, base=0,
                                   pattern=[[1, 128]], channel_multiplier=-1).then_inc(cst, 1)
                with pool.Fori(0, NFG // 2) as i:
                    for p in range(2):
                        n = i * 2 + p
                        hold(pool, agg, n + 1, own)
                        pool.tensor_scalar(ve[:, p, :], mv[:, p, :, 1], EPS, None, ALU.add).then_inc(eps, 1)
                        hold(pool, eps, n + 1, own)
                        pool.tensor_tensor(rs[:, p, :], ve[:, p, :], half[:, :], ALU.pow).then_inc(rstd, 1)
                pool.wait_ge(slot_ok, 1)
                pool.wait_ge(copied, NFG + 1)
                for f in range(NF):
                    pool.indirect_dma_start(
                        out=buf_d, out_offset=bass.IndirectOffsetOnAxis(ap=slots[:, 0, f:f + 1], axis=0),
                        in_=hall[:, f, :], in_offset=None, bounds_check=E8 * SLOTS - 1, oob_is_err=False)\
                        .then_inc(sent, 16)
                pool.wait_ge(sent, 16 * NF)

            @block.tensor
            def _(pe):
                pe.wait_ge(g_in, 32)

                def turn(n, p):
                    hold(pe, hn_ok, n + 1, own)
                    hold(pe, ht_ok, n + 1, own)
                    for i in range(FG):
                        mm = pe.transpose(ps_t[p][:, i // 4, (i % 4) * 128:(i % 4 + 1) * 128], hn[:, p, i, :],
                                          ident[:, :])
                    mm.then_inc(hT, 1)

                def gate(n, p):
                    hold(pe, ht_ok, n + 3, own)
                    hold(pe, lg_ok, n + 1, own)
                    for i in range(FG):
                        mm = pe.matmul(ps_l[p][:, i * E8:(i + 1) * E8], ht[:, p, i * 128:(i + 1) * 128], gw[:, :],
                                       start=True, stop=True)
                    mm.then_inc(l_ps, 1)

                with pe.Fori(0, NFG // 2) as i:
                    for p in range(2):
                        turn(i * 2 + p, p)
                    for p in range(2):
                        gate(i * 2 + p, p)
                pe.wait_ge(ct, 1)
                pe.matmul(ps_l[0][:, 0:E8], tri[:, :], tot[:, :], start=True, stop=True).then_inc(tri_ps, 1)

            @block.scalar
            def _(act):
                act.sem_inc(ht_ok, 2)
                with act.Fori(0, NFG // 2) as i:
                    for p in range(2):
                        n = i * 2 + p
                        hold(act, hT, n + 1, own)
                        for hb, w in ((0, 4), (1, FG - 4)):
                            last = nc.scalar.activation(ht[:, p, hb * 512:hb * 512 + w * 128],
                                                        ps_t[p][:, hb, 0:w * 128], ACT.Copy)
                        last.then_inc(ht_ok, 1)
                        nc.scalar.activation(hall[:, bass.ds(n * FG, FG), :], hn[:, p, :, :], ACT.Copy)\
                            .then_inc(copied, 1)
                act.wait_ge(sm_ok, 1)
                nc.scalar.activation(ex[:, :, :], ex[:, :, :], ACT.Exp).then_inc(sm_ok, 1)

            @block.vector
            def _(dve):
                dve.sem_inc(lg_ok, 2)
                dve.sem_inc(copied, 1)
                dve.wait_ge(g_in, 32)
                with dve.Fori(0, NFG // 2) as i:
                    for p in range(2):
                        n = i * 2 + p
                        hold(dve, t_in, n * 16 + 16, own)
                        for j in range(FG):
                            last = nc.vector.bn_stats(st[:, p, j, :], tok[:, n * FG + j, :])
                        last.then_inc(stat, 1)
                    for p in range(2):
                        hold(dve, stat, i * 2 + p + 1, own)
                        for j in range(FG):
                            last = nc.vector.bn_aggr(mv[:, p, j, :], st[:, p, j, :])
                        last.then_inc(agg, 1)
                    for p in range(2):
                        n = i * 2 + p
                        hold(dve, rstd, n + 1, own)
                        hold(dve, copied, i * 2 + 1, own)
                        for j in range(FG):
                            last = nc.vector.tensor_scalar(hn[:, p, j, :], tok[:, n * FG + j, :], mv[:, p, j, 0:1],
                                                           rs[:, p, j:j + 1], ALU.subtract, ALU.mult)
                        last.then_inc(hn_ok, 1)
                    for p in range(2):
                        n = i * 2 + p
                        hold(dve, l_ps, n + 1, own)
                        nc.vector.tensor_tensor(lg[:, bass.ds(n * FG, FG), :],
                                                ps_l[p][:, 0:FG * E8].rearrange("p (f e) -> p f e", e=E8),
                                                spread(gb[:, :], 1, FG), ALU.add).then_inc(lg_ok, 1)
                n = [0]

                def do(ins_):
                    n[0] += 1
                    ins_.then_inc(step, 1)
                    dve.wait_ge(step, n[0])

                dve.wait_ge(lg_ok, NFG + 2)
                dve.wait_ge(cst, 4)
                do(nc.vector.memset(one[:, :], 1.0))
                do(nc.vector.tensor_copy(iot[:, :], iot_i[:, :]))
                do(nc.vector.tensor_scalar(less8[:, :], iot[:, :], -float(E8), None, ALU.add))
                do(nc.vector.tensor_reduce(mx[:, :], lg[:, :, :], AX, ALU.max))
                nc.vector.tensor_tensor(ex[:, :, :], lg[:, :, :], spread(mx[:, :], 2, E8), ALU.subtract)\
                    .then_inc(sm_ok, 1)
                do(nc.vector.tensor_tensor(hot[:, :, :], lg[:, :, :], spread(mx[:, :], 2, E8), ALU.is_equal))
                do(nc.vector.tensor_tensor(hot[:, :, :], hot[:, :, :], spread(less8[:, :], 1, NF), ALU.mult))
                do(nc.vector.tensor_reduce(idx[:, :], hot[:, :, :], AX, ALU.min))
                do(nc.vector.tensor_scalar(idx[:, :], idx[:, :], float(E8), None, ALU.add))
                do(nc.vector.tensor_tensor(hot[:, :, :], spread(iot[:, :], 1, NF), spread(idx[:, :], 2, E8),
                                           ALU.is_equal))
                for e in range(E8):
                    do(nc.vector.tensor_tensor_scan(cum[:, :, e], one[:, :], hot[:, :, e], 0.0, ALU.mult, ALU.add))
                nc.vector.tensor_copy(tot[:, :], cum[:, NF - 1, :]).then_inc(ct, 1)
                dve.wait_ge(tri_ps, 1)
                do(nc.vector.tensor_tensor(cum[:, :, :], cum[:, :, :], spread(ps_l[0][:, 0:E8], 1, NF), ALU.add))
                do(nc.vector.tensor_tensor(cum[:, :, :], cum[:, :, :], hot[:, :, :], ALU.mult))
                do(nc.vector.tensor_reduce(pos[:, :], cum[:, :, :], AX, ALU.add))
                do(nc.vector.tensor_scalar(pos[:, :], pos[:, :], -1.0, None, ALU.add))
                do(nc.vector.tensor_scalar(kept[:, :], pos[:, :], float(CAP), None, ALU.is_lt))
                do(nc.vector.tensor_scalar(pos[:, :], pos[:, :], float(CAP - 1), None, ALU.min))
                do(nc.vector.tensor_scalar(tmp[:, :], idx[:, :], float(SLOTS), None, ALU.mult))
                do(nc.vector.tensor_tensor(pos[:, :], pos[:, :], tmp[:, :], ALU.add))
                do(nc.vector.tensor_copy(slots[:, 1, :], pos[:, :]))
                do(nc.vector.tensor_scalar(tmp[:, :], kept[:, :], -float(DROPPED), float(DROPPED), ALU.mult, ALU.add))
                do(nc.vector.tensor_tensor(pos[:, :], pos[:, :], tmp[:, :], ALU.add))
                do(nc.vector.tensor_copy(slots[:, 0, :], pos[:, :]))
                dve.sem_inc(slot_ok, 1)
                dve.wait_ge(sm_ok, 2)
                do(nc.vector.tensor_reduce(sm[:, :], ex[:, :, :], AX, ALU.add))
                do(nc.vector.reciprocal(sm[:, :], sm[:, :]))
                do(nc.vector.tensor_tensor(weight[:, :], sm[:, :], kept[:, :], ALU.mult))


def experts_stage(nc, k, ins, buf_d, res_d):
    own, ident = k["own"], k["ident"]
    NI = EBATCH // 128
    with ExitStack() as es:
        t = Ctx(nc, es, "experts")
        w1 = t.sb("w1", [C, 2, F])
        w2 = t.sb("w2", [128, 2, FB, C])
        b1r = t.sb("b1r", [E8 * FB, 128])
        b1t = t.sb("b1t", [128, E8 * FB])
        b2 = t.sb("b2", [128, E8, C])
        bi = t.sb("bi", [128, 2, NI, C])
        bt_ = t.sb("bt", [C, 2, EBATCH])
        hid = t.sb("hid", [128, 2, FB, EBATCH])
        yo = t.sb("yo", [128, 2, NI, C])
        ps_t = [t.ps(f"ps_t{i}", [C, 512]) for i in range(2)]
        ps_u = [t.ps(f"ps_u{i}", [128, 512]) for i in range(4)]
        ps_y = [t.ps(f"ps_y{i}", [128, 512]) for i in range(2)]
        (b_in, b1_ps, b1_ok, bT, bt_ok, u_ps, hid_ok, y_ps, y_ok) = [t.sem(s) for s in (
            "biases_loaded b1_in_psum b1_ready bT_in_psum bt_ready u_in_psum hidden_ready y_in_psum y_ready").split()]
        w_in, bi_in, y_st = ([t.sem(f"{s}{p}") for p in range(2)] for s in (
            "weights_loaded", "rows_loaded", "y_stored"))
        bufv = buf_d.rearrange("(b i p) c -> b p i c", p=128, i=NI)
        resv = res_d.rearrange("(b i p) c -> b p i c", p=128, i=NI)

        with nc.Block() as block:

            @block.sync
            def _(sp):
                sp.dma_start(b1r[:, :], ins["L1_ffn_b1"].rearrange("e (f p) -> (e f) p", p=128)).then_inc(b_in, 16)
                sp.dma_start(b2[:, :, :], ins["L1_ffn_b2"].rearrange("e c -> (e c)").rearrange("(a n) -> a n", a=1)
                             .to_broadcast([128, E8 * C]).rearrange("p (e c) -> p e c", c=C)).then_inc(b_in, 16)
                with sp.Fori(0, E8 // 2) as i:
                    for x in range(2):
                        e = i * 2 + x
                        hold(sp, y_ps, e * NEB + 1, own)
                        sp.dma_start(w1[:, x, :], ins["L1_ffn_w1"][e, :, :]).then_inc(w_in[x], 16)
                        sp.dma_start(w2[:, x, :, :], ins["L1_ffn_w2"][e, :, :].rearrange("(f p) c -> p f c", p=128))\
                            .then_inc(w_in[x], 16)
                        for q in range(NEB):
                            n = e * NEB + q
                            hold(sp, bT, n + 1, own)
                            sp.dma_start(bi[:, q % 2, :, :], bufv[n]).then_inc(bi_in[q % 2], 16)

            @block.tensor
            def _(pe):
                pe.sem_inc(y_ps, NEB + 1)
                pe.sem_inc(bT, 2)
                pe.wait_ge(b_in, 32)
                pe.transpose(ps_t[0][:, 0:E8 * FB], b1r[:, :], ident[0:E8 * FB, 0:E8 * FB]).then_inc(b1_ps, 1)
                pe.wait_ge(b1_ok, 1)
                with pe.Fori(0, E8 // 2) as i:
                    for x in range(2):
                        hold(pe, w_in[x], i * 32 + 32, own)
                        for q in range(NEB):
                            n = (i * 2 + x) * NEB + q
                            p = q % 2
                            hold(pe, bi_in[p], (i * 2 + x) * (8 * NEB) + 16 * (q // 2 + 1), own)
                            hold(pe, bt_ok, n + 1, own)
                            for j in range(NI):
                                mm = pe.transpose(ps_t[p][:, j * 128:(j + 1) * 128], bi[:, p, j, :], ident[:, :])
                            mm.then_inc(bT, 1)
                            hold(pe, bt_ok, n + 3, own)
                            for f in range(FB):
                                hold(pe, hid_ok, n * FB + (f + 1), own)
                                pe.matmul(ps_u[f][:, :], w1[:, x, f * 128:(f + 1) * 128], bt_[:, p, :], start=True,
                                          stop=True).then_inc(u_ps, 1)
                            hold(pe, hid_ok, n * FB + 2 * FB, own)
                            hold(pe, y_ok, n + 1, own)
                            for j in range(NI):
                                for f in range(FB):
                                    mm = pe.matmul(ps_y[p][:, j * C:(j + 1) * C],
                                                   hid[:, p, f, j * 128:(j + 1) * 128], w2[:, x, f, :],
                                                   start=(f == 0), stop=(f == FB - 1))
                            mm.then_inc(y_ps, 1)

            @block.scalar
            def _(act):
                act.sem_inc(bt_ok, 2)
                act.sem_inc(hid_ok, FB)
                act.wait_ge(b1_ps, 1)
                nc.scalar.activation(b1t[:, :], ps_t[0][:, 0:E8 * FB], ACT.Copy).then_inc(b1_ok, 1)
                act.wait_ge(b1_ok, 1)
                with act.Fori(0, E8 // 2) as i:
                    for x in range(2):
                        e = i * 2 + x
                        for q in range(NEB):
                            n = e * NEB + q
                            p = q % 2
                            hold(act, bT, n + 3, own)
                            nc.scalar.activation(bt_[:, p, :], ps_t[p][:, :], ACT.Copy).then_inc(bt_ok, 1)
                            for f in range(FB):
                                hold(act, u_ps, n * FB + (f + 1), own)
                                nc.scalar.activation(hid[:, p, f, :], ps_u[f][:, :], ACT.Relu,
                                                     bias=b1t[:, bass.ds(e * FB + f, 1)], scale=1.0).then_inc(hid_ok, 1)
                            hold(act, y_ok, n + 3, own)
                            act.dma_start(resv[n], yo[:, p, :, :]).then_inc(y_st[p], 16)
                for p in range(2):
                    act.wait_ge(y_st[p], 16 * E8 * NEB // 2 + 1)

            @block.vector
            def _(dve):
                dve.sem_inc(y_ok, 2)
                for s in y_st:
                    dve.sem_inc(s, 1)
                with dve.Fori(0, E8 // 2) as i:
                    for x in range(2):
                        e = i * 2 + x
                        for q in range(NEB):
                            n = e * NEB + q
                            p = q % 2
                            hold(dve, y_ps, n + NEB + 2, own)
                            hold(dve, y_st[p], e * (8 * NEB) + 16 * (q // 2) + 1, own)
                            nc.vector.tensor_tensor(yo[:, p, :, :], ps_y[p][:, :].rearrange("p (t c) -> p t c", c=C),
                                                    spread(b2[:, e, :], 1, NI), ALU.add).then_inc(y_ok, 1)


def combine_stage(nc, k, res_d, tok, slots, weight, out):
    own = k["own"]
    with ExitStack() as es:
        t = Ctx(nc, es, "combine")
        yg = t.sb("yg", [128, 2, FG, C])
        yc = t.sb("yc", [128, 2, FG, C])
        fx = t.sb("fx", [128, 2, FG, C])
        mk = t.sb("mk", [128, 3, FG, C], I32)
        lim = t.sb("lim", [128, 2, FG, C])
        step, res, cst = (t.sem(s) for s in ("step", "result_ready", "constants_ready"))
        freed = t.sem("rows_freed")
        got = [t.sem(f"gathered{p}") for p in range(2)]
        stored = t.sem("stored")
        outv = out.rearrange("(p f) c -> p f c", p=128)

        with nc.Block() as block:

            @block.gpsimd
            def _(pool):
                pool.memset(lim[:, 0, :, :], 1e4).then_inc(cst, 1)
                pool.memset(lim[:, 1, :, :], -1e4).then_inc(cst, 1)
                for g in range(NFG):
                    if g >= 2:
                        pool.wait_ge(freed, g - 1)
                    for j in range(FG):
                        f = g * FG + j
                        pool.indirect_dma_start(
                            out=yg[:, g % 2, j, :], out_offset=None, in_=res_d,
                            in_offset=bass.IndirectOffsetOnAxis(ap=slots[:, 1, f:f + 1], axis=0),
                            bounds_check=E8 * SLOTS - 1, oob_is_err=False).then_inc(got[g % 2], 16)

            @block.vector
            def _(dve):
                n = [0]

                def do(ins_):
                    n[0] += 1
                    ins_.then_inc(step, 1)
                    return n[0]

                dve.wait_ge(cst, 2)
                for g in range(NFG):
                    p = g % 2
                    part = tok[:, g * FG:(g + 1) * FG, :]
                    dve.wait_ge(got[p], 16 * FG * (g // 2 + 1))
                    a = do(nc.vector.memset(fx[:, p, :, :], 0.0))
                    nc.vector.tensor_tensor(yc[:, p, :, :], yg[:, p, :, :],
                                            spread(weight[:, g * FG:(g + 1) * FG], 2, C), ALU.mult)\
                        .then_inc(freed, 1)
                    dve.wait_ge(freed, g + 1)
                    y = yc[:, p, :, :]
                    do(nc.vector.tensor_tensor(mk[:, 0, :, :], y, y, ALU.is_equal))
                    do(nc.vector.tensor_scalar(mk[:, 1, :, :], y, BIGGEST, None, ALU.is_gt))
                    a = do(nc.vector.tensor_scalar(mk[:, 2, :, :], y, -BIGGEST, None, ALU.is_lt))
                    dve.wait_ge(step, a)
                    dve.wait_ge(step, do(nc.vector.copy_predicated(fx[:, p, :, :], mk[:, 0, :, :], y)))
                    for i in range(2):
                        dve.wait_ge(step, do(nc.vector.copy_predicated(fx[:, p, :, :], mk[:, 1 + i, :, :],
                                                                       lim[:, i, :, :])))
                    nc.vector.tensor_tensor(part, part, fx[:, p, :, :], ALU.add).then_inc(res, 1)

            @block.sync
            def _(sp):
                for g in range(NFG):
                    sp.wait_ge(res, g + 1)
                    sp.dma_start(outv[:, g * FG:(g + 1) * FG, :], tok[:, g * FG:(g + 1) * FG, :]).then_inc(stored, 16)
                sp.wait_ge(stored, 16 * NFG)


def ffn(nc, k, c, ins, t4_d, buf_d, res_d, out):
    tok = c.sb("tokens", [128, NF, C])
    slots = c.sb("slots", [128, 2, NF], I32)
    weight = c.sb("weight", [128, NF])
    route_stage(nc, k, ins, t4_d, buf_d, tok, slots, weight)
    experts_stage(nc, k, ins, buf_d, res_d)
    combine_stage(nc, k, res_d, tok, slots, weight, out)


_NAMES = ["x", "L0_conv_w_in", "L0_conv_b_in", "L0_conv_w_dw", "L0_conv_b_dw", "L0_conv_ln_dw_g", "L0_conv_ln_dw_b",
          "L0_conv_w_off", "L0_conv_b_off", "L0_conv_w_mask", "L0_conv_b_mask", "L0_conv_w_out", "L0_conv_b_out",
          "L0_conv_ln1_g", "L0_conv_ln1_b", "L0_conv_w_fc1", "L0_conv_b_fc1", "L0_conv_w_fc2", "L0_conv_b_fc2",
          "L0_conv_ln2_g", "L0_conv_ln2_b", "L0_conv_gamma1", "L0_conv_gamma2", "L1_attn_Wq", "L1_attn_Wk",
          "L1_attn_Wv", "L1_attn_bv", "L1_attn_Wt", "L1_attn_bt", "L1_attn_gamma", "L1_attn_beta", "L1_attn_bn_mean",
          "L1_attn_bn_var", "L1_ffn_gate_w", "L1_ffn_gate_b", "L1_ffn_w1", "L1_ffn_b1", "L1_ffn_w2", "L1_ffn_b2"]


def build(nc, ins, out):
    def scratch(name, shape):
        return nc.dram_tensor(name, shape, F32, kind="Internal").ap()

    xp_d = scratch("projected", (T + 2 * PAD, C))
    om_d = scratch("offsets_masks", (B * HH, TP, OM))
    y_d = scratch("deformed", (B * HH, TP, C))
    t_d = scratch("block_out", (B * HH, TP, C))
    xc_d = scratch("block_out_normed", (B * HH, TP, C))
    t4_d = scratch("attended", (T, C))
    buf_d = scratch("dispatched", (E8 * SLOTS, C))
    res_d = scratch("expert_out", (E8 * SLOTS, C))

    with ExitStack() as everything:
        k = identity(nc, Ctx(nc, everything, "all"))
        with ExitStack() as block:
            c = Ctx(nc, block, "block")
            constants(nc, c, ins, k)
            shift_tables(nc, k, c)
            extremes = c.sb("extremes", [TP, NB, 4])
            base = c.sb("base", [TP, 2])
            counts = c.sb("counts", [1, 4], I32)
            zero_stage(nc, [y_d.rearrange("t p c -> (t p c)"), buf_d.rearrange("n c -> (n c)")])
            offsets_stage(nc, k, ins["x"], xp_d, om_d, extremes)
            window_stage(nc, k, extremes, base, counts)
            deformable_stage(nc, k, xp_d, om_d, y_d, base, counts)
            rows_stage(nc, k, ins["x"], y_d, t_d, xc_d)
        attention_stage(nc, k, ins, xc_d, t_d, t4_d)
        ffn(nc, k, Ctx(nc, everything, "ffn"), ins, t4_d, buf_d, res_d, out.rearrange("b y x c -> (b y x) c"))


def kernel(**inputs):
    import numpy as np
    import concourse.bacc as bacc
    from concourse.bass_utils import run_bass_kernel_spmd as run

    nc = bacc.Bacc("TRN2", target_bir_lowering=False, num_devices=1)
    arrays, ins = {}, {}
    for name in _NAMES:
        a = np.ascontiguousarray(inputs[name])
        arrays[f"in_{name}"] = a
        ins[name] = nc.dram_tensor(f"in_{name}", a.shape, mybir.dt.from_np(a.dtype), kind="ExternalInput").ap()
    out = nc.dram_tensor("out", (B, H, W, C), F32, kind="ExternalOutput").ap()
    build(nc, ins, out)
    return run(nc, [arrays], core_ids=[0]).results[0]["out"]
```

```python
from contextlib import ExitStack

import concourse.bass as bass
from concourse import mybir

F32 = mybir.dt.float32
I32 = mybir.dt.int32
ALU = mybir.AluOpType
ACT = mybir.ActivationFunctionType
AX = mybir.AxisListType.X
MAX = bass.bass_isa.ReduceOp.max

B, H, W, C = 4, 56, 56, 128
G, K = 16, 9
GC = C // G
HH = H // 2
TP = 2 * W
NPIX = H * W
T = B * NPIX
GK = G * K
OM = 3 * GK
QT = 4
NQ = HH // QT
NB = B * NQ

R = 7
CW = R + 2
ROWS = HH + CW - 1
RING = 16
OFFMAX = 60.0
PAD = (int(OFFMAX) + R + 6) * W
EPS = 1e-5


class Ctx:

    def __init__(self, nc, stack, stage):
        self.nc, self.stack, self.stage, self.sems = nc, stack, stage, []
        stack.callback(self.close)

    def sb(self, name, shape, dt=F32):
        return self.stack.enter_context(self.nc.sbuf_tensor(f"{self.stage}_{name}", shape, dt))

    def ps(self, name, shape):
        return self.stack.enter_context(self.nc.psum_tensor(f"{self.stage}_{name}", shape, F32))

    def sem(self, name):
        self.sems.append(self.nc.alloc_semaphore(f"{self.stage}_{name}"))
        return self.sems[-1]

    def close(self):
        if self.sems:
            self.nc.clear_and_free_semaphores(self.sems)
            self.nc.all_engine_barrier()


def spread(ap, axis, n):
    v = ap.unsqueeze(axis)
    shape = list(v.shape)
    shape[axis] = n
    return v.to_broadcast(shape)


def row(ap):
    return ap.rearrange("(a n) -> a n", a=1)


def col(ap):
    return ap.rearrange("(n a) -> n a", a=1)


def hold(eng, sem, value, own):
    eng.wait_ge(sem, value)
    eng.sem_inc(own, 1)


def identity(nc, c):
    k = {"ident": c.sb("ident", [128, 128]), "own": c.sem("wait_carrier")}
    with ExitStack() as es:
        t = Ctx(nc, es, "identity")
        zeroed = t.sem("zeroed")
        with nc.Block() as block:

            @block.gpsimd
            def _(pool):
                pool.memset(k["ident"][:, :], 0.0).then_inc(zeroed, 1)
                pool.wait_ge(zeroed, 1)
                pool.affine_select(out=k["ident"][:, :], in_=k["ident"][:, :], compare_op=ALU.not_equal, fill=1.0,
                                   base=0, pattern=[[-1, 128]], channel_multiplier=1)
    return k


def constants(nc, c, ins, k):
    for name, src in (("w_in", "L0_conv_w_in"), ("w_out", "L0_conv_w_out"), ("w_fc1", "L0_conv_w_fc1"),
                      ("w_fc2", "L0_conv_w_fc2")):
        k[name] = c.sb(name, [C, C])
    k["w_dw"] = c.sb("w_dw", [C, K])
    k["w_om"] = c.sb("w_om", [C, OM])
    k["b_om"] = c.sb("b_om", [128, OM])
    for name in ("b_in", "b_out", "ln1_g", "ln1_b", "b_fc2", "ln2_g", "ln2_b", "gamma1", "gamma2"):
        k[name] = c.sb(name + "_rows", [128, C])
    for name in ("b_dw", "ln_dw_g", "ln_dw_b", "b_fc1"):
        k[name] = c.sb(name + "_col", [C, 1])
    with ExitStack() as es:
        t = Ctx(nc, es, "const")
        raw_w = t.sb("raw_w", [C, OM])
        raw_b = t.sb("raw_b", [128, OM])
        raw_d = t.sb("raw_dw", [K, C])
        loaded, turned = t.sem("loaded"), t.sem("turned")
        psw = t.ps("psw", [C, 512])
        with nc.Block() as block:
            n_loads = [0]

            @block.sync
            def _(sp):
                def load(dst, src):
                    sp.dma_start(dst, src).then_inc(loaded, 16)
                    n_loads[0] += 16

                for name in ("w_in", "w_out", "w_fc1", "w_fc2"):
                    load(k[name][:, :], ins["L0_conv_" + name])
                load(raw_d[:, :], ins["L0_conv_w_dw"].rearrange("a b o c -> (a b o) c"))
                load(raw_w[:, 0:2 * GK], ins["L0_conv_w_off"])
                load(raw_w[:, 2 * GK:OM], ins["L0_conv_w_mask"])
                load(raw_b[:, 0:2 * GK], row(ins["L0_conv_b_off"]).to_broadcast([128, 2 * GK]))
                load(raw_b[:, 2 * GK:OM], row(ins["L0_conv_b_mask"]).to_broadcast([128, GK]))
                for name in ("b_in", "b_out", "ln1_g", "ln1_b", "b_fc2", "ln2_g", "ln2_b", "gamma1", "gamma2"):
                    load(k[name][:, :], row(ins["L0_conv_" + name]).to_broadcast([128, C]))
                for name in ("b_dw", "ln_dw_g", "ln_dw_b", "b_fc1"):
                    load(k[name][:, :], col(ins["L0_conv_" + name]))

            @block.tensor
            def _(pe):
                pe.wait_ge(loaded, n_loads[0])
                pe.transpose(psw[:, 0:K], raw_d[:, :], k["ident"][0:K, 0:K]).then_inc(turned, 1)

            @block.vector
            def _(dve):
                dve.wait_ge(loaded, n_loads[0])
                for raw, dst in ((raw_w, k["w_om"]), (raw_b, k["b_om"])):
                    for xy in range(2):
                        nc.vector.tensor_copy(
                            dst[:, xy * GK:(xy + 1) * GK].rearrange("c (k g) -> c k g", g=G),
                            raw[:, 0:2 * GK].rearrange("c (g k d) -> c k g d", k=K, d=2)[:, :, :, xy])
                    nc.vector.tensor_copy(dst[:, 2 * GK:OM].rearrange("c (k g) -> c k g", g=G),
                                          raw[:, 2 * GK:OM].rearrange("c (g k) -> c k g", k=K))
                dve.wait_ge(turned, 1)
                nc.vector.tensor_copy(k["w_dw"][:, :], psw[:, 0:K])


NBUF = 3


def offsets_stage(nc, k, x, xp_d, om_d, extremes):
    own, ident = k["own"], k["ident"]
    with ExitStack() as es:
        t = Ctx(nc, es, "offs")
        x_sb = t.sb("x_sb", [TP, HH, C])
        xpad = t.sb("xpad", [C, (H + 2) * (W + 2)])
        xt = t.sb("xt", [C, HH, TP])
        conv = t.sb("conv", [C, HH, 2, W])
        st = t.sb("st", [TP, 2, QT, 6])
        mv = t.sb("mv", [TP, 2, QT, 2])
        ve = t.sb("ve", [TP, 2, QT])
        rs = t.sb("rs", [TP, 2, QT])
        half = t.sb("half", [TP, QT])
        xn = t.sb("xn", [TP, 2, QT, C])
        x1t = t.sb("x1t", [C, 2, QT * TP])
        om = t.sb("om", [TP, NBUF, QT, OM])
        mx = t.sb("mx", [TP, NBUF, QT, G])
        xp = t.sb("xp", [TP, 2, QT, C])
        zero = t.sb("zero", [TP, 4 * C])
        ps_x = [t.ps(f"ps_x{i}", [C, 512]) for i in range(1)]
        ps_c = t.ps("ps_c", [TP, 512])
        ps_n = t.ps("ps_n", [C, 512])
        ps_o = t.ps("ps_o", [TP, QT, 512])
        ps_p = t.ps("ps_p", [TP, 512])
        (x_in, x_used, xT, xT_ev, xT_out, conv_step, conv_done, convT, convT_used, stat, agg, eps, rstd, xn_ok, xnT,
         x1, om_ps, om_ev, om_sub, om_exp, om_clamp, om_max, om_sum,
         om_rec, om_ok, xp_ok, om_st, xp_st, ext, zr, half_ok, xz, pad_st) = [
            t.sem(s) for s in (
                "x_loaded", "x_used", "xT_in_psum", "xT_evacuated", "xT_copied", "conv_step", "conv_done",
                "convT_in_psum", "convT_used", "stats_ready", "mean_var_ready", "var_eps_ready", "rstd_ready",
                "xn_ready", "xnT_in_psum", "x1_ready", "om_in_psum", "om_evacuated", "om_less_max", "om_exp",
                "om_clamped", "om_max_ready", "om_sum_ready", "om_reciprocal_ready",
                "om_ready", "xp_ready", "om_stored", "xp_stored", "extremes_done", "pad_zero_ready", "half_ready",
                "xpad_zeroed", "pad_stored")]
        xv = x.rearrange("b (h j) x c -> b h x j c", h=2)
        xpv = xp_d[PAD:PAD + T, :].rearrange("(b h j x) c -> b h x j c", b=B, h=2, x=W)
        xpad3 = xpad[:, :].rearrange("c (y x) -> c y x", x=W + 2)
        with nc.Block() as block:

            @block.sync
            def _(sp):
                sp.wait_ge(zr, 1)
                rows_out = TP * 4
                for base in (0, PAD + T):
                    for r0 in range(0, PAD, rows_out):
                        n = min(rows_out, PAD - r0) // 4
                        sp.dma_start(xp_d[base + r0:base + r0 + 4 * n, :].rearrange("(p f) c -> p (f c)", f=4),
                                     zero[0:n, :]).then_inc(pad_st, 16)
                npad = 2 * len(range(0, PAD, rows_out))

                def load(b):
                    for h in range(2):
                        sp.dma_start(x_sb[h * W:(h + 1) * W, :, :], xv[b, h]).then_inc(x_in, 16)

                def store_xp(b, q):
                    n = q + b * NQ
                    sp.wait_ge(xp_ok, n + 1)
                    for h in range(2):
                        sp.dma_start(xpv[b, h, :, bass.ds(q * QT, QT), :],
                                     xp[h * W:(h + 1) * W, n % 2, :, :]).then_inc(xp_st, 16)

                def store_om(n):
                    hold(sp, om_st, 16 * n + (16 * (NBUF - 1) + 1), own)
                    sp.wait_ge(om_ok, n + 1)
                    sp.dma_start(om_d[bass.ds(n * QT, QT), :, :].rearrange("t p o -> p t o"),
                                 om[:, n % NBUF, :, :]).then_inc(om_st, 16)

                load(0)
                for b in range(B):
                    if b + 1 < B:
                        sp.wait_ge(x_used, b + 1)
                        load(b + 1)
                    store_xp(b, 0)
                    with sp.Fori(1, NQ) as q:
                        store_xp(b, q)
                        store_om(q + (b * NQ - 1))
                    store_om(b * NQ + (NQ - 1))
                sp.wait_ge(pad_st, 16 * npad)
                sp.wait_ge(xp_st, 32 * NB + 1)
                sp.wait_ge(om_st, 16 * (NB + NBUF - 1) + 1)

            @block.gpsimd
            def _(pool):
                pool.memset(half[:, :], -0.5).then_inc(half_ok, 1)
                pool.wait_ge(half_ok, 1)
                with pool.Fori(0, B) as b:

                    def rstds(q):
                        n = b * NQ + q
                        hold(pool, agg, n + 1, own)
                        pool.tensor_scalar(ve[:, q % 2, :], mv[:, q % 2, :, 1], EPS, None, ALU.add).then_inc(eps, 1)
                        hold(pool, eps, n + 1, own)
                        pool.tensor_tensor(rs[:, q % 2, :], ve[:, q % 2, :], half[:, :], ALU.pow).then_inc(rstd, 1)

                    def masks(q):
                        n = b * NQ + q
                        hold(pool, om_rec, n + 1, own)
                        lk = om[:, n % NBUF, :, 2 * GK:OM].rearrange("p t (k g) -> p t k g", g=G)
                        pool.tensor_tensor(lk, lk, spread(mx[:, n % NBUF, :, :], 2, K), ALU.mult).then_inc(om_ok, 1)

                    def less_max(q):
                        n = b * NQ + q
                        hold(pool, om_max, n + 1, own)
                        lk = om[:, n % NBUF, :, 2 * GK:OM].rearrange("p t (k g) -> p t k g", g=G)
                        pool.tensor_tensor(lk, lk, spread(mx[:, n % NBUF, :, :], 2, K), ALU.subtract).then_inc(om_sub, 1)

                    rstds(0)
                    rstds(1)
                    for q in range(NQ):
                        less_max(q)
                        if q + 2 < NQ:
                            rstds(q + 2)
                        if q:
                            masks(q - 1)
                    masks(NQ - 1)

            @block.tensor
            def _(pe):
                def conv_turn(n, q):
                    hold(pe, convT_used, n + 1, own)
                    for i in range(QT):
                        mm = pe.transpose(ps_c[:, i * C:(i + 1) * C],
                                          conv[:, q * QT + i, :, :].rearrange("c h x -> c (h x)"), ident[:, :])
                    mm.then_inc(convT, 1)

                with pe.Fori(0, B) as b:
                    hold(pe, x_in, 32 * b + 32, own)
                    for q in range(NQ):
                        hold(pe, xT_ev, b * NQ + q + 1, own)
                        for i in range(QT):
                            mm = pe.transpose(ps_x[0][:, i * TP:(i + 1) * TP], x_sb[:, q * QT + i, :],
                                              ident[0:TP, 0:TP])
                        mm.then_inc(xT, 1)
                    hold(pe, conv_done, b + 1 + 1, own)
                    for q in range(2):
                        conv_turn(b * NQ + q, q)
                    for q in range(NQ):
                        n = b * NQ + q
                        hold(pe, xn_ok, n + 1, own)
                        hold(pe, x1, n + 1, own)
                        for i in range(QT):
                            mm = pe.transpose(ps_n[:, i * TP:(i + 1) * TP], xn[:, q % 2, i, :],
                                              ident[0:TP, 0:TP])
                        mm.then_inc(xnT, 1)
                        hold(pe, om_ev, n + 1, own)
                        for i in range(QT):
                            mm = pe.matmul(ps_p[:, i * C:(i + 1) * C], xt[:, q * QT + i, :], k["w_in"][:, :],
                                           start=True, stop=True)
                        hold(pe, x1, n + 2, own)
                        for i in range(QT):
                            mm = pe.matmul(ps_o[:, i, 0:OM], x1t[:, q % 2, i * TP:(i + 1) * TP],
                                           k["w_om"][:, :], start=True, stop=True)
                        mm.then_inc(om_ps, 1)
                        if q + 2 < NQ:
                            conv_turn(n + 2, q + 2)

            @block.scalar
            def _(act):
                act.sem_inc(xT_ev, 1)
                act.sem_inc(x1, 1)
                act.wait_ge(xz, 1)
                with act.Fori(0, B) as b:
                    for q in range(NQ):
                        n = b * NQ + q
                        if q == 0:
                            hold(act, conv_done, b + 1, own)
                            hold(act, om_ps, b * NQ + 1, own)
                        hold(act, xT, n + 1, own)
                        src = ps_x[0][:, 0:QT * TP].rearrange("c (j h x) -> c j h x", h=2, x=W)
                        for h in range(2):
                            y = h * HH + q * QT + 1
                            nc.scalar.activation(xpad3[:, y:y + QT, 1:W + 1], src[:, :, h, :], ACT.Copy)
                        nc.scalar.activation(xt[:, q * QT:(q + 1) * QT, :],
                                             ps_x[0][:, 0:QT * TP].rearrange("c (j p) -> c j p", p=TP),
                                             ACT.Copy).then_inc(xT_ev, 1)
                        if q == NQ - 1:
                            act.drain().then_inc(x_used, 1)

                    def gelu(q):
                        n = b * NQ + q
                        hold(act, xnT, n + 1, own)
                        hold(act, om_ps, n + 1, own)
                        nc.scalar.activation(x1t[:, q % 2, :], ps_n[:, 0:QT * TP], ACT.Gelu,
                                             bias=k["ln_dw_b"][:, 0:1], scale=k["ln_dw_g"][:, 0:1]).then_inc(x1, 1)

                    gelu(0)
                    for q in range(NQ):
                        n = b * NQ + q
                        if q + 1 < NQ:
                            gelu(q + 1)
                        hold(act, om_sub, n + 1, own)
                        masks = om[:, n % NBUF, :, 2 * GK:OM]
                        nc.scalar.activation(masks, masks, ACT.Exp).then_inc(om_exp, 1)

            @block.vector
            def _(dve):
                nc.vector.memset(zero[:, :], 0.0).then_inc(zr, 1)
                nc.vector.memset(xpad[:, :], 0.0).then_inc(xz, 1)
                dve.sem_inc(convT_used, 1)
                dve.sem_inc(om_ev, 1)
                dve.sem_inc(om_st, 16 * (NBUF - 1))
                for s in (convT, conv_done, om_ps, om_st, xp_st):
                    dve.sem_inc(s, 1)

                def statistics(n, q):
                    hold(dve, convT, n + 1 + 1, own)
                    for i in range(QT):
                        ins_ = nc.vector.bn_stats(st[:, q % 2, i, :], ps_c[:, i * C:(i + 1) * C])
                    ins_.then_inc(stat, 1)
                    hold(dve, stat, n + 1, own)
                    for i in range(QT):
                        ins_ = nc.vector.bn_aggr(mv[:, q % 2, i, :], st[:, q % 2, i, :])
                    ins_.then_inc(agg, 1)

                def normalise(n, q):
                    hold(dve, rstd, n + 1, own)
                    for i in range(QT):
                        ins_ = nc.vector.tensor_scalar(xn[:, q % 2, i, :], ps_c[:, i * C:(i + 1) * C],
                                                       mv[:, q % 2, i, 0:1], rs[:, q % 2, i:i + 1],
                                                       ALU.subtract, ALU.mult)
                    ins_.then_inc(xn_ok, 1)
                    dve.wait_ge(xn_ok, n + 1)
                    dve.sem_inc(convT_used, 1)

                def evacuate(n, q):
                    hold(dve, om_ps, n + 1 + 1, own)
                    hold(dve, om_st, 16 * n + 1, own)
                    hold(dve, xp_st, 32 * n + 1, own)
                    nc.vector.tensor_tensor(xp[:, n % 2, :, :],
                                            ps_p[:, :].rearrange("p (t c) -> p t c", c=C),
                                            spread(k["b_in"][0:TP, :], 1, QT), ALU.add).then_inc(xp_ok, 1)
                    nc.vector.tensor_tensor(om[:, n % NBUF, :, :], ps_o[:, :, 0:OM],
                                            spread(k["b_om"][0:TP, :], 1, QT), ALU.add).then_inc(om_ev, 1)
                    hold(dve, om_ev, n + 2, own)
                    logits = om[:, n % NBUF, :, 2 * GK:OM]
                    nc.vector.tensor_reduce(mx[:, n % NBUF, :, :], logits.rearrange("p t (k g) -> p t g k", g=G),
                                            AX, ALU.max).then_inc(om_max, 1)
                    nc.vector.tensor_scalar(om[:, n % NBUF, :, 0:2 * GK], om[:, n % NBUF, :, 0:2 * GK],
                                            OFFMAX, -OFFMAX, ALU.min, ALU.max).then_inc(om_clamp, 1)

                def extreme(n):
                    hold(dve, om_clamp, n + 1, own)
                    for xy in range(2):
                        part = om[:, n % NBUF, :, xy * GK:(xy + 1) * GK]
                        nc.vector.tensor_reduce(extremes[:, n, 2 * xy:2 * xy + 1], part, mybir.AxisListType.XY,
                                                ALU.min, negate=True)
                        nc.vector.tensor_reduce(extremes[:, n, 2 * xy + 1:2 * xy + 2], part,
                                                mybir.AxisListType.XY, ALU.max)

                def sums(n):
                    hold(dve, om_exp, n + 1, own)
                    nc.vector.tensor_reduce(mx[:, n % NBUF, :, :],
                                            om[:, n % NBUF, :, 2 * GK:OM].rearrange("p t (k g) -> p t g k", g=G),
                                            AX, ALU.add).then_inc(om_sum, 1)
                    hold(dve, om_sum, n + 1, own)
                    nc.vector.reciprocal(mx[:, n % NBUF, :, :], mx[:, n % NBUF, :, :]).then_inc(om_rec, 1)

                taps = [(ky, kx, h) for ky in range(3) for kx in range(3) for h in range(2)]
                with dve.Fori(0, B) as b:
                    hold(dve, xT_ev, NQ * b + NQ + 1, own)
                    hold(dve, convT, NQ * b + 1, own)
                    for s, (ky, kx, h) in enumerate(taps):
                        out = conv[:, :, h, :]
                        src = xpad3[:, h * HH + ky:h * HH + ky + HH, kx:kx + W]
                        tap = k["w_dw"][:, 3 * ky + kx:3 * ky + kx + 1]
                        if s < 2:
                            nc.vector.tensor_scalar(out, src, tap, k["b_dw"][:, 0:1], ALU.mult, ALU.add)\
                                .then_inc(conv_step, 1)
                        else:
                            dve.wait_ge(conv_step, b * len(taps) + s - 1)
                            nc.vector.scalar_tensor_tensor(out, src, tap, out, ALU.mult, ALU.add)\
                                .then_inc(conv_step, 1)
                    hold(dve, conv_step, b * len(taps) + len(taps), own)
                    dve.sem_inc(conv_done, 1)
                    for q in range(2):
                        statistics(b * NQ + q, q)
                        normalise(b * NQ + q, q)
                    for q in range(NQ):
                        n = b * NQ + q
                        evacuate(n, q)
                        if q + 2 < NQ:
                            statistics(n + 2, q)
                        extreme(n)
                        if q:
                            sums(n - 1)
                        if q + 2 < NQ:
                            normalise(n + 2, q)
                    sums(b * NQ + (NQ - 1))


def window_stage(nc, k, extremes, base, counts):
    own = k["own"]
    with ExitStack() as es:
        t = Ctx(nc, es, "window")
        ext = t.sb("ext", [TP, 4])
        ext_all = t.sb("ext_all", [TP, 4])
        ei = t.sb("ei", [TP, 4], I32)
        ef = t.sb("ef", [TP, 4])
        eg = t.sb("eg", [TP, 4])
        nb = t.sb("nb", [TP, 2])
        step, allm = t.sem("w_step"), t.sem("w_all")
        with nc.Block() as block:

            @block.gpsimd
            def _(pool):
                pool.wait_ge(step, 1)
                pool.partition_all_reduce(ext_all[:, :], ext[:, :], TP, MAX).then_inc(allm, 1)

            @block.vector
            def _(dve):
                n = [0]

                def do(ins_):
                    n[0] += 1
                    ins_.then_inc(step, 1)
                    dve.wait_ge(step, n[0])

                do(nc.vector.tensor_reduce(ext[:, :], extremes[:, :, :].rearrange("p n s -> p s n"), AX, ALU.max))
                dve.wait_ge(allm, 1)
                for c0 in (0, 2):
                    do(nc.vector.tensor_scalar(ext_all[:, c0:c0 + 1], ext_all[:, c0:c0 + 1], -1.0, None, ALU.mult))

                def floor(v, out, i, f):
                    do(nc.vector.tensor_copy(i, v))
                    do(nc.vector.tensor_copy(f, i))
                    do(nc.vector.tensor_tensor(out, f, v, ALU.is_gt))
                    do(nc.vector.tensor_tensor(out, f, out, ALU.subtract))

                floor(ext_all[:, :], eg[:, :], ei[:, :], ef[:, :])
                do(nc.vector.tensor_copy(base[:, :], eg[:, 0::2]))
                do(nc.vector.tensor_tensor(nb[:, :], eg[:, 1::2], eg[:, 0::2], ALU.subtract))
                do(nc.vector.tensor_scalar(nb[:, :], nb[:, :], float(2 + R - 1) + 0.1, 1.0 / R, ALU.add, ALU.mult))
                floor(nb[:, :], ef[:, 0:2], ei[:, 0:2], eg[:, 0:2])
                do(nc.vector.tensor_copy(counts[:, 0:2], ef[0:1, 0:2]))
                do(nc.vector.tensor_copy(counts[:, 2:4], base[0:1, 0:2]))


def shift_tables(nc, k, c):
    k["steps"] = c.sb("steps", [TP, R])
    k["xpos"] = c.sb("xpos", [TP, CW])
    k["ypos"] = c.sb("ypos", [TP, ROWS])
    with ExitStack() as es:
        t = Ctx(nc, es, "tables")
        raw = t.sb("raw", [TP, ROWS], I32)
        part = t.sb("part", [TP, 1], I32)
        pf = t.sb("pf", [TP, 1])
        hf = t.sb("hf", [TP, 1])
        hx = t.sb("hx", [TP, 1])
        made, step = t.sem("t_made"), t.sem("t_step")
        with nc.Block() as block:

            @block.gpsimd
            def _(pool):
                pool.iota(raw[:, :], [[1, ROWS]], base=0, channel_multiplier=0).then_inc(made, 1)
                pool.iota(part[:, :], [[1, 1]], base=0, channel_multiplier=1).then_inc(made, 1)

            @block.vector
            def _(dve):
                n = [0]

                def do(ins_):
                    n[0] += 1
                    ins_.then_inc(step, 1)
                    dve.wait_ge(step, n[0])

                dve.wait_ge(made, 2)
                do(nc.vector.tensor_copy(pf[:, :], part[:, :]))
                do(nc.vector.tensor_copy(k["steps"][:, :], raw[:, 0:R]))
                do(nc.vector.tensor_copy(k["xpos"][:, :], raw[:, 0:CW]))
                do(nc.vector.tensor_copy(k["ypos"][:, :], raw[:, :]))
                do(nc.vector.tensor_scalar(hf[:, :], pf[:, :], W - 0.5, None, ALU.is_gt))
                do(nc.vector.tensor_scalar(hx[:, :], hf[:, :], -float(W), pf[:, 0:1], ALU.mult, ALU.add))
                do(nc.vector.tensor_scalar(k["xpos"][:, :], k["xpos"][:, :], hx[:, 0:1], -1.0, ALU.add, ALU.add))
                do(nc.vector.tensor_scalar(hf[:, :], hf[:, :], float(HH), -1.0, ALU.mult, ALU.add))
                do(nc.vector.tensor_scalar(k["ypos"][:, :], k["ypos"][:, :], hf[:, 0:1], None, ALU.add))


def zero_stage(nc, regions):
    with ExitStack() as es:
        t = Ctx(nc, es, "zero")
        wide = 64 * C
        z = t.sb("z", [128, wide])
        made, stored = t.sem("made"), t.sem("stored")
        with nc.Block() as block:

            @block.vector
            def _(dve):
                nc.vector.memset(z[:, :], 0.0).then_inc(made, 1)

            @block.sync
            def _(sp):
                sp.wait_ge(made, 1)
                count = 0
                for flat in regions:
                    v = flat.rearrange("(p n) -> p n", p=128)
                    for i in range(0, v.shape[1], wide):
                        n = min(wide, v.shape[1] - i)
                        sp.dma_start(v[:, i:i + n], z[:, 0:n]).then_inc(stored, 16)
                        count += 16
                sp.wait_ge(stored, count)


POOL_TAPS = [6, 7, 8, 5, 4]
DVE_TAPS = [k for k in range(K) if k not in POOL_TAPS]
NPROD = 4
NOM = 4
LOW = 1


def window_pass(nc, k, t, bufs, sems, xp_d, om_d, y_d, row0, col0):
    own, ident = k["own"], k["ident"]
    (om, ab, hat, hym, wd, wp, ad, ap, prod, ring, yprev, yout, mask, negr, zeros, cur, vt) = bufs
    (setup, om_in, yp_in, row_in, masked, abs_ok, hats_ok, blank, hym_ok, pstep, wp_ok, w_done, dstep,
     prod_ok, prod_used, acc_free, y_ok, y_st, tile_done, applied) = sems
    acc = t["acc"]
    xpt = xp_d.tensor

    with nc.Block() as block:

        @block.sync
        def _(sp):
            def load_row(b, u, prior):
                if prior is not None:
                    sp.wait_ge(row_in, prior)
                slot = (u + b * ROWS) % RING
                for h in range(2):
                    pix = (u + (row0 - 1 + h * HH)) * W + (col0 - 1 + PAD + b * NPIX)
                    src = bass.AP(xpt, pix * C, [[C, W], [1, CW * C]])
                    sp.dma_start(ring[h * W:(h + 1) * W, slot, :], src).then_inc(row_in, 16)

            def load_tile(n):
                sp.dma_start(om[:, n % NOM, :], om_d[n, :, :]).then_inc(om_in, 16)
                sp.dma_start(yprev[:, n % NOM, :], y_d[n, :, :]).then_inc(yp_in, 16)

            def store(n):
                hold(sp, y_ok, n + 1, own)
                sp.dma_start(y_d[n, :, :], yout[:, n % 2, :]).then_inc(y_st, 16)

            load_tile(0)
            load_row(0, 0, None)
            for n in range(1, NOM - 1):
                sp.wait_ge(om_in, 16 * n)
                sp.wait_ge(yp_in, 16 * n)
                load_tile(n)
            with sp.Fori(1, RING) as u:
                load_row(0, u, 32 * u)
            for b in range(B):
                def step(j, tile, next_row):
                    n = j + b * HH
                    hold(sp, tile_done, n + 1, own)
                    if tile:
                        sp.wait_ge(om_in, 16 * (n + NOM - 1))
                        sp.wait_ge(yp_in, 16 * (n + NOM - 1))
                        load_tile(n + (NOM - 1))
                    if next_row == "same":
                        load_row(b, j + RING, 32 * (j + RING + b * ROWS))
                    elif next_row == "next":
                        load_row(b + 1, j - (ROWS - RING), 32 * (j + RING + b * ROWS))
                    if type(n) is not int:
                        store(n - 1)

                first = 0
                if b == 0:
                    step(0, True, "same")
                    first = 1
                with sp.Fori(first, ROWS - RING) as j:
                    step(j, True, "same")
                if b + 1 < B:
                    with sp.Fori(ROWS - RING, HH) as j:
                        step(j, True, "next")
                    with sp.Fori(HH - (ROWS - RING), RING) as u:
                        load_row(b + 1, u, 32 * (u + (b + 1) * ROWS))
                else:
                    with sp.Fori(ROWS - RING, HH - NOM + 1) as j:
                        step(j, True, None)
                    with sp.Fori(HH - NOM + 1, HH) as j:
                        step(j, False, None)
            store(B * HH - 1)
            sp.wait_ge(y_st, 16 * B * HH + 1)

        def grid(w):
            return w.rearrange("p (y x g) -> p y x g", y=CW, x=CW)

        @block.scalar
        def _(act):
            act.wait_ge(setup, 1)

            def hats(n):
                hold(act, om_in, n * 16 + 16, own)
                hold(act, w_done, n + 1, own)
                for xy in range(2):
                    for r in range(R):
                        last = nc.scalar.activation(ab[:, n % 2, xy, r, :], om[:, n % NOM, xy * GK:(xy + 1) * GK],
                                                    ACT.Abs, bias=negr[:, xy, r:r + 1], scale=1.0)
                last.then_inc(abs_ok, 1)
                clear_edge(wp[:, n % 2, :], CW - R)
                nc.scalar.activation(wp[:, n % 2, LOW * CW * G:(CW - R) * CW * G],
                                     zeros[:, 0:(CW - R - LOW) * CW * G], ACT.Copy)
                hold(act, abs_ok, n + 1, own)
                nc.scalar.activation(hat[:, n % 2, :, :, :], ab[:, n % 2, :, :, :], ACT.Relu, bias=1.0, scale=-1.0)\
                    .then_inc(hats_ok, 1)

            def clear_edge(w, y):
                right = grid(w)[:, y:y + R, R:CW, :]
                nc.scalar.activation(right.rearrange("p y x g -> p y (x g)"), spread(zeros[:, 0:(CW - R) * G], 1, R),
                                     ACT.Copy)

            def clear_sum(n):
                hold(act, applied, n + 1, own)
                clear_edge(wd[:, n % 2, :], 0)
                nc.scalar.activation(wd[:, n % 2, R * CW * G:CW * CW * G], zeros[:, :], ACT.Copy).then_inc(blank, 1)

            def mask_row(b, u):
                row_n = u + b * ROWS
                hold(act, row_in, 32 * (row_n + 1), own)
                r3 = ring[:, row_n % RING, :].rearrange("p (s c) -> p s c", c=C)
                for s in range(CW):
                    last = nc.scalar.activation(r3[:, s, :], r3[:, s, :], ACT.Copy, scale=mask[:, u, s:s + 1])
                last.then_inc(masked, 1)

            def finish(n):
                hold(act, prod_used, n * CW + (CW + NPROD), own)
                hold(act, y_st, n * 16 + 1, own)
                nc.scalar.activation(yout[:, n % 2, :], acc[:, n % 2, 0:C], ACT.Copy).then_inc(y_ok, 1)
                hold(act, y_ok, n + 1, own)
                act.sem_inc(acc_free, 1)

            for n in range(2):
                hats(n)
                clear_sum(n)
            for b in range(B):
                with act.Fori(0, CW) as u:
                    mask_row(b, u)
                with act.Fori(0, HH - 1 if b + 1 < B else HH - 2) as j:
                    n = j + b * HH
                    hats(n + 2)
                    mask_row(b, j + CW)
                    clear_sum(n + 2)
                    finish(n)
                if b + 1 < B:
                    n = b * HH + HH - 1
                    hats(n + 2)
                    clear_sum(n + 2)
                    finish(n)
            mask_row(B - 1, ROWS - 1)
            for n in range(B * HH - 2, B * HH):
                finish(n)

        def outer(dst, hx, hy, tap):
            return (dst, spread(hx[:, :, tap * G:(tap + 1) * G], 1, R), spread(hy[:, :, tap * G:(tap + 1) * G], 2, R))

        def region(w, tap):
            ky, kx = tap // 3, tap % 3
            return grid(w)[:, ky:ky + R, kx:kx + R, :]

        def box(a):
            return a.rearrange("p (y x g) -> p y x g", y=R, x=R)

        @block.gpsimd
        def _(pool):
            pool.wait_ge(setup, 1)

            PER = 2 * len(POOL_TAPS) - 2
            with pool.Fori(0, B * HH) as n:
                hold(pool, w_done, n + 1, own)
                hold(pool, hats_ok, n + 1, own)
                hx, hy = hat[:, n % 2, 0, :, :], hat[:, n % 2, 1, :, :]
                hm = hym[:, n % 2, :, :]
                pool.tensor_tensor(hm, hy, spread(om[:, n % NOM, 2 * GK:OM], 1, R), ALU.mult).then_inc(hym_ok, 1)
                w = wp[:, n % 2, :]
                hold(pool, hym_ok, n + 1, own)
                o, a, c = outer(region(w, POOL_TAPS[0]), hx, hm, POOL_TAPS[0])
                pool.tensor_tensor(o, a, c, ALU.mult).then_inc(pstep, 1)
                done = 1

                def mul(i):
                    o, a, c = outer(box(ap[:, i % 3, :]), hx, hm, POOL_TAPS[i])
                    pool.tensor_tensor(o, a, c, ALU.mult).then_inc(pstep, 1)

                mul(1)
                done += 1
                for i in range(1, len(POOL_TAPS)):
                    ready = done
                    if i + 1 < len(POOL_TAPS):
                        mul(i + 1)
                        done += 1
                    hold(pool, pstep, n * PER + ready, own)
                    r = region(w, POOL_TAPS[i])
                    last = pool.tensor_tensor(r, r, box(ap[:, i % 3, :]), ALU.add)
                    if i + 1 < len(POOL_TAPS):
                        last.then_inc(pstep, 1)
                        done += 1
                last.then_inc(wp_ok, 1)
                assert done == PER, (done, PER)

        @block.tensor
        def _(pe):
            with pe.Fori(0, B * HH) as n:
                pe.wait_ge(acc_free, n + 1)
                out = acc[:, n % 2, 0:C]
                for s in range(CW):
                    pe.wait_ge(prod_ok, n * CW + (s + 1))
                    for i in range(CW):
                        mm = pe.matmul(out, ident[0:TP, 0:TP], prod[:, (n + s) % NPROD, i * C:(i + 1) * C],
                                       start=(s == 0 and i == 0), stop=(s == CW - 1 and i == CW - 1))
                    mm.then_inc(prod_used, 1)
                    if s == 0:
                        hold(pe, yp_in, 16 * n + 16, own)
                        pe.matmul(out, ident[0:TP, 0:TP], yprev[:, n % NOM, :], start=False, stop=False)

        @block.vector
        def _(dve):
            cnt = [0]

            def do(ins_):
                cnt[0] += 1
                ins_.then_inc(vt["sem"], 1)
                dve.wait_ge(vt["sem"], cnt[0])

            for xy in range(2):
                do(nc.vector.tensor_scalar(negr[:, xy, :], k["steps"][:, :], cur[:, xy:xy + 1], -1.0, ALU.add,
                                           ALU.mult))
            for pos, c0, lim, v in ((k["xpos"], 0, W, vt["x"]), (k["ypos"], 1, H, vt["y"])):
                do(nc.vector.tensor_scalar(v[:, 0, :], pos[:, :], cur[:, c0:c0 + 1], None, ALU.add))
                do(nc.vector.tensor_scalar(v[:, 1, :], v[:, 0, :], -0.5, None, ALU.is_gt))
                do(nc.vector.tensor_scalar(v[:, 0, :], v[:, 0, :], lim - 0.5, None, ALU.is_lt))
                do(nc.vector.tensor_tensor(v[:, 0, :], v[:, 0, :], v[:, 1, :], ALU.mult))
            do(nc.vector.memset(zeros[:, :], 0.0))
            dve.sem_inc(applied, 2)
            dve.sem_inc(w_done, 2)
            dve.sem_inc(prod_used, NPROD)
            dve.sem_inc(acc_free, 2)
            dve.sem_inc(y_st, 1)
            nc.vector.tensor_tensor(mask[:, :, :], spread(vt["y"][:, 0, :], 2, CW), spread(vt["x"][:, 0, :], 1, ROWS),
                                    ALU.mult).then_inc(setup, 2)

            PER = 2 * len(DVE_TAPS) - 1

            def multiply(n, i):
                hx, hm = hat[:, n % 2, 0, :, :], hym[:, n % 2, :, :]
                dst = region(wd[:, n % 2, :], DVE_TAPS[0]) if i == 0 else box(ad[:, i % 3, :])
                o, a, c = outer(dst, hx, hm, DVE_TAPS[i])
                nc.vector.tensor_tensor(o, a, c, ALU.mult).then_inc(dstep, 1)

            def add(n, i, ready):
                dve.wait_ge(dstep, n * PER + ready)
                r = region(wd[:, n % 2, :], DVE_TAPS[i])
                nc.vector.tensor_tensor(r, r, box(ad[:, i % 3, :]), ALU.add).then_inc(dstep, 1)

            def begin(n):
                hold(dve, hym_ok, n + 1, own)
                hold(dve, blank, n + 1, own)
                multiply(n, 0)

            def end(n):
                hold(dve, dstep, n * PER + PER, own)
                hold(dve, wp_ok, n + 1, own)
                low = wd[:, n % 2, LOW * CW * G:]
                nc.vector.tensor_tensor(low, low, wp[:, n % 2, LOW * CW * G:], ALU.add).then_inc(w_done, 1)

            steps = [begin, lambda n: multiply(n, 1), lambda n: multiply(n, 2), lambda n: add(n, 1, 2),
                     lambda n: multiply(n, 3), lambda n: add(n, 2, 4), lambda n: add(n, 3, 6), end]
            assert len(DVE_TAPS) == 4 and len(steps) == CW - 1

            def apply(n, j, b, next_tile):
                hold(dve, masked, j + (CW + b * ROWS), own)
                hold(dve, w_done, n + 3, own)
                for s in range(CW):
                    dve.wait_ge(prod_used, n * CW + (s + 1))
                    slot = (j + (s + b * ROWS)) % RING
                    nc.vector.tensor_tensor(
                        prod[:, (n + s) % NPROD, :].rearrange("p (a c) -> p a c", c=GC),
                        ring[:, slot, :].rearrange("p (a c) -> p a c", c=GC),
                        spread(wd[:, n % 2, s * CW * G:(s + 1) * CW * G], 2, GC), ALU.mult).then_inc(prod_ok, 1)
                    if next_tile and s >= 1:
                        steps[s - 1](n + 1)
                dve.wait_ge(prod_ok, n * CW + CW)
                dve.sem_inc(tile_done, 1)
                dve.sem_inc(applied, 1)

            for step in steps:
                step(0)
            for b in range(B):
                with dve.Fori(0, HH if b + 1 < B else HH - 1) as j:
                    apply(j + b * HH, j, b, True)
            apply(B * HH - 1, HH - 1, B - 1, False)


def deformable_stage(nc, k, xp_d, om_d, y_d, base, counts):
    with ExitStack() as es:
        t = Ctx(nc, es, "deform")
        names = ("setup om_loaded yprev_loaded row_loaded row_masked abs_ready hats_ready grids_blank "
                 "hym_ready pool_step pool_weights_ready weights_done dve_step prod_ready prod_used "
                 "acc_free y_ready y_stored tile_done applied win_step").split()
        sems = [t.sem(s) for s in names]
        NW = CW * CW * G
        cur = t.sb("cur", [TP, 2])
        vt = {"x": t.sb("vx", [TP, 2, CW]), "y": t.sb("vy", [TP, 2, ROWS]), "sem": sems[-1]}
        zeros = t.sb("zeros", [TP, (CW - R) * CW * G])
        bufs = (t.sb("om", [TP, NOM, OM]), t.sb("ab", [TP, 2, 2, R, GK]), t.sb("hat", [TP, 2, 2, R, GK]),
                t.sb("hym", [TP, 2, R, GK]), t.sb("wd", [TP, 2, NW]), t.sb("wp", [TP, 2, NW]),
                t.sb("ad", [TP, 3, R * R * G]), t.sb("ap", [TP, 3, R * R * G]), t.sb("prod", [TP, NPROD, CW * C]),
                t.sb("ring", [TP, RING, CW * C]), t.sb("yprev", [TP, NOM, C]), t.sb("yout", [TP, 2, C]),
                t.sb("mask", [TP, ROWS, CW]), t.sb("negr", [TP, 2, R]), zeros, cur, vt)
        acc = t.ps("acc", [TP, 2, 512])

        def move(body):
            with nc.Block() as block:
                @block.vector
                def _(dve):
                    body(dve)

        def restart(dve):
            nc.vector.tensor_copy(cur[:, :], base[:, :])
        def restart_x(dve):
            nc.vector.tensor_copy(cur[:, 0:1], base[:, 0:1])

        move(restart)
        why = "a count of windows and a whole offset, bounded by the clamp of the offsets"
        lim = int(OFFMAX)
        nx, ny = (nc.values_load(counts[0:1, i:i + 1], min_val=1, max_val=(2 * lim + 2) // R + 1,
                                 skip_runtime_bounds_check_because=why) for i in range(2))
        x0, y0 = (nc.values_load(counts[0:1, i:i + 1], min_val=-lim, max_val=lim,
                                 skip_runtime_bounds_check_because=why) for i in (2, 3))
        with nc.Fori(0, ny) as iy:
            with nc.Fori(0, nx) as ix:
                window_pass(nc, k, {"acc": acc}, bufs, sems[:-1], xp_d, om_d, y_d, 
                            (y0 + iy * R).with_bounds(min_val=-lim, max_val=lim + 1),
                            (x0 + ix * R).with_bounds(min_val=-lim, max_val=lim + 1))
                for s in sems + [k["own"]]:
                    nc.gpsimd.sem_clear(s)
                nc.all_engine_barrier()
                move(lambda dve: nc.vector.tensor_scalar(cur[:, 0:1], cur[:, 0:1], float(R), None, ALU.add))
            move(lambda dve: nc.vector.tensor_scalar(cur[:, 1:2], cur[:, 1:2], float(R), None, ALU.add))
            move(restart_x)


def rows_stage(nc, k, x, y_d, t_d, xc_d):
    own, ident = k["own"], k["ident"]
    with ExitStack() as es:
        t = Ctx(nc, es, "rows")
        y = t.sb("y", [TP, 2, QT, C])
        xr = t.sb("x", [TP, 2, QT, C])
        turned = t.sb("turned", [C, 2, QT * TP])
        x2t = t.sb("x2t", [C, 2, QT * TP])
        hid = t.sb("hid", [C, 2, QT * TP])
        z = t.sb("z", [TP, 2, QT, C])
        z2 = t.sb("z2", [TP, 2, QT, C])
        x2 = t.sb("x2", [TP, 2, QT, C])
        x2b = t.sb("x2b", [TP, 2, QT, C])
        tok = t.sb("tok", [TP, 2, QT, C])
        xc = t.sb("xc", [TP, 2, QT, C])
        st = t.sb("st", [TP, 3, QT, 6])
        mv = t.sb("mv", [TP, 2, 3, QT, 2])
        ve = t.sb("ve", [TP, 2, 3, QT])
        rs = t.sb("rs", [TP, 2, 3, QT])
        half = t.sb("half", [TP, QT])
        gg = [t.sb(f"gg{i}", [TP, C]) for i in range(2)]
        gb = [t.sb(f"gb{i}", [TP, C]) for i in range(2)]
        ps_t = [t.ps(f"ps_t{i}", [C, 512]) for i in range(2)]
        ps_o = [t.ps(f"ps_o{i}", [TP, 512]) for i in range(2)]
        ps_f = [t.ps(f"ps_f{i}", [C, 512]) for i in range(2)]
        ps_m = [t.ps(f"ps_m{i}", [TP, 512]) for i in range(2)]
        y_in, x_in, tok_st, xc_st = ([t.sem(f"{s}{p}") for p in range(2)] for s in (
            "y_loaded", "x_loaded", "tokens_stored", "xc_stored"))
        z_ok, stat, agg, eps, rstd, normed, scaled = ([t.sem(f"{s}{i}") for i in range(3)] for s in (
            "z_ready", "stats_ready", "mean_var_ready", "var_eps_ready", "rstd_ready", "normalised", "scaled"))
        (yT, yT_ok, o_ps, x2_ok, x2T, x2T_ok, f_ps, hid_ok, m_ps, xb_ok, x2b_ok, tok_ok, xc_ok, cst, half_ok) = [
            t.sem(s) for s in (
                "yT_in_psum yT_ready o_in_psum x2_ready x2T_in_psum x2T_ready f_in_psum hid_ready m_in_psum "
                "x_plus_bias_ready x2_plus_bias_ready tokens_ready xc_ready constants_ready half_ready").split()]
        LAG1, LAG2, LAG_TOK, LAG_XC = 2, 3, 3, 4
        FIRST, LAST = -1, NB + LAG_XC
        LOOP0, LOOP1 = LAG_XC, NB - 2

        def run(eng, step):
            for n in range(FIRST, LOOP0):
                step(n // 2, n % 2, n)
            with eng.Fori(LOOP0 // 2, LOOP1 // 2) as i:
                for p in range(2):
                    step(i, p, None)
            for n in range(LOOP1, LAST):
                step(n // 2, n % 2, n)

        def there(n, lag):
            return n is None or 0 <= n - lag < NB

        def batch(i, p, lag):
            return i * 2 + (p - lag), (p - lag) % 2, i + (p - lag) // 2

        with nc.Block() as block:

            @block.sync
            def _(sp):
                with sp.Fori(0, NB // 2) as i:
                    for p in range(2):
                        n = i * 2 + p
                        hold(sp, x2_ok, n + 1, own)
                        sp.dma_start(y[:, p, :, :], y_d[bass.ds(n * QT, QT), :, :].rearrange("t p c -> p t c"))\
                            .then_inc(y_in[p], 16)
                        for h in range(2):
                            src = bass.AP(x.tensor, ((n // NQ) * NPIX + (n % NQ) * (QT * W) + h * HH * W) * C,
                                          [[C, W], [W * C, QT], [1, C]])
                            sp.dma_start(xr[h * W:(h + 1) * W, p, :, :], src).then_inc(x_in[p], 16)

            @block.gpsimd
            def _(pool):
                pool.memset(half[:, :], -0.5).then_inc(half_ok, 1)
                pool.wait_ge(half_ok, 1)
                pool.wait_ge(cst, 2)

                def step(i, p, n):
                    if there(n, 0):
                        m, q, used = batch(i, p, 0)
                        hold(pool, x_in[q], used * 32 + 32, own)
                        pool.tensor_tensor(xr[:, q, :, :], xr[:, q, :, :], spread(gb[0][:, :], 1, QT),
                                           ALU.add).then_inc(xb_ok, 1)
                    if there(n, 1):
                        m, q, used = batch(i, p, 1)
                        hold(pool, x2_ok, m + 3, own)
                        pool.tensor_tensor(x2b[:, q, :, :], x2[:, q, :, :], spread(gb[1][:, :], 1, QT),
                                           ALU.add).then_inc(x2b_ok, 1)
                    for s, lag in ((2, LAG2), (0, 0), (1, LAG1)):
                        if there(n, lag):
                            m, q, used = batch(i, p, lag)
                            hold(pool, agg[s], m + 1, own)
                            pool.tensor_scalar(ve[:, q, s, :], mv[:, q, s, :, 1], EPS, None, ALU.add)\
                                .then_inc(eps[s], 1)
                            hold(pool, eps[s], m + 1, own)
                            pool.tensor_tensor(rs[:, q, s, :], ve[:, q, s, :], half[:, :], ALU.pow)\
                                .then_inc(rstd[s], 1)

                run(pool, step)

            @block.tensor
            def _(pe):
                def step(i, p, n):
                    after, before = there(n, -1), there(n, 1)
                    if before:
                        m, q, used = batch(i, p, 1)
                        hold(pe, x2_ok, m + 3, own)
                        for j in range(QT):
                            mm = pe.transpose(ps_t[q][:, j * TP:(j + 1) * TP], x2[:, q, j, :], ident[0:TP, 0:TP])
                        mm.then_inc(x2T, 1)
                        hold(pe, x2T_ok, m + 3, own)
                        pe.matmul(ps_f[q][:, 0:QT * TP], k["w_fc1"][:, :], x2t[:, q, :], start=True, stop=True)\
                            .then_inc(f_ps, 1)
                    if after:
                        a, r, a_used = batch(i, p, -1)
                        hold(pe, y_in[r], a_used * 16 + 16, own)
                        hold(pe, x2T_ok, a + 1, own)
                        for j in range(QT):
                            mm = pe.transpose(ps_t[r][:, j * TP:(j + 1) * TP], y[:, r, j, :], ident[0:TP, 0:TP])
                        mm.then_inc(yT, 1)
                    if before:
                        hold(pe, hid_ok, m + 1, own)
                        for j in range(QT):
                            mm = pe.matmul(ps_m[q][:, j * C:(j + 1) * C], hid[:, q, j * TP:(j + 1) * TP],
                                           k["w_fc2"][:, :], start=True, stop=True)
                        mm.then_inc(m_ps, 1)
                    if after:
                        hold(pe, yT_ok, a + 1, own)
                        for j in range(QT):
                            mm = pe.matmul(ps_o[r][:, j * C:(j + 1) * C], turned[:, r, j * TP:(j + 1) * TP],
                                           k["w_out"][:, :], start=True, stop=True)
                        mm.then_inc(o_ps, 1)

                run(pe, step)

            @block.scalar
            def _(act):
                act.sem_inc(x2T_ok, 2)

                def step(i, p, n):
                    if there(n, 1):
                        m, q, used = batch(i, p, 1)
                        hold(act, x2T, m + 1, own)
                        nc.scalar.activation(x2t[:, q, :], ps_t[q][:, 0:QT * TP], ACT.Copy).then_inc(x2T_ok, 1)
                        hold(act, f_ps, m + 1, own)
                        nc.scalar.activation(hid[:, q, :], ps_f[q][:, 0:QT * TP], ACT.Gelu,
                                             bias=k["b_fc1"][:, 0:1], scale=1.0).then_inc(hid_ok, 1)
                    if there(n, -1):
                        m, q, used = batch(i, p, -1)
                        hold(act, yT, m + 1, own)
                        nc.scalar.activation(turned[:, q, :], ps_t[q][:, 0:QT * TP], ACT.Copy).then_inc(yT_ok, 1)
                    if there(n, LAG_TOK):
                        m, q, used = batch(i, p, LAG_TOK)
                        hold(act, tok_ok, m + 1, own)
                        act.dma_start(t_d[bass.ds(m * QT, QT), :, :].rearrange("t p c -> p t c"), tok[:, q, :, :])\
                            .then_inc(tok_st[q], 16)
                    if there(n, LAG_XC):
                        m, q, used = batch(i, p, LAG_XC)
                        hold(act, xc_ok, m + 1, own)
                        act.dma_start(xc_d[bass.ds(m * QT, QT), :, :].rearrange("t p c -> p t c"), xc[:, q, :, :])\
                            .then_inc(xc_st[q], 16)

                run(act, step)
                for p in range(2):
                    act.wait_ge(tok_st[p], 8 * NB + 1)
                    act.wait_ge(xc_st[p], 8 * NB + 1)

            @block.vector
            def _(dve):
                dve.sem_inc(x2_ok, 2)
                for s in (*tok_st, *xc_st):
                    dve.sem_inc(s, 1)
                for s, (gm, g, b_) in enumerate((("gamma1", "ln1_g", "ln1_b"), ("gamma2", "ln2_g", "ln2_b"))):
                    nc.vector.tensor_tensor(gg[s][:, :], k[gm][0:TP, :], k[g][0:TP, :], ALU.mult)
                    nc.vector.tensor_tensor(gb[s][:, :], k[gm][0:TP, :], k[b_][0:TP, :], ALU.mult).then_inc(cst, 1)
                dve.wait_ge(cst, 2)

                def add_bias(s, m, ps, bias, ready):
                    hold(dve, ready, m + 1, own)
                    nc.vector.tensor_tensor(z[:, s, :, :], ps[:, :].rearrange("p (t c) -> p t c", c=C),
                                            spread(k[bias][0:TP, :], 1, QT), ALU.add).then_inc(z_ok[s], 1)

                def stats(s, src):
                    for q in range(QT):
                        last = nc.vector.bn_stats(st[:, s, q, :], src[:, q, :])
                    last.then_inc(stat[s], 1)

                def aggregate(s, m, p):
                    hold(dve, stat[s], m + 1, own)
                    for q in range(QT):
                        last = nc.vector.bn_aggr(mv[:, p, s, q, :], st[:, s, q, :])
                    last.then_inc(agg[s], 1)

                def normalise(s, m, p, dst, src):
                    hold(dve, rstd[s], m + 1, own)
                    for q in range(QT):
                        last = nc.vector.tensor_scalar(dst[:, q, :], src[:, q, :], mv[:, p, s, q, 0:1],
                                                       rs[:, p, s, q:q + 1], ALU.subtract, ALU.mult)
                    return last

                def scale(s, m):
                    hold(dve, normed[s], m + 1, own)
                    nc.vector.tensor_tensor(z2[:, s, :, :], z2[:, s, :, :], spread(gg[s][:, :], 1, QT), ALU.mult)\
                        .then_inc(scaled[s], 1)

                def step(i, p, n):
                    on0, on1, on2 = there(n, 0), there(n, LAG1), there(n, LAG2)
                    m0, p0, _u = batch(i, p, 0)
                    m1, p1, used1 = batch(i, p, LAG1)
                    m2, p2, used2 = batch(i, p, LAG2)
                    if on2:
                        hold(dve, tok_ok, m2 + 1, own)
                        stats(2, tok[:, p2])
                    if on0:
                        add_bias(0, m0, ps_o[p0], "b_out", o_ps)
                    if on2:
                        aggregate(2, m2, p2)
                    if on0:
                        hold(dve, z_ok[0], m0 + 1, own)
                        stats(0, z[:, 0])
                    if on1:
                        add_bias(1, m1, ps_m[p1], "b_fc2", m_ps)
                    if on0:
                        aggregate(0, m0, p0)
                    if on1:
                        hold(dve, z_ok[1], m1 + 1, own)
                        stats(1, z[:, 1])
                    if on2:
                        hold(dve, xc_st[p2], used2 * 16 + 1, own)
                        normalise(2, m2, p2, xc[:, p2], tok[:, p2]).then_inc(xc_ok, 1)
                    if on1:
                        aggregate(1, m1, p1)
                    if on0:
                        normalise(0, m0, p0, z2[:, 0], z[:, 0]).then_inc(normed[0], 1)
                        scale(0, m0)
                    if on1:
                        normalise(1, m1, p1, z2[:, 1], z[:, 1]).then_inc(normed[1], 1)
                        scale(1, m1)
                        hold(dve, x2b_ok, m1 + 1, own)
                        hold(dve, tok_st[p1], used1 * 16 + 1, own)
                        hold(dve, scaled[1], m1 + 1, own)
                        nc.vector.tensor_tensor(tok[:, p1, :, :], z2[:, 1, :, :], x2b[:, p1, :, :], ALU.add)\
                            .then_inc(tok_ok, 1)
                    if on0:
                        hold(dve, xb_ok, m0 + 1, own)
                        hold(dve, scaled[0], m0 + 1, own)
                        nc.vector.tensor_tensor(x2[:, p0, :, :], z2[:, 0, :, :], xr[:, p0, :, :], ALU.add)\
                            .then_inc(x2_ok, 1)

                run(dve, step)


C4 = C // 4
NCH = 4
CK = NPIX // NCH
MT = CK // TP
ST = 4
NS = HH // ST
BK = CK // 2
NMG = NPIX // BK
EPS_SUM = 1e-6
NE = 3
BF16 = mybir.dt.bfloat16
NEXT_QUERY = 0
BN_EPS = 1e-5


def attention_stage(nc, k, ins, xc_d, t_d, t4_d):
    own, ident = k["own"], k["ident"]
    with ExitStack() as es:
        t = Ctx(nc, es, "attn")
        wraw = t.sb("wraw", [128, C])
        wq, wk = (t.sb(w, [C, 4, C4]) for w in ("wq", "wk"))
        ones = t.sb("ones", [C, TP])
        wt = t.sb("wt", [C, C])
        wtt = t.sb("wtt", [C, C])
        diag = t.sb("diag", [C, C])
        shift = t.sb("shift", [TP, C])
        bn = t.sb("bn", [C, 5])
        bs = t.sb("bs", [C, 2])
        bneg = t.sb("bneg", [C, 1])
        xa = t.sb("xa", [TP, HH, C])
        xct = t.sb("xct", [C, NPIX])
        ka, kb = t.sb("ka", [4 * C4, NPIX], BF16), t.sb("kb", [2 * C4, NPIX], BF16)
        qa, qb = t.sb("qa", [4 * C4, 2, ST * TP], BF16), t.sb("qb", [2 * C4, 2, ST * TP], BF16)
        k_mid, q_mid = t.sb("k_mid", [4 * C4, 2, QT * TP], BF16), t.sb("q_mid", [4 * C4, ST * TP], BF16)
        q_rest = t.sb("q_rest", [4 * C4, ST * TP])
        prob = t.sb("prob", [TP, 2, ST, NPIX])
        xs = t.sb("xs", [TP, 2, ST, NCH, C])
        xr = t.sb("xr", [C, NPIX])
        cs = t.sb("cs", [TP, NPIX])
        nm = t.sb("nm", [TP, 2, ST, NCH])
        zs = t.sb("zs", [TP, 2, ST, NCH])
        wz = t.sb("wz", [TP, 2, ST, NCH])
        ez = t.sb("ez", [TP, 2, ST, NCH])
        dm = t.sb("dm", [TP, 2, ST, NCH])
        mn = t.sb("mn", [TP, 2, ST])
        zt = t.sb("zt", [TP, 2, ST])
        zr = t.sb("zr", [TP, 2, ST])
        k_rest = t.sb("k_rest", [4 * C4, 2, QT * TP])
        rc = t.sb("rc", [TP, HH])
        un = t.sb("un", [TP, 2, QT, C])
        tin = t.sb("tin", [TP, 2, QT, C])
        tout = t.sb("tout", [TP, 2, QT, C])
        ps_e = [t.ps(f"ps_e{i}", [C, 2, 512]) for i in range(NE)]
        ps_r = [t.ps(f"ps_r{i}", [C, 512]) for i in range(2)]
        (w_in, xa_in, wT, w_ok, bstep, bn_done, xT, xT_ok, k_ps, k_hi, k_ok, k_step, k_low, q_ps, q_hi, q_left,
         q_step, qs_ok, e_ps, mx_ok, ex_ok, sstep, dm_ok,
         ez_ok, w_rdy, xs_ok, r_ps, r_ok, zeroed, cstep, c_ps, pstep, u_ps, u_sum, u_ok, tin_ok, t_ok,
         image_done, const_ok) = [
             t.sem(s) for s in (
                 "weights_loaded xa_loaded weights_turned weights_ready bn_step bn_done xT_in_psum xT_ready "
                 "keys_in_psum keys_rounded keys_rest_ready keys_step keys_ready query_in_psum query_rounded "
                 "query_rest_ready query_step query_ready energy_in_psum max_ready exp_ready soft_step "
                 "below_ready rescale_ready chunk_weights_ready xs_ready sums_in_psum sums_added sums_zeroed "
                 "column_step columns_in_psum post_step u_in_psum u_summed u_ready "
                 "residual_ready tokens_ready image_done constants_ready")
             .split()]
        t_in, t_st = ([t.sem(f"{s}{p}") for p in range(2)] for s in ("t_loaded", "t_stored"))

        def uses(p, b, g):
            return b * ((NQ + 1 - p) // 2) + g // 2

        def steps():
            order = [(j / 16.0, 0, j) for j in range(ST * NCH)] + \
                    [(0.28 + 0.72 * g / NMG, 1, g) for g in range(NMG)]
            return [(kind, j) for _, kind, j in sorted(order)]

        ENERGY, SUMS = 0, 1

        def superblocks(eng, b, part):
            part(0, 0, None, None)
            with eng.Fori(0, NS // 2) as i:
                part(i * 2 + 1, 1, i * 2, 0)
                part(i * 2 + 2, 0, i * 2 + 1, 1)
            part(None, None, NS - 1, 0)

        def energies(e, j):
            return ps_e[(j + e) % NE]

        def overall(b, s):
            return None if s is None else s + b * NS

        def interleaved(s_e, s_r):
            return [(kind, j) for kind, j in steps()
                    if (kind == ENERGY and s_e is not None) or (kind == SUMS and s_r is not None)]

        with nc.Block() as block:

            @block.sync
            def _(sp):
                sp.dma_start(wraw[0:C4, :], ins["L1_attn_Wq"]).then_inc(w_in, 16)
                sp.dma_start(wraw[C4:2 * C4, :], ins["L1_attn_Wk"]).then_inc(w_in, 16)
                for i, name in enumerate(("gamma", "beta", "bn_mean", "bn_var", "bt")):
                    sp.dma_start(bn[:, i:i + 1], col(ins["L1_attn_" + name])).then_inc(w_in, 16)
                sp.dma_start(wt[:, :], ins["L1_attn_Wt"]).then_inc(w_in, 16)
                with sp.Fori(0, B) as b:
                    hold(sp, image_done, b + 1, own)
                    sp.dma_start(xa[:, :, :], xc_d[bass.ds(b * HH, HH), :, :].rearrange("t p c -> p t c"))\
                        .then_inc(xa_in, 16)
                    for g in range(NQ):
                        n = b * NQ + g
                        hold(sp, t_ok, n + (2 if g == 0 else 1), own)
                        sp.dma_start(tin[:, g % 2, :, :], t_d[bass.ds(n * QT, QT), :, :].rearrange("t p c -> p t c"))\
                            .then_inc(t_in[g % 2], 16)

            @block.gpsimd
            def _(pool):
                pool.memset(bneg[:, :], -0.5).then_inc(const_ok, 1)
                pool.memset(ones[:, :], 1.0).then_inc(const_ok, 1)
                pool.wait_ge(w_in, 128)
                pool.wait_ge(const_ok, 2)
                pool.tensor_scalar(bs[:, 0:1], bn[:, 3:4], BN_EPS, None, ALU.add).then_inc(bstep, 1)
                pool.wait_ge(bstep, 1)
                pool.tensor_tensor(bs[:, 0:1], bs[:, 0:1], bneg[:, :], ALU.pow).then_inc(bstep, 1)
                with pool.Fori(0, B) as b:
                    hold(pool, image_done, b + 1, own)
                    pool.memset(xr[:, :], 0.0)
                    pool.memset(cs[:, :], 0.0).then_inc(zeroed, 1)
                    hold(pool, xa_in, b * 16 + 16, own)

                    def part(s_e, e, s_r, r):
                        if s_r is not None:
                            hold(pool, w_rdy, overall(b, s_r) + 1, own)
                            for i in range(ST):
                                tile = s_r * ST + i
                                last = pool.tensor_tensor(xs[:, r, i, :, :], spread(xa[:, tile, :], 1, NCH),
                                                          spread(wz[:, r, i, :], 2, C), ALU.mult)
                            last.then_inc(xs_ok, 1)

                    superblocks(pool, b, part)
                    for g in range(NQ):
                        hold(pool, t_in[g % 2], uses(g % 2, b, g) * 16 + 16, own)
                        pool.tensor_tensor(tin[:, g % 2, :, :], tin[:, g % 2, :, :], xa[:, g * QT:(g + 1) * QT, :],
                                           ALU.add).then_inc(tin_ok, 1)

            @block.tensor
            def _(pe):
                pe.wait_ge(w_in, 128)
                pe.transpose(ps_e[0][:, 0, 0:2 * C4], wraw[0:2 * C4, :], ident[0:2 * C4, 0:2 * C4]).then_inc(wT, 1)
                pe.wait_ge(bn_done, 3)
                pe.transpose(ps_e[1][:, 0, 0:C], wt[:, :], ident[:, :])
                pe.wait_ge(const_ok, 2)
                pe.matmul(ps_e[2][0:TP, 0, 0:C], ones[:, :], diag[:, :], start=True, stop=True).then_inc(wT, 1)
                pe.wait_ge(w_ok, 1)
                with pe.Fori(0, B) as b:
                    hold(pe, xa_in, b * 16 + 16, own)
                    hold(pe, t_ok, b * NQ + 2, own)

                    def turn_x(g):
                        hold(pe, xT_ok, b * NQ + g + 1, own)
                        for i in range(QT):
                            mm = pe.transpose(ps_r[g % 2][:, i * TP:(i + 1) * TP], xa[:, g * QT + i, :],
                                              ident[0:TP, 0:TP])
                        mm.then_inc(xT, 1)

                    def keys(g):
                        hold(pe, xT_ok, b * NQ + g + 3, own)
                        hold(pe, k_ok, b * NQ + g + 1, own)
                        pe.matmul(ps_e[g % 2][:, 0, 0:QT * TP], wk[:, :, :].rearrange("c a n -> c (a n)"),
                                  xct[:, g * QT * TP:(g + 1) * QT * TP], start=True, stop=True).then_inc(k_ps, 1)

                    def query(s):
                        pe.matmul(ps_r[1][:, 0:ST * TP], wq[:, :, :].rearrange("c a n -> c (a n)"),
                                  xct[:, bass.ds((s % NS) * (ST * TP), ST * TP)], start=True, stop=True)\
                            .then_inc(q_ps, 1)

                    turn_x(0)
                    for g in range(NQ):
                        if g + 1 < NQ:
                            turn_x(g + 1)
                        keys(g)
                    hold(pe, k_ok, b * NQ + NQ + 2, own)
                    query(0)
                    hold(pe, k_low, b * NQ + NQ + 2, own)
                    hold(pe, k_step, (b + 1) * (2 * NQ), own)

                    def part(s_e, e, s_r, r):
                        if s_e is not None:
                            hold(pe, qs_ok, b * (NS + 1) + (s_e + 2), own)
                        s_n = s_e
                        s_e, s_r = overall(b, s_e), overall(b, s_r)
                        for kind, j in interleaved(s_e, s_r):
                            if kind == ENERGY:
                                i, ch = j // NCH, j % NCH
                                pe.wait_ge(ex_ok, s_e * (ST * NCH) + (j + 1 + (e == 0 and j < 2)))
                                q_ = slice(i * TP, (i + 1) * TP)
                                for qp, kp in ((qa, ka), (qb, kb)):
                                    for hf in range(2):
                                        m0 = ch * CK + hf * BK
                                        mm = pe.matmul(energies(e, j)[0:TP, hf, 0:BK], qp[:, e, q_], kp[:, m0:m0 + BK],
                                                       start=qp is qa, stop=qp is qb)
                                mm.then_inc(e_ps, 1)
                                if j == NEXT_QUERY:
                                    if s_r is not None:
                                        hold(pe, r_ok, s_r * NMG + 2, own)
                                    query(s_n + 1)
                            else:
                                if j == 0:
                                    hold(pe, xs_ok, s_r + 1, own)
                                if j == 1 and s_n is not None:
                                    hold(pe, q_left, b * (NS + 1) + (s_n + 2), own)
                                hold(pe, r_ok, s_r * NMG + (j + 1), own)
                                for i in range(ST):
                                    mm = pe.matmul(ps_r[j % 2][:, 0:BK], xs[:, r, i, j // 2, :],
                                                   prob[:, r, i, j * BK:(j + 1) * BK], start=(i == 0),
                                                   stop=(i == ST - 1))
                                mm.then_inc(r_ps, 1)

                    superblocks(pe, b, part)

                    def project(g):
                        hold(pe, u_ok, b * NQ + g + 1, own)
                        for hf, src in enumerate((xr, xct)):
                            for i in range(QT):
                                m = g * QT + i
                                mm = pe.matmul(ps_e[g % 2][0:TP, hf, i * C:(i + 1) * C], src[:, m * TP:(m + 1) * TP],
                                               wtt[:, :], start=True, stop=True)
                        mm.then_inc(u_ps, 1)

                    hold(pe, qs_ok, b * (NS + 1) + (NS + 2), own)
                    hold(pe, r_ok, (b + 1) * (NS * NMG) + 2, own)
                    hold(pe, ex_ok, (b + 1) * (NS * ST * NCH) + NE, own)
                    project(0)
                    project(1)
                    hold(pe, cstep, (b + 1) * (NS * ST * NCH) + 1, own)
                    for m in range(HH):
                        mm = pe.matmul(ps_r[0][0:TP, m:m + 1], cs[:, m * TP:(m + 1) * TP], ones[0:TP, 0:1],
                                       start=True, stop=True)
                    mm.then_inc(c_ps, 1)
                    for g in range(2, NQ):
                        project(g)

            @block.scalar
            def _(act):
                act.sem_inc(xT_ok, 2)
                act.sem_inc(ex_ok, NE)
                act.wait_ge(wT, 2)
                for i, w in enumerate((wq, wk)):
                    nc.scalar.activation(w[:, :, :], spread(ps_e[0][:, 0, i * C4:(i + 1) * C4], 1, 4), ACT.Copy)
                nc.scalar.activation(shift[:, :], ps_e[2][0:TP, 0, 0:C], ACT.Copy)
                nc.scalar.activation(wtt[:, :], ps_e[1][:, 0, 0:C], ACT.Copy).then_inc(w_ok, 1)
                with act.Fori(0, B) as b:
                    def keys_mid(g):
                        hold(act, k_ok, b * NQ + g + 3, own)
                        for blk in (1, 3):
                            rows = slice(blk * C4, (blk + 1) * C4)
                            last = nc.scalar.activation(ka[rows, g * QT * TP:(g + 1) * QT * TP],
                                                        k_rest[rows, g % 2, :], ACT.Copy)
                        last.then_inc(k_low, 1)

                    def query_mid(s, slot):
                        hold(act, q_left, b * (NS + 1) + (s + 1), own)
                        lo, mid = slice(C4, 2 * C4), slice(2 * C4, 4 * C4)
                        nc.scalar.activation(q_mid[lo, :], q_rest[lo, :], ACT.Copy)
                        nc.scalar.activation(qa[mid, slot, :], q_rest[mid, :], ACT.Copy).then_inc(q_step, 1)

                    def keys(g):
                        hold(act, k_ps, b * NQ + g + 1, own)
                        cols = slice(g * QT * TP, (g + 1) * QT * TP)
                        nc.scalar.activation(kb[C4:2 * C4, cols], ps_e[g % 2][C4:2 * C4, 0, 0:QT * TP], ACT.Copy)
                        nc.scalar.activation(ka[:, cols], ps_e[g % 2][:, 0, 0:QT * TP], ACT.Copy).then_inc(k_hi, 1)

                    for g in range(NQ):
                        n = b * NQ + g
                        hold(act, xT, n + 1, own)
                        nc.scalar.activation(xct[:, g * QT * TP:(g + 1) * QT * TP], ps_r[g % 2][:, 0:QT * TP], ACT.Copy)\
                            .then_inc(xT_ok, 1)
                        if g >= 1:
                            keys(g - 1)
                        if g >= 2:
                            keys_mid(g - 2)
                    keys(NQ - 1)
                    keys_mid(NQ - 2)
                    keys_mid(NQ - 1)

                    def query(s, slot):
                        hold(act, q_ps, b * (NS + 1) + (s + 1), own)
                        nc.scalar.activation(qb[0:C4, slot, :], ps_r[1][0:C4, 0:ST * TP], ACT.Copy)
                        nc.scalar.activation(qa[:, slot, :], ps_r[1][:, 0:ST * TP], ACT.Copy).then_inc(q_hi, 1)

                    query(0, 0)
                    query_mid(0, 0)

                    def rescale(S, slot):
                        hold(act, dm_ok, S + 1, own)
                        nc.scalar.activation(ez[:, slot, :, :], dm[:, slot, :, :], ACT.Exp).then_inc(ez_ok, 1)

                    def part(s_e, e, s_r, r):
                        s_n = s_e
                        s_e, s_r = overall(b, s_e), overall(b, s_r)
                        if s_r is not None:
                            rescale(s_r, r)
                        if s_e is None:
                            return
                        if s_r is not None:
                            hold(act, r_ps, s_r * NMG + 1, own)
                            hold(act, cstep, s_r * (ST * NCH) + 1, own)
                        for j in range(ST * NCH):
                            i, ch = j // NCH, j % NCH
                            act.wait_ge(mx_ok, s_e * (ST * NCH) + (j + 1))
                            nc.scalar.activation(prob[:, e, i, ch * CK:(ch + 1) * CK]
                                                 .rearrange("p (a f) -> p a f", a=2), energies(e, j)[0:TP, :, 0:BK],
                                                 ACT.Exp, bias=nm[:, e, i, ch:ch + 1], scale=1.0,
                                                 accum_out=zs[:, e, i, ch:ch + 1]).then_inc(ex_ok, 1)
                            if j == NEXT_QUERY + 1:
                                query(s_n + 1, 1 - e)
                            elif j == NEXT_QUERY + 3:
                                query_mid(s_n + 1, 1 - e)

                    superblocks(act, b, part)

                    def store(g):
                        n = b * NQ + g
                        hold(act, t_ok, n + 3, own)
                        for h in range(2):
                            dst = bass.AP(t4_d.tensor, (b * NPIX + (g * QT * W + h * HH * W)) * C,
                                          [[C, W], [W * C, QT], [1, C]])
                            act.dma_start(dst, tout[h * W:(h + 1) * W, g % 2, :, :]).then_inc(t_st[g % 2], 16)

                    for g in range(NQ):
                        store(g)
                for p in range(2):
                    act.wait_ge(t_st[p], 32 * B * ((NQ + 1 - p) // 2) + 1)

            @block.vector
            def _(dve):
                dve.sem_inc(image_done, 1)
                dve.sem_inc(k_ok, 2)
                dve.sem_inc(k_low, 2)
                dve.sem_inc(qs_ok, 1)
                dve.sem_inc(u_ok, 2)
                dve.sem_inc(r_ok, 2)
                dve.sem_inc(t_ok, 2)
                for s in (r_ps, cstep, *t_st):
                    dve.sem_inc(s, 1)
                dve.wait_ge(bstep, 2)
                nc.vector.tensor_tensor(bs[:, 0:1], bs[:, 0:1], bn[:, 0:1], ALU.mult).then_inc(bstep, 1)
                nc.vector.tensor_tensor(bs[:, 1:2], bn[:, 4:5], bn[:, 2:3], ALU.subtract).then_inc(bstep, 1)
                dve.wait_ge(bstep, 4)
                nc.vector.tensor_tensor(bs[:, 1:2], bs[:, 1:2], bs[:, 0:1], ALU.mult).then_inc(bstep, 1)
                dve.wait_ge(bstep, 5)
                nc.vector.tensor_tensor(bs[:, 1:2], bs[:, 1:2], bn[:, 1:2], ALU.add).then_inc(bn_done, 1)
                dve.wait_ge(bn_done, 1)
                nc.vector.tensor_scalar(wt[:, :], wt[:, :], bs[:, 0:1], None, ALU.mult).then_inc(bn_done, 1)
                nc.vector.tensor_scalar(diag[:, :], ident[:, :], bs[:, 1:2], None, ALU.mult).then_inc(bn_done, 1)
                dve.wait_ge(w_ok, 1)
                SOFT = 4
                POST = 2
                with dve.Fori(0, B) as b:
                    for g in range(NQ):
                        n = b * NQ + g
                        cols = slice(g * QT * TP, (g + 1) * QT * TP)
                        rest, mid = k_rest[:, g % 2, :], k_mid[0:C4, g % 2, :]
                        hold(dve, k_hi, n + 1, own)
                        hold(dve, k_low, n + 1, own)
                        nc.vector.tensor_tensor(rest, ps_e[g % 2][:, 0, 0:QT * TP], ka[:, cols], ALU.subtract)\
                            .then_inc(k_ok, 1)
                        hold(dve, k_ok, n + 3, own)
                        nc.vector.tensor_copy(mid, rest[0:C4]).then_inc(k_step, 1)
                        hold(dve, k_step, n * 2 + 1, own)
                        nc.vector.tensor_tensor(kb[0:C4, cols], rest[0:C4], mid, ALU.subtract).then_inc(k_step, 1)

                    def query(s, slot):
                        qn = b * (NS + 1) + s
                        hold(dve, q_hi, qn + 1, own)
                        hold(dve, qs_ok, qn + 1, own)
                        nc.vector.tensor_tensor(q_rest[:, :], ps_r[1][:, 0:ST * TP], qa[:, slot, :],
                                                ALU.subtract).then_inc(q_left, 1)

                    def query_low(s, slot):
                        hold(dve, q_step, b * (NS + 1) + (s + 1), own)
                        lo = slice(C4, 2 * C4)
                        nc.vector.tensor_tensor(qb[lo, slot, :], q_rest[lo, :], q_mid[lo, :], ALU.subtract)\
                            .then_inc(qs_ok, 1)

                    query(0, 0)
                    query_low(0, 0)
                    hold(dve, zeroed, b + 1, own)

                    def below(S, slot):
                        hold(dve, mx_ok, (S + 1) * (ST * NCH), own)
                        d = S * SOFT
                        nc.vector.tensor_reduce(mn[:, slot, :], nm[:, slot, :, :], AX, ALU.min).then_inc(sstep, 1)
                        dve.wait_ge(sstep, d + 1)
                        nc.vector.tensor_tensor(dm[:, slot, :, :], spread(mn[:, slot, :], 2, NCH), nm[:, slot, :, :],
                                                ALU.subtract).then_inc(dm_ok, 1)

                    def chunk_weights(S, slot):
                        d = S * SOFT
                        hold(dve, ez_ok, S + 1, own)
                        nc.vector.tensor_tensor(zs[:, slot, :, :], zs[:, slot, :, :], ez[:, slot, :, :], ALU.mult)\
                            .then_inc(sstep, 1)
                        dve.wait_ge(sstep, d + 2)
                        nc.vector.tensor_reduce(zt[:, slot, :], zs[:, slot, :, :], AX, ALU.add).then_inc(sstep, 1)
                        dve.wait_ge(sstep, d + 3)
                        nc.vector.reciprocal(zr[:, slot, :], zt[:, slot, :]).then_inc(sstep, 1)
                        dve.wait_ge(sstep, d + 4)
                        nc.vector.tensor_tensor(wz[:, slot, :, :], ez[:, slot, :, :], spread(zr[:, slot, :], 2, NCH),
                                                ALU.mult).then_inc(w_rdy, 1)

                    def column(S, slot, j):
                        i, ch = j // NCH, j % NCH
                        dve.wait_ge(cstep, S * (ST * NCH) + max(j - NCH + 1, 0) + 1)
                        part_ = cs[:, ch * CK:(ch + 1) * CK]
                        nc.vector.scalar_tensor_tensor(part_, prob[:, slot, i, ch * CK:(ch + 1) * CK],
                                                       wz[:, slot, i, ch:ch + 1], part_, ALU.mult, ALU.add)\
                            .then_inc(cstep, 1)

                    def part(s_e, e, s_r, r):
                        s_n = s_e
                        s_e, s_r = overall(b, s_e), overall(b, s_r)
                        if s_r is not None:
                            below(s_r, r)
                        left = list(range(ST * NCH)) if s_r is not None else []
                        ready = False
                        for at, (kind, j) in enumerate(interleaved(s_e, s_r)):
                            if at == (2 if s_e is not None else 0) and s_r is not None:
                                chunk_weights(s_r, r)
                                hold(dve, w_rdy, s_r + 1, own)
                                ready = True
                            if kind == ENERGY:
                                i, ch = j // NCH, j % NCH
                                dve.wait_ge(e_ps, s_e * (ST * NCH) + (j + 1))
                                nc.vector.tensor_reduce(nm[:, e, i, ch:ch + 1], energies(e, j)[0:TP, :, 0:BK],
                                                        mybir.AxisListType.XY, ALU.max, negate=True).then_inc(mx_ok, 1)
                                if j == NEXT_QUERY + 2:
                                    query(s_n + 1, 1 - e)
                                elif j == NEXT_QUERY + 6:
                                    query_low(s_n + 1, 1 - e)
                            else:
                                hold(dve, r_ps, s_r * NMG + (j + 1) + 1, own)
                                part_ = xr[:, j * BK:(j + 1) * BK]
                                nc.vector.tensor_tensor(part_, part_, ps_r[j % 2][:, 0:BK], ALU.add)\
                                    .then_inc(r_ok, 1)
                            if ready and left and (kind == ENERGY or s_e is None):
                                for _ in range(1 if kind == ENERGY else 2):
                                    column(s_r, r, left.pop(0))
                        for j in left:
                            column(s_r, r, j)

                    superblocks(dve, b, part)
                    hold(dve, r_ok, (b + 1) * (NS * NMG) + 2, own)
                    d = b * POST
                    hold(dve, c_ps, b + 1, own)
                    nc.vector.tensor_scalar(rc[:, :], ps_r[0][0:TP, 0:HH], -1.0, -EPS_SUM, ALU.mult, ALU.add)\
                        .then_inc(pstep, 1)
                    hold(dve, pstep, d + 1, own)
                    nc.vector.reciprocal(rc[:, :], rc[:, :]).then_inc(pstep, 1)
                    hold(dve, pstep, d + 2, own)

                    def summed(g):
                        n = b * NQ + g
                        hold(dve, u_ps, n + 1, own)
                        for i in range(QT):
                            m = g * QT + i
                            last = nc.vector.tensor_scalar(un[:, g % 2, i, :], ps_e[g % 2][0:TP, 0, i * C:(i + 1) * C],
                                                           rc[:, m:m + 1], None, ALU.mult)
                        last.then_inc(u_sum, 1)
                        if g:
                            residual(g - 1)
                        hold(dve, u_sum, n * 3 + 1, own)
                        nc.vector.tensor_tensor(un[:, g % 2, :, :], un[:, g % 2, :, :],
                                                ps_e[g % 2][0:TP, 1, 0:QT * C].rearrange("p (t c) -> p t c", c=C),
                                                ALU.add).then_inc(u_sum, 1)
                        hold(dve, u_sum, n * 3 + 2, own)
                        dve.sem_inc(u_ok, 1)
                        nc.vector.tensor_tensor(un[:, g % 2, :, :], un[:, g % 2, :, :], spread(shift[:, :], 1, QT),
                                                ALU.add).then_inc(u_sum, 1)

                    def residual(g):
                        n = b * NQ + g
                        hold(dve, u_sum, n * 3 + 3, own)
                        hold(dve, tin_ok, n + 1, own)
                        hold(dve, t_st[g % 2], uses(g % 2, b, g) * 32 + 1, own)
                        nc.vector.scalar_tensor_tensor(tout[:, g % 2, :, :], un[:, g % 2, :, :], 0.0,
                                                       tin[:, g % 2, :, :], ALU.max, ALU.add).then_inc(t_ok, 1)

                    for g in range(NQ):
                        summed(g)
                    residual(NQ - 1)
                    hold(dve, t_ok, (b + 1) * NQ + 2, own)
                    dve.sem_inc(image_done, 1)


E8, F = 8, 512
FB = F // 128
CAP = -(-5 * T // (4 * E8))
EBATCH = 512
SLOTS = -(-CAP // EBATCH) * EBATCH
NEB = SLOTS // EBATCH
DROPPED = 1 << 20
NF = T // 128
FG = 7
NFG = NF // FG
BIGGEST = 3.4028234663852886e38


def route_stage(nc, k, ins, t4_d, buf_d, tok, slots, weight):
    own, ident = k["own"], k["ident"]
    with ExitStack() as es:
        t = Ctx(nc, es, "route")
        hall = t.sb("hall", [128, NF, C])
        hn = t.sb("hn", [128, 2, FG, C])
        ht = t.sb("ht", [C, 2, FG * 128])
        gw = t.sb("gw", [C, E8])
        gb = t.sb("gb", [128, E8])
        lg = t.sb("lg", [128, NF, E8])
        ex = t.sb("ex", [128, NF, E8])
        hot = t.sb("hot", [128, NF, E8])
        cum = t.sb("cum", [128, NF, E8])
        iot_i = t.sb("iota_i", [128, E8], I32)
        iot = t.sb("iota", [128, E8])
        less8 = t.sb("iota_less_8", [128, E8])
        one = t.sb("one", [128, NF])
        tri = t.sb("tri", [128, 128])
        tot = t.sb("tot", [128, E8])
        mx, sm, idx, pos, kept, tmp = (t.sb(n, [128, NF]) for n in ("mx", "sm", "idx", "pos", "kept", "tmp"))
        st = t.sb("st", [128, 2, FG, 6])
        mv = t.sb("mv", [128, 2, FG, 2])
        ve = t.sb("ve", [128, 2, FG])
        rs = t.sb("rs", [128, 2, FG])
        half = t.sb("half", [128, FG])
        ps_t = [t.ps(f"ps_t{i}", [C, 2, 512]) for i in range(2)]
        ps_l = [t.ps(f"ps_l{i}", [128, 512]) for i in range(2)]
        (t_in, g_in, stat, agg, eps, rstd, hn_ok, hT, ht_ok, copied, l_ps, lg_ok, cst, step, sm_ok, tri_ps, slot_ok,
         sent, ct) = [t.sem(s) for s in (
             "tokens_loaded gate_loaded stats_ready mean_var_ready var_eps_ready rstd_ready hn_ready hT_in_psum "
             "ht_ready hn_kept logits_in_psum logits_ready constants_ready step exp_ready prefix_in_psum slots_ready "
             "rows_sent totals_ready").split()]

        with nc.Block() as block:

            @block.sync
            def _(sp):
                sp.dma_start(gw[:, :], ins["L1_ffn_gate_w"]).then_inc(g_in, 16)
                sp.dma_start(gb[:, :], row(ins["L1_ffn_gate_b"]).to_broadcast([128, E8])).then_inc(g_in, 16)
                tv = t4_d.rearrange("(p f) c -> p f c", p=128)
                for g in range(NFG):
                    if g:
                        sp.wait_ge(t_in, 16 * g)
                    sp.dma_start(tok[:, g * FG:(g + 1) * FG, :], tv[:, g * FG:(g + 1) * FG, :]).then_inc(t_in, 16)

            @block.gpsimd
            def _(pool):
                pool.memset(half[:, :], -0.5).then_inc(cst, 1)
                pool.iota(iot_i[:, :], [[1, E8]], base=0, channel_multiplier=0).then_inc(cst, 1)
                pool.memset(tri[:, :], 1.0).then_inc(cst, 1)
                pool.wait_ge(cst, 3)
                pool.affine_select(out=tri[:, :], in_=tri[:, :], compare_op=ALU.is_gt, fill=0.0, base=0,
                                   pattern=[[1, 128]], channel_multiplier=-1).then_inc(cst, 1)
                with pool.Fori(0, NFG // 2) as i:
                    for p in range(2):
                        n = i * 2 + p
                        hold(pool, agg, n + 1, own)
                        pool.tensor_scalar(ve[:, p, :], mv[:, p, :, 1], EPS, None, ALU.add).then_inc(eps, 1)
                        hold(pool, eps, n + 1, own)
                        pool.tensor_tensor(rs[:, p, :], ve[:, p, :], half[:, :], ALU.pow).then_inc(rstd, 1)
                pool.wait_ge(slot_ok, 1)
                pool.wait_ge(copied, NFG + 2)
                for f in range(NF):
                    pool.indirect_dma_start(
                        out=buf_d, out_offset=bass.IndirectOffsetOnAxis(ap=slots[:, 0, f:f + 1], axis=0),
                        in_=hall[:, f, :], in_offset=None, bounds_check=E8 * SLOTS - 1, oob_is_err=False)\
                        .then_inc(sent, 16)
                pool.wait_ge(sent, 16 * NF)

            @block.tensor
            def _(pe):
                pe.wait_ge(g_in, 32)

                def turn(n, p):
                    hold(pe, hn_ok, n + 1, own)
                    hold(pe, ht_ok, n + 1, own)
                    for i in range(FG):
                        mm = pe.transpose(ps_t[p][:, i // 4, (i % 4) * 128:(i % 4 + 1) * 128], hn[:, p, i, :],
                                          ident[:, :])
                    mm.then_inc(hT, 1)

                def gate(n, p):
                    hold(pe, ht_ok, n + 3, own)
                    hold(pe, lg_ok, n + 1, own)
                    for i in range(FG):
                        mm = pe.matmul(ps_l[p][:, i * E8:(i + 1) * E8], ht[:, p, i * 128:(i + 1) * 128], gw[:, :],
                                       start=True, stop=True)
                    mm.then_inc(l_ps, 1)

                with pe.Fori(0, NFG // 2) as i:
                    for p in range(2):
                        turn(i * 2 + p, p)
                    for p in range(2):
                        gate(i * 2 + p, p)
                pe.wait_ge(ct, 1)
                pe.matmul(ps_l[0][:, 0:E8], tri[:, :], tot[:, :], start=True, stop=True).then_inc(tri_ps, 1)

            @block.scalar
            def _(act):
                act.sem_inc(ht_ok, 2)
                with act.Fori(0, NFG // 2) as i:
                    for p in range(2):
                        n = i * 2 + p
                        hold(act, hT, n + 1, own)
                        for hb, w in ((0, 4), (1, FG - 4)):
                            last = nc.scalar.activation(ht[:, p, hb * 512:hb * 512 + w * 128],
                                                        ps_t[p][:, hb, 0:w * 128], ACT.Copy)
                        last.then_inc(ht_ok, 1)
                        nc.scalar.activation(hall[:, bass.ds(n * FG, FG), :], hn[:, p, :, :], ACT.Copy)\
                            .then_inc(copied, 1)
                act.wait_ge(sm_ok, 1)
                nc.scalar.activation(ex[:, :, :], ex[:, :, :], ACT.Exp).then_inc(sm_ok, 1)

            @block.vector
            def _(dve):
                dve.sem_inc(lg_ok, 2)
                dve.sem_inc(copied, 2)
                dve.wait_ge(g_in, 32)

                def stats(n, p):
                    hold(dve, t_in, n * 16 + 16, own)
                    for j in range(FG):
                        last = nc.vector.bn_stats(st[:, p, j, :], tok[:, n * FG + j, :])
                    last.then_inc(stat, 1)
                    hold(dve, stat, n + 1, own)
                    for j in range(FG):
                        last = nc.vector.bn_aggr(mv[:, p, j, :], st[:, p, j, :])
                    last.then_inc(agg, 1)

                def normalize(n, p):
                    hold(dve, rstd, n + 1, own)
                    hold(dve, copied, n + 1, own)
                    for j in range(FG):
                        last = nc.vector.tensor_scalar(hn[:, p, j, :], tok[:, n * FG + j, :], mv[:, p, j, 0:1],
                                                       rs[:, p, j:j + 1], ALU.subtract, ALU.mult)
                    last.then_inc(hn_ok, 1)
                    hold(dve, hn_ok, n + 1, own)

                def logits(n, p):
                    hold(dve, l_ps, n + 1, own)
                    nc.vector.tensor_tensor(lg[:, bass.ds(n * FG, FG), :],
                                            ps_l[p][:, 0:FG * E8].rearrange("p (f e) -> p f e", e=E8),
                                            spread(gb[:, :], 1, FG), ALU.add).then_inc(lg_ok, 1)

                for p in range(2):
                    stats(p, p)
                with dve.Fori(0, NFG // 2 - 1) as i:
                    for p in range(2):
                        normalize(i * 2 + p, p)
                        stats(i * 2 + (p + 2), p)
                    for p in range(2):
                        logits(i * 2 + p, p)
                for p in range(2):
                    normalize(NFG - 2 + p, p)
                for p in range(2):
                    logits(NFG - 2 + p, p)
                n = [0]

                def do(ins_):
                    n[0] += 1
                    ins_.then_inc(step, 1)
                    dve.wait_ge(step, n[0])

                dve.wait_ge(lg_ok, NFG + 2)
                dve.wait_ge(cst, 4)
                do(nc.vector.memset(one[:, :], 1.0))
                do(nc.vector.tensor_copy(iot[:, :], iot_i[:, :]))
                do(nc.vector.tensor_scalar(less8[:, :], iot[:, :], -float(E8), None, ALU.add))
                do(nc.vector.tensor_reduce(mx[:, :], lg[:, :, :], AX, ALU.max))
                nc.vector.tensor_tensor(ex[:, :, :], lg[:, :, :], spread(mx[:, :], 2, E8), ALU.subtract)\
                    .then_inc(sm_ok, 1)
                do(nc.vector.tensor_tensor(hot[:, :, :], lg[:, :, :], spread(mx[:, :], 2, E8), ALU.is_equal))
                do(nc.vector.tensor_tensor(hot[:, :, :], hot[:, :, :], spread(less8[:, :], 1, NF), ALU.mult))
                do(nc.vector.tensor_reduce(idx[:, :], hot[:, :, :], AX, ALU.min))
                do(nc.vector.tensor_scalar(idx[:, :], idx[:, :], float(E8), None, ALU.add))
                do(nc.vector.tensor_tensor(hot[:, :, :], spread(iot[:, :], 1, NF), spread(idx[:, :], 2, E8),
                                           ALU.is_equal))
                for e in range(E8):
                    do(nc.vector.tensor_tensor_scan(cum[:, :, e], one[:, :], hot[:, :, e], 0.0, ALU.mult, ALU.add))
                nc.vector.tensor_copy(tot[:, :], cum[:, NF - 1, :]).then_inc(ct, 1)
                dve.wait_ge(tri_ps, 1)
                do(nc.vector.tensor_tensor(cum[:, :, :], cum[:, :, :], spread(ps_l[0][:, 0:E8], 1, NF), ALU.add))
                do(nc.vector.tensor_tensor(cum[:, :, :], cum[:, :, :], hot[:, :, :], ALU.mult))
                do(nc.vector.tensor_reduce(pos[:, :], cum[:, :, :], AX, ALU.add))
                do(nc.vector.tensor_scalar(pos[:, :], pos[:, :], -1.0, None, ALU.add))
                do(nc.vector.tensor_scalar(kept[:, :], pos[:, :], float(CAP), None, ALU.is_lt))
                do(nc.vector.tensor_scalar(pos[:, :], pos[:, :], float(CAP - 1), None, ALU.min))
                do(nc.vector.tensor_scalar(tmp[:, :], idx[:, :], float(SLOTS), None, ALU.mult))
                do(nc.vector.tensor_tensor(pos[:, :], pos[:, :], tmp[:, :], ALU.add))
                do(nc.vector.tensor_copy(slots[:, 1, :], pos[:, :]))
                do(nc.vector.tensor_scalar(tmp[:, :], kept[:, :], -float(DROPPED), float(DROPPED), ALU.mult, ALU.add))
                do(nc.vector.tensor_tensor(pos[:, :], pos[:, :], tmp[:, :], ALU.add))
                do(nc.vector.tensor_copy(slots[:, 0, :], pos[:, :]))
                dve.sem_inc(slot_ok, 1)
                dve.wait_ge(sm_ok, 2)
                do(nc.vector.tensor_reduce(sm[:, :], ex[:, :, :], AX, ALU.add))
                do(nc.vector.reciprocal(sm[:, :], sm[:, :]))
                do(nc.vector.tensor_tensor(weight[:, :], sm[:, :], kept[:, :], ALU.mult))


def experts_stage(nc, k, ins, buf_d, res_d):
    own, ident = k["own"], k["ident"]
    NI = EBATCH // 128
    with ExitStack() as es:
        t = Ctx(nc, es, "experts")
        w1 = t.sb("w1", [C, 2, F])
        w2 = t.sb("w2", [128, 2, FB, C])
        b1r = t.sb("b1r", [E8 * FB, 128])
        b1t = t.sb("b1t", [128, E8 * FB])
        b2 = t.sb("b2", [128, E8, C])
        bi = t.sb("bi", [128, 2, NI, C])
        bt_ = t.sb("bt", [C, 2, EBATCH])
        hid = t.sb("hid", [128, 2, FB, EBATCH])
        yo = t.sb("yo", [128, 2, NI, C])
        ps_t = [t.ps(f"ps_t{i}", [C, 512]) for i in range(2)]
        ps_u = [t.ps(f"ps_u{i}", [128, 512]) for i in range(4)]
        ps_y = [t.ps(f"ps_y{i}", [128, 512]) for i in range(2)]
        (b_in, b1_ps, b1_ok, bT, bt_ok, u_ps, hid_ok, y_ps, y_ok) = [t.sem(s) for s in (
            "biases_loaded b1_in_psum b1_ready bT_in_psum bt_ready u_in_psum hidden_ready y_in_psum y_ready").split()]
        w_in, bi_in, y_st = ([t.sem(f"{s}{p}") for p in range(2)] for s in (
            "weights_loaded", "rows_loaded", "y_stored"))
        bufv = buf_d.rearrange("(b i p) c -> b p i c", p=128, i=NI)
        resv = res_d.rearrange("(b i p) c -> b p i c", p=128, i=NI)

        with nc.Block() as block:

            @block.sync
            def _(sp):
                sp.dma_start(b1r[:, :], ins["L1_ffn_b1"].rearrange("e (f p) -> (e f) p", p=128)).then_inc(b_in, 16)
                sp.dma_start(b2[:, :, :], ins["L1_ffn_b2"].rearrange("e c -> (e c)").rearrange("(a n) -> a n", a=1)
                             .to_broadcast([128, E8 * C]).rearrange("p (e c) -> p e c", c=C)).then_inc(b_in, 16)
                with sp.Fori(0, E8 // 2) as i:
                    for x in range(2):
                        e = i * 2 + x
                        hold(sp, y_ps, e * NEB + 1, own)
                        sp.dma_start(w1[:, x, :], ins["L1_ffn_w1"][e, :, :]).then_inc(w_in[x], 16)
                        sp.dma_start(w2[:, x, :, :], ins["L1_ffn_w2"][e, :, :].rearrange("(f p) c -> p f c", p=128))\
                            .then_inc(w_in[x], 16)
                        for q in range(NEB):
                            n = e * NEB + q
                            hold(sp, bT, n + 1, own)
                            sp.dma_start(bi[:, q % 2, :, :], bufv[n]).then_inc(bi_in[q % 2], 16)

            @block.tensor
            def _(pe):
                pe.sem_inc(y_ps, NEB + 1)
                pe.sem_inc(bT, 2)
                pe.wait_ge(b_in, 32)
                pe.transpose(ps_t[0][:, 0:E8 * FB], b1r[:, :], ident[0:E8 * FB, 0:E8 * FB]).then_inc(b1_ps, 1)
                pe.wait_ge(b1_ok, 1)
                def turn(i, at):
                    n, p = i * (2 * NEB) + at, at % 2
                    hold(pe, bi_in[p], i * (16 * NEB) + 16 * (at // 2 + 1), own)
                    hold(pe, bt_ok, n + 1, own)
                    for j in range(NI):
                        mm = pe.transpose(ps_t[p][:, j * 128:(j + 1) * 128], bi[:, p, j, :], ident[:, :])
                    mm.then_inc(bT, 1)

                def pair(i, last):
                    for at in range(2 * NEB):
                        n, x, p = i * (2 * NEB) + at, at // NEB, at % 2
                        if at % NEB == 0:
                            hold(pe, w_in[x], i * 32 + 32, own)
                        hold(pe, bt_ok, n + 3, own)
                        for f in range(FB):
                            hold(pe, hid_ok, n * FB + (f + 1), own)
                            pe.matmul(ps_u[f][:, :], w1[:, x, f * 128:(f + 1) * 128], bt_[:, p, :], start=True,
                                      stop=True).then_inc(u_ps, 1)
                        if at + 1 < 2 * NEB:
                            turn(i, at + 1)
                        elif not last:
                            turn(i + 1, 0)
                        hold(pe, hid_ok, n * FB + 2 * FB, own)
                        hold(pe, y_ok, n + 1, own)
                        for j in range(NI):
                            for f in range(FB):
                                mm = pe.matmul(ps_y[p][:, j * C:(j + 1) * C], hid[:, p, f, j * 128:(j + 1) * 128],
                                               w2[:, x, f, :], start=(f == 0), stop=(f == FB - 1))
                        mm.then_inc(y_ps, 1)

                turn(0, 0)
                with pe.Fori(0, E8 // 2 - 1) as i:
                    pair(i, False)
                pair(E8 // 2 - 1, True)

            @block.scalar
            def _(act):
                act.sem_inc(bt_ok, 2)
                act.sem_inc(hid_ok, FB)
                act.wait_ge(b1_ps, 1)
                nc.scalar.activation(b1t[:, :], ps_t[0][:, 0:E8 * FB], ACT.Copy).then_inc(b1_ok, 1)
                act.wait_ge(b1_ok, 1)

                def turned(n, p):
                    hold(act, bT, n + 3, own)
                    nc.scalar.activation(bt_[:, p, :], ps_t[p][:, :], ACT.Copy).then_inc(bt_ok, 1)

                def store(n, p):
                    hold(act, y_ok, n + 3, own)
                    act.dma_start(resv[n], yo[:, p, :, :]).then_inc(y_st[p], 16)

                def pair(i, first, last):
                    for at in range(2 * NEB):
                        n, e, p = i * (2 * NEB) + at, i * 2 + at // NEB, at % 2
                        for f in range(FB):
                            hold(act, u_ps, n * FB + (f + 1), own)
                            nc.scalar.activation(hid[:, p, f, :], ps_u[f][:, :], ACT.Relu,
                                                 bias=b1t[:, bass.ds(e * FB + f, 1)], scale=1.0).then_inc(hid_ok, 1)
                        if not (last and at == 2 * NEB - 1):
                            turned(n + 1, 1 - p)
                        if not (first and at == 0):
                            store(n - 1, 1 - p)

                turned(0, 0)
                pair(0, True, False)
                with act.Fori(1, E8 // 2 - 1) as i:
                    pair(i, False, False)
                pair(E8 // 2 - 1, False, True)
                store(E8 * NEB - 1, 1)
                for p in range(2):
                    act.wait_ge(y_st[p], 16 * E8 * NEB // 2 + 1)

            @block.vector
            def _(dve):
                dve.sem_inc(y_ok, 2)
                for s in y_st:
                    dve.sem_inc(s, 1)
                with dve.Fori(0, E8 // 2) as i:
                    for x in range(2):
                        e = i * 2 + x
                        for q in range(NEB):
                            n = e * NEB + q
                            p = q % 2
                            hold(dve, y_ps, n + NEB + 2, own)
                            hold(dve, y_st[p], e * (8 * NEB) + 16 * (q // 2) + 1, own)
                            nc.vector.tensor_tensor(yo[:, p, :, :], ps_y[p][:, :].rearrange("p (t c) -> p t c", c=C),
                                                    spread(b2[:, e, :], 1, NI), ALU.add).then_inc(y_ok, 1)


def combine_stage(nc, k, res_d, tok, slots, weight, out):
    own = k["own"]
    with ExitStack() as es:
        t = Ctx(nc, es, "combine")
        yg = t.sb("yg", [128, 2, FG, C])
        yc = t.sb("yc", [128, 2, FG, C])
        fx = t.sb("fx", [128, 2, FG, C])
        mk = t.sb("mk", [128, 3, FG, C], I32)
        lim = t.sb("lim", [128, 2, FG, C])
        step, res, cst, scaled = (t.sem(s) for s in ("step", "result_ready", "constants_ready", "rows_scaled"))
        zeros = t.sb("zeros", [128, FG, C])
        got = [t.sem(f"gathered{p}") for p in range(2)]
        stored = t.sem("stored")
        outv = out.rearrange("(p f) c -> p f c", p=128)

        with nc.Block() as block:

            @block.gpsimd
            def _(pool):
                pool.memset(lim[:, 0, :, :], 1e4).then_inc(cst, 1)
                pool.memset(lim[:, 1, :, :], -1e4).then_inc(cst, 1)
                pool.memset(zeros[:, :, :], 0.0).then_inc(cst, 1)
                for g in range(NFG):
                    if g >= 2:
                        pool.wait_ge(scaled, g - 1)
                    for j in range(FG):
                        f = g * FG + j
                        pool.indirect_dma_start(
                            out=yg[:, g % 2, j, :], out_offset=None, in_=res_d,
                            in_offset=bass.IndirectOffsetOnAxis(ap=slots[:, 1, f:f + 1], axis=0),
                            bounds_check=E8 * SLOTS - 1, oob_is_err=False).then_inc(got[g % 2], 16)

            @block.scalar
            def _(act):
                act.wait_ge(cst, 3)
                for g in range(NFG):
                    p = g % 2
                    if g >= 2:
                        act.wait_ge(res, g - 1)
                    nc.scalar.activation(fx[:, p, :, :], zeros[:, :, :], ACT.Copy)
                    act.wait_ge(got[p], 16 * FG * (g // 2 + 1))
                    for j in range(FG):
                        f = g * FG + j
                        last = nc.scalar.activation(yc[:, p, j, :], yg[:, p, j, :], ACT.Copy, scale=weight[:, f:f + 1])
                    last.then_inc(scaled, 1)

            @block.vector
            def _(dve):
                n = [0]

                def do(ins_):
                    n[0] += 1
                    ins_.then_inc(step, 1)
                    return n[0]

                dve.wait_ge(cst, 3)
                for g in range(NFG):
                    p = g % 2
                    part = tok[:, g * FG:(g + 1) * FG, :]
                    dve.wait_ge(scaled, g + 1)
                    y = yc[:, p, :, :]
                    do(nc.vector.tensor_tensor(mk[:, 0, :, :], y, y, ALU.is_equal))
                    do(nc.vector.tensor_scalar(mk[:, 1, :, :], y, BIGGEST, None, ALU.is_gt))
                    a = do(nc.vector.tensor_scalar(mk[:, 2, :, :], y, -BIGGEST, None, ALU.is_lt))
                    dve.wait_ge(step, a)
                    dve.wait_ge(step, do(nc.vector.copy_predicated(fx[:, p, :, :], mk[:, 0, :, :], y)))
                    for i in range(2):
                        dve.wait_ge(step, do(nc.vector.copy_predicated(fx[:, p, :, :], mk[:, 1 + i, :, :],
                                                                       lim[:, i, :, :])))
                    nc.vector.tensor_tensor(part, part, fx[:, p, :, :], ALU.add).then_inc(res, 1)

            @block.sync
            def _(sp):
                for g in range(NFG):
                    sp.wait_ge(res, g + 1)
                    sp.dma_start(outv[:, g * FG:(g + 1) * FG, :], tok[:, g * FG:(g + 1) * FG, :]).then_inc(stored, 16)
                sp.wait_ge(stored, 16 * NFG)


def ffn(nc, k, c, ins, t4_d, buf_d, res_d, out):
    tok = c.sb("tokens", [128, NF, C])
    slots = c.sb("slots", [128, 2, NF], I32)
    weight = c.sb("weight", [128, NF])
    route_stage(nc, k, ins, t4_d, buf_d, tok, slots, weight)
    experts_stage(nc, k, ins, buf_d, res_d)
    combine_stage(nc, k, res_d, tok, slots, weight, out)


_NAMES = ["x", "L0_conv_w_in", "L0_conv_b_in", "L0_conv_w_dw", "L0_conv_b_dw", "L0_conv_ln_dw_g", "L0_conv_ln_dw_b",
          "L0_conv_w_off", "L0_conv_b_off", "L0_conv_w_mask", "L0_conv_b_mask", "L0_conv_w_out", "L0_conv_b_out",
          "L0_conv_ln1_g", "L0_conv_ln1_b", "L0_conv_w_fc1", "L0_conv_b_fc1", "L0_conv_w_fc2", "L0_conv_b_fc2",
          "L0_conv_ln2_g", "L0_conv_ln2_b", "L0_conv_gamma1", "L0_conv_gamma2", "L1_attn_Wq", "L1_attn_Wk",
          "L1_attn_Wv", "L1_attn_bv", "L1_attn_Wt", "L1_attn_bt", "L1_attn_gamma", "L1_attn_beta", "L1_attn_bn_mean",
          "L1_attn_bn_var", "L1_ffn_gate_w", "L1_ffn_gate_b", "L1_ffn_w1", "L1_ffn_b1", "L1_ffn_w2", "L1_ffn_b2"]


def build(nc, ins, out):
    def scratch(name, shape):
        return nc.dram_tensor(name, shape, F32, kind="Internal").ap()

    xp_d = scratch("projected", (T + 2 * PAD, C))
    om_d = scratch("offsets_masks", (B * HH, TP, OM))
    y_d = scratch("deformed", (B * HH, TP, C))
    t_d = scratch("block_out", (B * HH, TP, C))
    xc_d = scratch("block_out_normed", (B * HH, TP, C))
    t4_d = scratch("attended", (T, C))
    buf_d = scratch("dispatched", (E8 * SLOTS, C))
    res_d = scratch("expert_out", (E8 * SLOTS, C))

    with ExitStack() as everything:
        k = identity(nc, Ctx(nc, everything, "all"))
        with ExitStack() as block:
            c = Ctx(nc, block, "block")
            constants(nc, c, ins, k)
            shift_tables(nc, k, c)
            extremes = c.sb("extremes", [TP, NB, 4])
            base = c.sb("base", [TP, 2])
            counts = c.sb("counts", [1, 4], I32)
            zero_stage(nc, [y_d.rearrange("t p c -> (t p c)"), buf_d.rearrange("n c -> (n c)")])
            offsets_stage(nc, k, ins["x"], xp_d, om_d, extremes)
            window_stage(nc, k, extremes, base, counts)
            deformable_stage(nc, k, xp_d, om_d, y_d, base, counts)
            rows_stage(nc, k, ins["x"], y_d, t_d, xc_d)
        attention_stage(nc, k, ins, xc_d, t_d, t4_d)
        ffn(nc, k, Ctx(nc, everything, "ffn"), ins, t4_d, buf_d, res_d, out.rearrange("b y x c -> (b y x) c"))


def kernel(**inputs):
    import numpy as np
    import concourse.bacc as bacc
    from concourse.bass_utils import run_bass_kernel_spmd as run

    nc = bacc.Bacc("TRN2", target_bir_lowering=False, num_devices=1)
    arrays, ins = {}, {}
    for name in _NAMES:
        a = np.ascontiguousarray(inputs[name])
        arrays[f"in_{name}"] = a
        ins[name] = nc.dram_tensor(f"in_{name}", a.shape, mybir.dt.from_np(a.dtype), kind="ExternalInput").ap()
    out = nc.dram_tensor("out", (B, H, W, C), F32, kind="ExternalOutput").ap()
    build(nc, ins, out)
    return run(nc, [arrays], core_ids=[0]).results[0]["out"]
```
